# Optimizing a Trainium2 kernel written in Bass

```python
import numpy as np
import jax
import jax.numpy as jnp

def _softmax(x, axis=-1):
    return jax.nn.softmax(x, axis=axis)

def _gelu(x):
    return jax.nn.gelu(x, approximate=True)

def _silu(x):
    return jax.nn.silu(x)

def _sigmoid(x):
    return jax.nn.sigmoid(x)

def _layernorm(x, axis=-1, eps=1e-05):
    m = jnp.mean(x, axis=axis, keepdims=True)
    v = jnp.var(x, axis=axis, keepdims=True)
    return (x - m) / jnp.sqrt(v + eps)

def _scatter_add(tgt, idx, src, axis=0):
    return tgt.at[idx].add(src)

def _segment_sum(src, seg, n):
    return jax.ops.segment_sum(src, seg, n)
kernel_name = 'mk_seq_postln_d2_jaxref_r8_1bdb87'

def setup_inputs(seed: int=0):
    np.random.seed(seed)
    _w = jnp.asarray

    def _L0_attn_setup():
        import jax, jax.numpy as jnp
        import numpy as np
        B, T, D, H = (2, 256, 128, 16)
        DH = D // H
        ROPE_BASE = 10000.0

        def _rope(Xh, cos, sin):
            x0 = Xh[..., 0::2]
            x1 = Xh[..., 1::2]
            r0 = cos * x0 - sin * x1
            r1 = sin * x0 + cos * x1
            return jnp.stack((r0, r1), axis=-1).reshape(Xh.shape)
        key = jax.random.key(seed)
        ks = jax.random.split(key, 5)
        s = 1.0 / np.sqrt(D)
        return {'X': jax.random.normal(ks[0], (B, T, D), dtype=jnp.float32), 'W_q': jax.random.normal(ks[1], (D, D), dtype=jnp.float32) * s, 'W_k': jax.random.normal(ks[2], (D, D), dtype=jnp.float32) * s, 'W_v': jax.random.normal(ks[3], (D, D), dtype=jnp.float32) * s, 'W_o': jax.random.normal(ks[4], (D, D), dtype=jnp.float32) * s}
    _L0_attn_in = _L0_attn_setup()

    def _L0_ffn_setup():
        import jax, jax.numpy as jnp
        import numpy as np
        B, S, DIM = (4, 512, 128)
        BASE_COUPLING = 0.1
        NUM_CYCLES = 3

        def _gelu(x):
            return jax.nn.gelu(x, approximate=False)

        def _coupling_net(h, w1, b1, w2, b2, w3, b3, w4, b4):
            h = _gelu(h @ w1 + b1)
            h = _gelu(h @ w2 + b2)
            h = _gelu(h @ w3 + b3)
            return jax.nn.sigmoid(h @ w4 + b4)

        def _global_net(h, w1, b1, w2, b2, w3, b3):
            h = _gelu(h @ w1 + b1)
            h = _gelu(h @ w2 + b2)
            return jax.nn.sigmoid(h @ w3 + b3)

        def _twist(x):
            o_r, o_i, p_r, p_i = jnp.split(x, 4, axis=-1)
            return jnp.concatenate([p_r, -p_i, -o_r, o_i], axis=-1)
        key = jax.random.key(seed)
        ks = jax.random.split(key, 9)
        d = DIM

        def w(k, fan_in, fan_out):
            return jax.random.normal(k, (fan_in, fan_out), dtype=jnp.float32) / np.sqrt(fan_in).astype(np.float32)
        inp = {'x': jax.random.normal(ks[0], (B, S, d), dtype=jnp.float32)}
        cn_dims = [(d, d), (d, d // 2), (d // 2, d // 4), (d // 4, 1)]
        for i, (a, b) in enumerate(cn_dims):
            inp[f'cn_w{i + 1}'] = w(ks[1 + i], a, b)
            inp[f'cn_b{i + 1}'] = jnp.zeros((b,), dtype=jnp.float32)
        gc_dims = [(d, d // 2), (d // 2, d // 4), (d // 4, 1)]
        for i, (a, b) in enumerate(gc_dims):
            inp[f'gc_w{i + 1}'] = w(ks[5 + i], a, b)
            inp[f'gc_b{i + 1}'] = jnp.zeros((b,), dtype=jnp.float32)
        inp['adaptive_range'] = jnp.full((1,), 0.2, dtype=jnp.float32)
        return inp
    _L0_ffn_in = _L0_ffn_setup()

    def _L1_attn_setup():
        import jax, jax.numpy as jnp
        import numpy as np
        B, S, D, H, R = (8, 128, 128, 8, 32)
        DH = D // H

        def _lowrank(xh, U, V, b):
            t = jnp.einsum('bshd,hrd->bshr', xh, V)
            return jnp.einsum('bshr,hdr->bshd', t, U) + b
        key = jax.random.key(seed)
        ks = jax.random.split(key, 10)
        p = lambda k, shape: jax.random.normal(k, shape, dtype=jnp.float32) * 0.02
        return {'x': jax.random.normal(ks[0], (B, S, D), dtype=jnp.float32), 'Uq': p(ks[1], (H, DH, R)), 'Vq': p(ks[2], (H, R, DH)), 'bq': p(ks[3], (H, DH)), 'Uk': p(ks[4], (H, DH, R)), 'Vk': p(ks[5], (H, R, DH)), 'bk': p(ks[6], (H, DH)), 'Uv': p(ks[7], (H, DH, R)), 'Vv': p(ks[8], (H, R, DH)), 'bv': p(ks[9], (H, DH))}
    _L1_attn_in = _L1_attn_setup()

    def _L1_ffn_setup():
        import jax, jax.numpy as jnp
        import numpy as np
        import math
        B, L, D = (4, 512, 128)
        F = 512
        E = 16
        CAP_FACTOR = 1.0
        EPS = 1e-05
        key = jax.random.key(seed)
        ks = jax.random.split(key, 8)
        std = 0.02
        return {'x': jax.random.normal(ks[0], (B, L, D), dtype=jnp.float32), 'norm_weight': jnp.ones((D,), dtype=jnp.float32), 'router_weight': jax.random.normal(ks[1], (E, D), dtype=jnp.float32) * std, 'router_bias': jnp.zeros((E,), dtype=jnp.float32), 'fc1_weight': jax.random.normal(ks[2], (E, F, D), dtype=jnp.float32) * std, 'fc1_bias': jnp.zeros((E, F), dtype=jnp.float32), 'fc2_weight': jax.random.normal(ks[3], (E, D, F), dtype=jnp.float32) * std, 'fc2_bias': jnp.zeros((E, D), dtype=jnp.float32)}
    _L1_ffn_in = _L1_ffn_setup()
    _d = {'L0_attn_X': _L0_attn_in['X'], 'L0_attn_W_q': _L0_attn_in['W_q'], 'L0_attn_W_k': _L0_attn_in['W_k'], 'L0_attn_W_v': _L0_attn_in['W_v'], 'L0_attn_W_o': _L0_attn_in['W_o'], 'L0_ffn_cn_w1': _L0_ffn_in['cn_w1'], 'L0_ffn_cn_b1': _L0_ffn_in['cn_b1'], 'L0_ffn_cn_w2': _L0_ffn_in['cn_w2'], 'L0_ffn_cn_b2': _L0_ffn_in['cn_b2'], 'L0_ffn_cn_w3': _L0_ffn_in['cn_w3'], 'L0_ffn_cn_b3': _L0_ffn_in['cn_b3'], 'L0_ffn_cn_w4': _L0_ffn_in['cn_w4'], 'L0_ffn_cn_b4': _L0_ffn_in['cn_b4'], 'L0_ffn_gc_w1': _L0_ffn_in['gc_w1'], 'L0_ffn_gc_b1': _L0_ffn_in['gc_b1'], 'L0_ffn_gc_w2': _L0_ffn_in['gc_w2'], 'L0_ffn_gc_b2': _L0_ffn_in['gc_b2'], 'L0_ffn_gc_w3': _L0_ffn_in['gc_w3'], 'L0_ffn_gc_b3': _L0_ffn_in['gc_b3'], 'L0_ffn_adaptive_range': _L0_ffn_in['adaptive_range'], 'L1_attn_Uq': _L1_attn_in['Uq'], 'L1_attn_Vq': _L1_attn_in['Vq'], 'L1_attn_bq': _L1_attn_in['bq'], 'L1_attn_Uk': _L1_attn_in['Uk'], 'L1_attn_Vk': _L1_attn_in['Vk'], 'L1_attn_bk': _L1_attn_in['bk'], 'L1_attn_Uv': _L1_attn_in['Uv'], 'L1_attn_Vv': _L1_attn_in['Vv'], 'L1_attn_bv': _L1_attn_in['bv'], 'L1_ffn_norm_weight': _L1_ffn_in['norm_weight'], 'L1_ffn_router_weight': _L1_ffn_in['router_weight'], 'L1_ffn_router_bias': _L1_ffn_in['router_bias'], 'L1_ffn_fc1_weight': _L1_ffn_in['fc1_weight'], 'L1_ffn_fc1_bias': _L1_ffn_in['fc1_bias'], 'L1_ffn_fc2_weight': _L1_ffn_in['fc2_weight'], 'L1_ffn_fc2_bias': _L1_ffn_in['fc2_bias']}
    _x0 = _d['L0_attn_X']
    _d['L0_attn_X'] = jax.random.normal(jax.random.fold_in(jax.random.key(seed), 1), (8, 256, 128), dtype=_x0.dtype)
    del _x0
    return _d

def reference(L0_attn_X, L0_attn_W_q, L0_attn_W_k, L0_attn_W_v, L0_attn_W_o, L0_ffn_cn_w1, L0_ffn_cn_b1, L0_ffn_cn_w2, L0_ffn_cn_b2, L0_ffn_cn_w3, L0_ffn_cn_b3, L0_ffn_cn_w4, L0_ffn_cn_b4, L0_ffn_gc_w1, L0_ffn_gc_b1, L0_ffn_gc_w2, L0_ffn_gc_b2, L0_ffn_gc_w3, L0_ffn_gc_b3, L0_ffn_adaptive_range, L1_attn_Uq, L1_attn_Vq, L1_attn_bq, L1_attn_Uk, L1_attn_Vk, L1_attn_bk, L1_attn_Uv, L1_attn_Vv, L1_attn_bv, L1_ffn_norm_weight, L1_ffn_router_weight, L1_ffn_router_bias, L1_ffn_fc1_weight, L1_ffn_fc1_bias, L1_ffn_fc2_weight, L1_ffn_fc2_bias):

    def _L0_attn_ref(X, W_q, W_k, W_v, W_o):
        import jax, jax.numpy as jnp
        import numpy as np
        B, T, D, H = (2, 256, 128, 16)
        DH = D // H
        ROPE_BASE = 10000.0

        def _rope(Xh, cos, sin):
            x0 = Xh[..., 0::2]
            x1 = Xh[..., 1::2]
            r0 = cos * x0 - sin * x1
            r1 = sin * x0 + cos * x1
            return jnp.stack((r0, r1), axis=-1).reshape(Xh.shape)
        b, t, d = X.shape
        Q = X @ W_q.T
        K = X @ W_k.T
        V = X @ W_v.T
        Qh = Q.reshape(b, t, H, DH).transpose(0, 2, 1, 3)
        Kh = K.reshape(b, t, H, DH).transpose(0, 2, 1, 3)
        Vh = V.reshape(b, t, H, DH).transpose(0, 2, 1, 3)
        theta = ROPE_BASE ** (-2.0 * jnp.arange(DH // 2, dtype=jnp.float32) / DH)
        pos = jnp.arange(t, dtype=jnp.float32)
        angles = pos[:, None] * theta[None, :]
        cos = jnp.cos(angles).astype(Qh.dtype)
        sin = jnp.sin(angles).astype(Qh.dtype)
        Qr = _rope(Qh, cos, sin)
        Kr = _rope(Kh, cos, sin)
        scores = jnp.einsum('bhqd,bhkd->bhqk', Qr, Kr) * DH ** (-0.5)
        causal = jnp.triu(jnp.ones((t, t), dtype=bool), 1)
        neg = jnp.finfo(scores.dtype).min
        scores = jnp.where(causal[None, None], neg, scores)
        pattern = jax.nn.softmax(scores, axis=-1)
        heads = jnp.einsum('bhqk,bhkd->bhqd', pattern, Vh)
        out = heads.transpose(0, 2, 1, 3).reshape(b, t, d)
        return out @ W_o.T

    def _L0_ffn_ref(x, cn_w1, cn_b1, cn_w2, cn_b2, cn_w3, cn_b3, cn_w4, cn_b4, gc_w1, gc_b1, gc_w2, gc_b2, gc_w3, gc_b3, adaptive_range):
        import jax, jax.numpy as jnp
        import numpy as np
        B, S, DIM = (4, 512, 128)
        BASE_COUPLING = 0.1
        NUM_CYCLES = 3

        def _gelu(x):
            return jax.nn.gelu(x, approximate=False)

        def _coupling_net(h, w1, b1, w2, b2, w3, b3, w4, b4):
            h = _gelu(h @ w1 + b1)
            h = _gelu(h @ w2 + b2)
            h = _gelu(h @ w3 + b3)
            return jax.nn.sigmoid(h @ w4 + b4)

        def _global_net(h, w1, b1, w2, b2, w3, b3):
            h = _gelu(h @ w1 + b1)
            h = _gelu(h @ w2 + b2)
            return jax.nn.sigmoid(h @ w3 + b3)

        def _twist(x):
            o_r, o_i, p_r, p_i = jnp.split(x, 4, axis=-1)
            return jnp.concatenate([p_r, -p_i, -o_r, o_i], axis=-1)
        global_context = x.mean(axis=1, keepdims=True)
        gf = _global_net(global_context, gc_w1, gc_b1, gc_w2, gc_b2, gc_w3, gc_b3)
        out = x
        for _ in range(NUM_CYCLES):
            tf = _coupling_net(out, cn_w1, cn_b1, cn_w2, cn_b2, cn_w3, cn_b3, cn_w4, cn_b4)
            combined = 0.7 * gf + 0.3 * tf
            coupling = BASE_COUPLING + adaptive_range * (combined - 0.5) * 2.0
            out = out + coupling * _twist(out)
        return out

    def _L1_attn_ref(x, Uq, Vq, bq, Uk, Vk, bk, Uv, Vv, bv):
        import jax, jax.numpy as jnp
        import numpy as np
        B, S, D, H, R = (8, 128, 128, 8, 32)
        DH = D // H

        def _lowrank(xh, U, V, b):
            t = jnp.einsum('bshd,hrd->bshr', xh, V)
            return jnp.einsum('bshr,hdr->bshd', t, U) + b
        b_, s_, _ = x.shape
        xh = x.reshape(b_, s_, H, DH)
        q = _lowrank(xh, Uq, Vq, bq)
        k = _lowrank(xh, Uk, Vk, bk)
        v = _lowrank(xh, Uv, Vv, bv)
        scores = jnp.einsum('bqhd,bkhd->bhqk', q, k) / DH ** 0.5
        attn = jax.nn.softmax(scores, axis=-1)
        out = jnp.einsum('bhqk,bkhd->bqhd', attn, v)
        return out.reshape(b_, s_, D)

    def _L1_ffn_ref(x, norm_weight, router_weight, router_bias, fc1_weight, fc1_bias, fc2_weight, fc2_bias):
        import jax, jax.numpy as jnp
        import numpy as np
        import math
        B, L, D = (4, 512, 128)
        F = 512
        E = 16
        CAP_FACTOR = 1.0
        EPS = 1e-05
        b, l, d = x.shape
        n_tokens = b * l
        n_experts = router_weight.shape[0]
        capacity = max(1, math.ceil(CAP_FACTOR * n_tokens / n_experts))
        top_k = min(capacity, n_tokens)
        xf = x.reshape(n_tokens, d)
        rms = jnp.sqrt(jnp.mean(xf * xf, axis=-1, keepdims=True) + EPS)
        xn = xf / rms * norm_weight
        logits = xn @ router_weight.T + router_bias
        probs = jax.nn.softmax(logits, axis=-1)
        _, idx = jax.lax.top_k(logits.T, top_k)
        xe = xn[idx]
        h = jnp.einsum('ecd,efd->ecf', xe, fc1_weight) + fc1_bias[:, None, :]
        h = jax.nn.gelu(h, approximate=False)
        y = jnp.einsum('ecf,edf->ecd', h, fc2_weight) + fc2_bias[:, None, :]
        gates = jnp.take_along_axis(probs.T, idx, axis=1)
        flat_idx = idx.reshape(-1)
        contrib = (y * gates[:, :, None]).reshape(-1, d)
        output = jnp.zeros((n_tokens, d), dtype=x.dtype).at[flat_idx].add(contrib)
        gate_sums = jnp.zeros((n_tokens, 1), dtype=x.dtype).at[flat_idx].add(gates.reshape(-1, 1))
        assigned = gate_sums > 0
        output = jnp.where(assigned, output / jnp.where(assigned, gate_sums, 1.0), output)
        return output.reshape(b, l, d)
    x = L0_attn_X
    x = _layernorm(x + _L0_attn_ref(x, L0_attn_W_q, L0_attn_W_k, L0_attn_W_v, L0_attn_W_o), axis=-1)
    x = _layernorm(x + _L0_ffn_ref(x, L0_ffn_cn_w1, L0_ffn_cn_b1, L0_ffn_cn_w2, L0_ffn_cn_b2, L0_ffn_cn_w3, L0_ffn_cn_b3, L0_ffn_cn_w4, L0_ffn_cn_b4, L0_ffn_gc_w1, L0_ffn_gc_b1, L0_ffn_gc_w2, L0_ffn_gc_b2, L0_ffn_gc_w3, L0_ffn_gc_b3, L0_ffn_adaptive_range), axis=-1)
    x = _layernorm(x + _L1_attn_ref(x, L1_attn_Uq, L1_attn_Vq, L1_attn_bq, L1_attn_Uk, L1_attn_Vk, L1_attn_bk, L1_attn_Uv, L1_attn_Vv, L1_attn_bv), axis=-1)
    x = _layernorm(x + _L1_ffn_ref(x, L1_ffn_norm_weight, L1_ffn_router_weight, L1_ffn_router_bias, L1_ffn_fc1_weight, L1_ffn_fc1_bias, L1_ffn_fc2_weight, L1_ffn_fc2_bias), axis=-1)
    return x

_drawn_inputs = setup_inputs


def setup_inputs(seed=0):
    import zlib

    import numpy as np

    out = dict(_drawn_inputs(seed))
    spreads = {'L0_ffn_cn_b1': (0.0, 0.8),
     'L0_ffn_cn_b2': (0.0, 2.0),
     'L0_ffn_cn_b3': (0.0, 2.0),
     'L0_ffn_gc_b1': (0.0, 0.8),
     'L0_ffn_gc_b2': (0.0, 0.8),
     'L1_ffn_norm_weight': (1.0, 0.2),
     'L1_ffn_router_bias': (0.0, 2.0),
     'L1_ffn_fc1_bias': (0.0, 0.471),
     'L1_ffn_fc2_bias': (0.0, 0.1)}
    factors = {'L0_ffn_cn_w1': 5.505,
     'L0_ffn_cn_w2': 5.064,
     'L0_ffn_cn_w3': 4.701,
     'L0_ffn_cn_w4': 3.244,
     'L0_ffn_gc_w1': 8.0,
     'L0_ffn_gc_w2': 5.032,
     'L0_ffn_gc_w3': 7.324,
     'L1_attn_Uq': 8.0,
     'L1_attn_Vq': 8.0,
     'L1_attn_bq': 24.537,
     'L1_attn_Uk': 8.0,
     'L1_attn_Vk': 8.0,
     'L1_attn_Uv': 8.0,
     'L1_attn_Vv': 8.0,
     'L1_attn_bk': 8.0}
    for name, (base, spread) in spreads.items():
        noise = np.random.default_rng([zlib.crc32(name.encode()), seed]).standard_normal(out[name].shape)
        drawn = base * np.exp(spread * noise) if base else spread * noise
        out[name] = jnp.asarray(drawn.astype(out[name].dtype))
    for name, factor in factors.items():
        out[name] = (out[name] * factor).astype(out[name].dtype)
    return out
```

```python
from contextlib import ExitStack

import numpy as np

import concourse.bass as bass
from concourse import mybir

F32 = mybir.dt.float32
BF16 = mybir.dt.bfloat16
I32 = mybir.dt.int32
ALU = mybir.AluOpType
ACT = mybir.ActivationFunctionType
AX = mybir.AxisListType.X

P = 128
NB, T, D = 8, 256, 128
NTOK = NB * T
NT = NTOK // P
EPS = 1e-5
NE, F, CAP = 16, 512, 128
NF = F // P
GROW = D + NE
AROW = 132
ROWS = 96
MASKED = -1e30
RING = 4
TWO_ONES = float(np.array([0x3F803F80], np.uint32).view(np.float32)[0])
NBITS = 31
WRING = 4
XRING = 4

K_PART = (0, 0, 0, 1, 1, 2)
Q_PART = (0, 1, 2, 0, 1, 0)


class Layer:

    def __init__(self, name, heads, causal):
        self.name, self.H, self.DH, self.causal = name, heads, D // heads, causal
        self.halves = ROWS // (6 * self.DH)
        self.PH = heads // self.halves
        self.GU = 3 if causal else 4
        self.NG = heads // 4
        self.U = self.GU * self.NG
        self.shift = self.U + 7
        self.ring = 2 * self.GU
        misc = {}
        def put(slot, *step):
            misc.setdefault(slot, []).append(step)
        for b in range(NB):
            front = -1 if b < 2 else (b - 2) * self.U
            put(front + (2 if b >= 2 else 0), "q", b)
            put(front + (4 if b >= 2 else 0), "k", b)
            put(front + (5 if b >= 2 else 0), "split", b)
            free = (b - RING + 1) * self.U + self.shift if b >= RING else -1
            put(max(free, front + (6 if b >= 2 else 0)), "stack", b)
            put(max(free + 4, front + 7) if b >= RING else front + (7 if b >= 2 else 0), "v", b)
            put((b + 1) * self.U + 1, "max", b)
            tail = (b + 1) * self.U + self.shift + 2
            put(tail, "heads0", b)
            put(tail + 1, "heads1", b)
            put(tail + 3, "proj_in", b)
            put(tail + 4, "add", b)
            put(tail + 6, "norm", b)
            put(tail + 7, "turn", b)
        absent = set() if causal else {"k", "heads1", "proj_in"} | set()
        if not causal:
            absent |= {"add", "turn"}
        self.misc = {t: [s for s in steps if s[0] not in absent] for t, steps in misc.items()}
        self.first, self.last = -1, max(self.misc) + 1
        self.number, n = {}, 0
        for t in sorted(self.misc):
            for s in self.misc[t]:
                if s[0] not in ("norm", "split", "stack"):
                    self.number[s] = n
                    n += 1
        self.nmisc = n

    def slots(self):
        for t in range(self.first, self.last + 1):
            s = t if 0 <= t < NB * self.U else None
            m = t - self.shift
            m = m if 0 <= m < NB * self.U else None
            g = t - self.shift - 2
            g = g // self.GU - 1 if g >= self.GU and g % self.GU == 0 and g // self.GU <= NB * self.NG else None
            yield s, m, g, self.misc.get(t, [])


L0, L1 = Layer("l0", 16, True), Layer("l1", 8, False)

WEIGHTS = {}


def lay_columns():
    at = 0
    for name, width in (
        ("wq", D), ("wq_swap", D), ("wk", D), ("wk_swap", D), ("wv", D), ("rope", 2 * T),
        ("ident", P), ("wo", D), ("cw1", D), ("cw2", D // 2), ("cw3", D // 4), ("cw4", P), ("twist", D),
        ("gw1", D // 2), ("gw2", D // 4), ("gw3", P), ("bv", D),
        ("nw", D), ("rb", NE), ("rw", NE), ("fb1", NE * NF), ("cols", 16), ("iota", P), ("emask", NE),
        ("kval", 2), ("bits", NBITS),
    ):
        WEIGHTS[name] = (at, at + width)
        at += width
    return at


NW = lay_columns()
NW_FIRST = WEIGHTS["wo"][1]
COLS = {n: i for i, n in enumerate(("cb1", "cb2", "cb3", "cb4", "gb1", "gb2", "gb3", "range", "bq", "bk", "slot"))}
NCB = 128 + 512 + 512 + 128 + 128


def build_program(nc, xT_in, xtok_in, w_in, lowrank_in, cb_in, bits_in, ew_in, out):
    ctx = ExitStack()
    with ctx:
        def sb(name, shape, dt=F32):
            return ctx.enter_context(nc.sbuf_tensor(name, shape, dt))

        def sem(name):
            return ctx.enter_context(nc.semaphore(name))

        bank = [ctx.enter_context(nc.psum_tensor(f"bank{i}", [P, 512], F32)) for i in range(8)]
        score_bank, turned_bank, value_bank, misc_bank = bank[0:2], bank[2:4], bank[4:6], bank[6:8]

        parts_dram = {L.name: nc.dram_tensor(f"parts_{L.name}", [NB, 3, 2, P, T], BF16, kind="Internal").ap() for L in (L0, L1)}
        maxes_dram = {L.name: nc.dram_tensor(f"maxes_{L.name}", [NB, 2, L.H, T], BF16, kind="Internal").ap() for L in (L0, L1)}
        rows_dram = nc.dram_tensor("rows", [NTOK, GROW], F32, kind="Internal").ap()
        acc_dram = [nc.dram_tensor(f"acc{i}", [NTOK, AROW], F32, kind="Internal").ap() for i in range(2)]

        w = sb("w", [P, NW])
        cb = sb("cb", [P, NCB], BF16)
        bits = sb("bits", [P, NBITS], I32)
        xT0 = sb("xT0", [P, NTOK])
        x0 = sb("x0", [P, NT, D])
        x1 = sb("x1", [P, NT, D])
        x1T = sb("x1T", [P, NTOK])
        xf = xT0
        x2 = sb("x2", [P, NT, D])
        lowrank = x2[:].rearrange("p t c -> p (t c)")[:, 0:12 * D]
        x2T = x1T
        x3 = x1
        rot = sb("rot", [P, 2, 2, 2, T])
        qk = sb("qk", [P, 2, 2, T])
        ones_t = sb("ones_t", [1, P])
        fstats, fmv, frstd = sb("fstats", [P, NT, 6]), sb("fmv", [P, NT, 2]), sb("frstd", [P, NT])
        left = rot[:, :, :, 0]
        parts = sb("parts", [P, 2, 3, 2, T], BF16)
        kst_all = sb("kst", [P, RING, 8, T], BF16)
        kst = [kst_all[:, r] for r in range(RING)]
        qst_all = sb("qst", [P, RING, 2, 8, T], BF16)
        qst = [[qst_all[:, r, h] for h in range(2)] for r in range(RING)]
        shared = qst_all[:].rearrange("p r h i t -> p (r h i t)").bitcast(F32)
        vst_all = sb("vst", [P, RING, 2, L0.H, 32])
        vst = {"l0": [vst_all[:, r] for r in range(RING)],
               "l1": [vst_all[:, r, 0].rearrange("p (k h) c -> p k h c", k=2) for r in range(RING)]}
        negmax = sb("negmax", [P, RING, 2, 16])
        maxT = sb("maxT", [16, RING, 2, T], BF16)
        probsT = sb("probsT", [P, 8, 512])
        headsT = sb("headsT", [P, 2, 4, T])
        rsum = sb("rsum", [P, 2, 16])
        heads = sb("heads", [P, 2, 2, D])
        headsF = sb("headsF", [P, 2, T])
        res = sb("res", [P, 2, 2, D])
        stats = sb("stats", [P, 2, 4, 6])
        mv = sb("mv", [P, 2, 4, 2])
        vpe = sb("vpe", [P, 2, 4])
        rstd = sb("rstd", [P, 2, 4])
        mhalf = sb("mhalf", [P, 16])
        lr = sb("lr", [P, 3, D])

        def qk_of(L, b):
            return qk[:, b % 2]

        def W(name):
            a, b = WEIGHTS[name]
            return w[:, a:b]

        def col(name, rows=P):
            a = WEIGHTS["cols"][0] + COLS[name]
            return w[0:rows, a:a + 1]

        ident = W("ident")
        identb, maskq, maskk = cb[:, 0:128], cb[:, 128:640], cb[:, 640:1152]
        same_expert, earlier = cb[:, 1152:1280], cb[:, 1280:1408]

        s_first, s_late, s_init_pool, s_init_dve, s_zero = sem("s_first"), sem("s_late"), sem("s_init_pool"), sem("s_init_dve"), sem("s_zero")
        S = {}
        for L in (L0, L1):
            for n in ("misc_ready", "misc_read", "added", "kept", "rest", "split", "score", "maxed", "turned", "exped",
                      "pv", "copied", "stats", "rstd", "normed", "written", "maxwritten"):
                S[L.name, n] = sem(f"{n}_{L.name}")
            for r in range(RING):
                S[L.name, "stacked", r] = sem(f"stacked{r}_{L.name}")
                S[L.name, "maxrows", r] = sem(f"maxrows{r}_{L.name}")
        dve_self, act_self, pool_self = sem("dve_self"), sem("act_self"), sem("pool_self")
        f_z, f_act, f_T, f_x, f_gf, f_gact, f_coef, f_r, f_stats, f_rstd, f_norm, f_tr, f_ev = (sem("f_" + n) for n in (
            "z", "act", "T", "x", "gf", "gact", "coef", "r", "stats", "rstd", "norm", "tr", "ev"))
        c_w, c_ev, f_pad = sem("c_w"), sem("c_ev"), sem("f_pad")
        NCHUNK, CH = 4, 512
        hid1 = shared[:, 0:NCHUNK * CH].rearrange("p (c t) -> p c t", c=NCHUNK)
        hid2 = probsT[:, 0:NCHUNK, :]
        tanh = shared[:, NCHUNK * CH:2 * NCHUNK * CH].rearrange("p (c t) -> p c t", c=NCHUNK)
        gsum = sb("gsum", [P, NB])
        gh1, gh2, gt = sb("gh1", [P, NB]), sb("gh2", [P, NB]), sb("gt", [P, NB])
        halfb = sb("halfb", [P, 2])
        coefA, coefB = sb("coefA", [P, NB]), sb("coefB", [P, 2])

        m_ms, m_rr, m_xn, m_tr, m_ev, m_log, m_L, m_z, m_exp, m_probs, m_rows, m_LT, m_cnt, m_tot, m_base, m_tot2, m_base2, m_oh, m_pos, m_idx = (
            sem("m_" + n) for n in ("ms", "rr", "xn", "tr", "ev", "log", "L", "z", "exp", "probs", "rows", "LT", "cnt",
                                    "tot", "base", "tot2", "base2", "oh", "pos", "idx"))
        m_count = sem("m_count")
        e_g = [sem(f"e_g{i}") for i in range(XRING)]
        e_w = [sem(f"e_w{i}") for i in range(WRING)]
        e_xt, e_xtc, e_h, e_gelu, e_y, e_yg = (sem("e_" + n) for n in ("xt", "xtc", "h", "gelu", "y", "yg"))
        e_add = [sem(f"e_add{i}") for i in range(2)]
        s_acc, d_sum, d_stats, d_rstd, d_norm, s_out = sem("s_acc"), sem("d_sum"), sem("d_stats"), sem("d_rstd"), sem("d_norm"), sem("s_out")
        rows = probsT[:].rearrange("p u t -> p (u t)")[:, 0:NT * GROW].rearrange("p (t c) -> p t c", t=NT)
        ms, rr = sb("ms", [P, NT]), sb("rr", [P, NT])
        junk = sb("junk", [P, 2, P])
        logit = sb("logit", [P, NT, NE])
        lmax, lsum, lrec = sb("lmax", [P, NT]), sb("lsum", [P, NT]), sb("lrec", [P, NT])
        lz = sb("lz", [P, NT, NE])
        LT = sb("LT", [P, 2, P])
        ubits, xbits, cand, inc = (sb(n, [P, 1], I32) for n in ("ubits", "xbits", "cand", "inc"))
        cnt = sb("cnt", [P, 1], BF16)
        gcount = sb("gcount", [P, 1], BF16)
        gtm, eqm, scan, selm = (sb(n, [P, 2, P]) for n in ("gtm", "eqm", "scan", "selm"))
        tot, tot2 = sb("tot", [P, 2], BF16), sb("tot2", [P, 2], BF16)
        base, lim, cend = sb("base", [P, 4]), sb("lim", [P, 2]), sb("cend", [P, 2])
        place = sb("place", [P, 2, P], BF16)
        oh = sb("oh", [P, 2, P], BF16)
        kst_flat = kst_all[:].rearrange("p r i t -> p (r i t)")
        ohe = kst_flat[:, 0:NE * 2 * P].rearrange("p (e h s) -> p e h s", e=NE, h=2)
        kvalb = sb("kvalb", [P, 2], BF16)
        le = kst_flat[:, NE * 2 * P:NE * 3 * P].rearrange("p (e j) -> p e j", e=NE)
        cntj = sb("cntj", [P, NE])
        idx = sb("idx", [P, NE], I32)
        ew = [sb(f"ew{i}", [P, 2 * F + D]) for i in range(WRING)]
        xe = [sb(f"xe{i}", [P, GROW]) for i in range(XRING)]
        xeT = [sb(f"xeT{i}", [P, P]) for i in range(2)]
        hidT = [headsT[:, i].rearrange("p f t -> p (f t)")[:, 0:NF * CAP].rearrange("p (f t) -> p f t", f=NF) for i in range(2)]
        yg = [sb(f"yg{i}", [P, AROW]) for i in range(2)]
        acc = [shared[:, i * NT * AROW:(i + 1) * NT * AROW].rearrange("p (t c) -> p t c", t=NT) for i in range(2)]
        zero = sb("zero", [P, NT * AROW // 8])

        block = ctx.enter_context(nc.Block())

        @block.sync
        def _(sp):
            sp.dma_start(w[:, 0:NW_FIRST], w_in[:, 0:NW_FIRST]).then_inc(s_first, 16)
            sp.dma_start(xT0[:], xT_in).then_inc(s_first, 16)
            sp.dma_start(cb[:], cb_in).then_inc(s_first, 16)

            def late_loads(t):
                if t == 1:
                    sp.dma_start(w[:, NW_FIRST:NW], w_in[:, NW_FIRST:NW]).then_inc(s_late, 16)
                    sp.dma_start(lowrank, lowrank_in).then_inc(s_late, 16)
                    sp.dma_start(x0[:], xtok_in).then_inc(s_late, 16)
                    sp.dma_start(bits[:], bits_in).then_inc(s_late, 16)
                if t == 2 * L0.U:
                    for a in range(2):
                        for i in range(8):
                            view = acc_dram[a].rearrange("(i p n) c -> i p (n c)", p=P, i=8)
                            sp.dma_start(view[i], zero[:]).then_inc(s_zero, 16)
                if t == 4 * L0.U:
                    for e in range(WRING):
                        sp.dma_start(ew[e][:], ew_in[e]).then_inc(e_w[e], 16)

            def unstacked(L, b):
                sp.wait_ge(S[L.name, "split"], b + 1)
                if b >= 1:
                    sp.wait_ge(S[L.name, "written"], 16 * b)
                sp.dma_start(parts_dram[L.name][b].rearrange("a s f t -> f (a s) t"),
                             parts[:, b % 2].rearrange("p a s t -> p (a s) t")).then_inc(S[L.name, "written"], 16)

            def stack(L, b):
                r = b % RING
                sp.wait_ge(S[L.name, "written"], 16 * (b + 1))
                if b >= RING:
                    sp.wait_ge(S[L.name, "turned"], L.U * (b - RING + 1))
                n = L.DH
                for h in range(L.halves):
                    for c, m in ((0, 3), (3, 2), (5, 1)):
                        at = (6 * h + c) * n
                        src = parts_dram[L.name][b, :, :, h * 64:h * 64 + n * 8, :].rearrange("a s (d p) t -> a s d (p t)", p=8)
                        k_src = src[K_PART[c], 1].unsqueeze(0).to_broadcast([m, n, 8 * T])
                        for t, x in ((kst[r], k_src), (qst[r][h], src[0:m, 0])):
                            sp.dma_start(t[at:at + m * n].rearrange("r p t -> r (p t)"), x)\
                              .then_inc(S[L.name, "stacked", r], 16)

            def max_rows(L, b):
                r = b % RING
                sp.wait_ge(S[L.name, "misc_read"], L.number["max", b] + 1)
                sp.dma_start(maxes_dram[L.name][b].rearrange("a h t -> h a t"), maxT[0:L.H, r])\
                  .then_inc(S[L.name, "maxwritten"], 16)
                sp.wait_ge(S[L.name, "maxwritten"], 16 * (b + 1))
                for h in range(L.halves):
                    sp.dma_start(qst[r][h][ROWS:ROWS + 2, :, :], maxes_dram[L.name][b, :, 8 * h:8 * h + 8, :])\
                      .then_inc(S[L.name, "maxrows", r], 16)

            sp.wait_ge(s_init_dve, 1)
            sp.wait_ge(s_init_pool, 1)
            for L in (L0, L1):
                for t, (_, _, _, steps) in enumerate(L.slots()):
                    if L is L0:
                        late_loads(t)
                    for kind, b in steps:
                        if kind == "split":
                            unstacked(L, b)
                        if kind == "stack":
                            stack(L, b)
                        if kind == "max":
                            max_rows(L, b)
            sp.wait_ge(m_probs, 1)
            sp.dma_start(rows_dram.rearrange("(t p) c -> p t c", p=P), rows).then_inc(m_rows, 16)
            for e in range(WRING, NE):
                sp.wait_ge(e_y, e - WRING + 1)
                sp.dma_start(ew[e % WRING][:], ew_in[e]).then_inc(e_w[e % WRING], 16)
            for a in range(2):
                sp.wait_ge(e_add[a], 16 * (NE // 2))
                sp.dma_start(acc[a], acc_dram[a].rearrange("(t p) c -> p t c", p=P)).then_inc(s_acc, 16)
            sp.wait_ge(d_norm, NT)
            sp.dma_start(out.rearrange("(t p) c -> p t c", p=P), x0[:]).then_inc(s_out, 16)
            sp.wait_ge(s_zero, 16 * 16)
            sp.wait_ge(s_out, 16)

        @block.tensor
        def _(pe):
            mm = nc.tensor.matmul
            tr = nc.tensor.transpose

            def attention(L, xT, wq, wk, wv):
                U, sems = L.U, lambda n: S[L.name, n]

                def misc(step):
                    n = L.number[step]
                    if n >= 2:
                        pe.wait_ge(sems("misc_read"), n - 1)
                    return misc_bank[n % 2]

                def score_unit(n):
                    b, u = divmod(n, U)
                    g, k = divmod(u, L.GU)
                    r = b % RING
                    if u == 0:
                        pe.wait_ge(S[L.name, "stacked", r], 16 * 6 * L.halves * (b // RING + 1))
                    if n >= 2:
                        pe.wait_ge(sems("maxed"), n - 1)
                    o = score_bank[n % 2]
                    if not L.causal:
                        for qt in range(2):
                            x = mm(o[:, qt * T:qt * T + T], qst[r][0][0:ROWS, u, qt * P:qt * P + P],
                                   kst[r][0:ROWS, u, :], start=True, stop=True)
                    else:
                        hs = range(4 * g, 4 * g + 4) if k == 0 else range(4 * g + 2 * k - 2, 4 * g + 2 * k)
                        qt, nk = (0, P) if k == 0 else (1, T)
                        ov = o[:].rearrange("p (h k) -> p h k", k=nk)
                        mm(ov[:, :, nk - P:nk], identb, maskq[:, 0:len(hs) * P].rearrange("p (h k) -> p h k", k=P),
                           start=True, stop=False, skip_group_check=True)
                        for i, h in enumerate(hs):
                            x = mm(ov[:, i, :], qst[r][h // 8][0:ROWS, h % 8, qt * P:qt * P + P],
                                   kst[r][0:ROWS, h % 8, 0:nk], start=False, stop=True, skip_group_check=True)
                    x.then_inc(sems("score"), 1)

                def turned_unit(m):
                    b, u = divmod(m, U)
                    g, k = divmod(u, L.GU)
                    r = b % RING
                    if u == 0:
                        pe.wait_ge(S[L.name, "maxrows", r], 16 * L.halves * (b // RING + 1))
                    if m >= 2:
                        pe.wait_ge(sems("exped"), m - 1)
                    o = turned_bank[m % 2]
                    K = ROWS + 2
                    if not L.causal:
                        for kt in range(2):
                            x = mm(o[:, kt * T:kt * T + T], kst[r][0:K, u, kt * P:kt * P + P],
                                   qst[r][0][0:K, u, :], start=True, stop=True)
                    else:
                        hs = range(4 * g + 2 * k, 4 * g + 2 * k + 2) if k < 2 else range(4 * g, 4 * g + 4)
                        kt, nq = (0, T) if k < 2 else (1, P)
                        ov = o[:].rearrange("p (h q) -> p h q", q=nq)
                        mm(ov[:, :, 0:P], identb, maskk[:, 0:len(hs) * P].rearrange("p (h k) -> p h k", k=P),
                           start=True, stop=False, skip_group_check=True)
                        for i, h in enumerate(hs):
                            x = mm(ov[:, i, :], kst[r][0:K, h % 8, kt * P:kt * P + P],
                                   qst[r][h // 8][0:K, h % 8, T - nq:T], start=False, stop=True, skip_group_check=True)
                    x.then_inc(sems("turned"), 1)

                def value_group(G):
                    b, g = divmod(G, L.NG)
                    pe.wait_ge(sems("exped"), L.GU * (G + 1))
                    pe.wait_ge(sems("misc_read"), L.number["v", b] + 1)
                    if G >= 2:
                        pe.wait_ge(sems("copied"), G - 1)
                    elif L is L0:
                        pe.wait_ge(c_ev, 1)
                    o = value_bank[G % 2]
                    v = vst[L.name][b % RING]
                    for kt in range(2):
                        for j in range(4):
                            if L.causal:
                                unit = L.GU * G + (j // 2 if kt == 0 else 2)
                                pr = probsT[:, unit % L.ring, :]
                                pr, q0 = (pr[:, (j % 2) * T:(j % 2) * T + T], 0) if kt == 0 else (pr[:, j * P:j * P + P], P)
                            else:
                                pr, q0 = probsT[:, (L.GU * G + j) % L.ring, kt * T:kt * T + T], 0
                            x = mm(o[32 * j:32 * j + 32, q0:T], v[:, kt, 4 * g + j, :], pr,
                                   start=(kt == 0), stop=(kt == 1), skip_group_check=True)
                    x.then_inc(sems("pv"), 1)

                def step(kind, b):
                    if kind in ("norm", "split", "stack"):
                        return
                    o = misc((kind, b))
                    x = None
                    cols = slice(b * T, b * T + T)
                    if kind in ("q", "k"):
                        for i, ww in enumerate(wq if kind == "q" else wk):
                            x = mm(o[:, i * T:i * T + T], ww, xT[:, cols], start=True, stop=True)
                    elif kind == "v":
                        for i in range(2):
                            x = mm(o[:, i * P:i * P + P], xT[:, b * T + i * P:b * T + i * P + P], wv, start=True, stop=True)
                    elif kind == "max":
                        pe.wait_ge(sems("maxed"), U * (b + 1))
                        for i in range(2):
                            x = tr(o[0:L.H, i * P:i * P + P], negmax[:, b % RING, i, 0:L.H], ident)
                    elif kind in ("heads0", "heads1"):
                        pe.wait_ge(sems("copied"), L.NG * (b + 1))
                        for qt in ((0, 1) if not L.causal else (int(kind[-1]),)):
                            for g in range(L.NG):
                                at = g * P + (qt * T if not L.causal else 0)
                                x = tr(o[:, at:at + P], headsT[:, b % 2, g, qt * P:qt * P + P], ident)
                    elif kind == "proj_in":
                        pe.wait_ge(sems("misc_read"), L.number["heads1", b] + 1)
                        for i in range(2):
                            x = tr(o[:, i * P:i * P + P], heads[:, b % 2, i, :], ident)
                    elif kind == "add":
                        pe.wait_ge(sems("misc_read"), L.number["proj_in", b] + 1)
                        for i in range(2):
                            x = mm(o[:, i * P:i * P + P], headsF[:, b % 2, i * P:i * P + P], W("wo"), start=True, stop=True)
                    elif kind == "turn":
                        pe.wait_ge(sems("normed"), b + 1)
                        for i in range(2):
                            x = tr(o[:, i * P:i * P + P], x1[:, 2 * b + i, :], ident)
                    x.then_inc(sems("misc_ready"), 1)

                for s, m, g, steps in L.slots():
                    if L is L0 and s == L.U:
                        compose()
                    if s is not None:
                        score_unit(s)
                    if m is not None:
                        turned_unit(m)
                    if g is not None:
                        value_group(g)
                    for st in steps:
                        step(*st)

            def compose():
                pe.wait_ge(s_late, 64)
                for i in range(3):
                    for c in range(2):
                        at = (2 * i + c) * 2 * D
                        v_f, u_f = lowrank[:, at:at + D], lowrank[:, at + D:at + 2 * D]
                        x = mm(value_bank[0][:, i * D:i * D + D], v_f, u_f, start=(c == 0), stop=(c == 1))
                x.then_inc(c_w, 1)

            pe.wait_ge(s_first, 48)
            pe.wait_ge(s_init_pool, 1)
            pe.wait_ge(s_init_dve, 1)
            attention(L0, xT0, (W("wq"), W("wq_swap")), (W("wk"), W("wk_swap")), W("wv"))

            pe.wait_ge(S["l0", "misc_read"], L0.nmisc)
            pe.wait_ge(S["l0", "exped"], NB * L0.U)
            pe.wait_ge(S["l0", "maxed"], NB * L0.U)
            pe.wait_ge(S["l0", "copied"], NB * L0.NG)
            n = 0
            for cyc in range(3):
                for layer in range(4):
                    for c in range(NCHUNK):
                        sl = slice(c * CH, c * CH + CH)
                        if n >= 4:
                            pe.wait_ge(f_act, n - 3)
                        o = bank[n % 4]
                        if layer == 0:
                            if cyc > 0:
                                pe.wait_ge(f_x, NCHUNK * (cyc - 1) + c + 1)
                            else:
                                pe.wait_ge(f_pad, 1)
                            x = mm(o[:], W("cw1"), (x1T if cyc == 0 else xf)[:, sl], start=True, stop=True)
                        else:
                            pe.wait_ge(f_act, n - 3)
                            src = (hid1, hid2, hid2)[layer - 1]
                            if layer == 1:
                                x = mm(o[0:64, :], W("cw2"), src[:, c, :], start=True, stop=True)
                            elif layer == 2:
                                x = mm(o[64:96, :], W("cw3"), src[:, c, :], start=True, stop=True)
                            else:
                                x = mm(o[:], W("cw4"), src[:, c, :], start=True, stop=True)
                        x.then_inc(f_z, 1)
                        n += 1
                    if layer == 0:
                        for c in range(NCHUNK):
                            if cyc > 0:
                                pe.wait_ge(f_x, NCHUNK * (cyc - 1) + c + 1)
                            mm(bank[4 + c][:], W("twist"), (x1T if cyc == 0 else xf)[:, c * CH:c * CH + CH],
                               start=True, stop=True).then_inc(f_T, 1)
                if cyc == 0:
                    pe.wait_ge(f_act, n)
                    for i, (wn, src, m_) in enumerate((("gw1", gsum, 64), ("gw2", gh1, 32), ("gw3", gh2, 128))):
                        pe.wait_ge(f_gf, 1) if i == 0 else pe.wait_ge(f_gact, i)
                        mm(bank[0][0:m_, 0:NB], W(wn), src[:], start=True, stop=True).then_inc(f_r, 1)
                    pe.wait_ge(f_gact, 3)
            for c in range(NCHUNK):
                pe.wait_ge(f_x, NCHUNK * 3 + c + 1)
                for i in range(4):
                    x = tr(bank[c][:, i * P:i * P + P], xf[:, c * CH + i * P:c * CH + i * P + P], ident)
                x.then_inc(f_tr, 1)
            for c in range(NCHUNK):
                pe.wait_ge(f_norm, c + 1)
                for i in range(4):
                    x = tr(bank[4 + c][:, i * P:i * P + P], x2[:, 4 * c + i, :], ident)
                x.then_inc(f_tr, 1)

            pe.wait_ge(f_ev, 4)
            attention(L1, x2T, (lr[:, 0, :], lr[:, 1, :]), None, lr[:, 2, :])

            pe.wait_ge(S["l1", "misc_read"], L1.nmisc)
            pe.wait_ge(S["l1", "exped"], NB * L1.U)
            pe.wait_ge(S["l1", "maxed"], NB * L1.U)
            pe.wait_ge(S["l1", "copied"], NB * L1.NG)
            for c in range(4):
                pe.wait_ge(m_xn, 4 * c + 4)
                for i in range(4):
                    x = tr(bank[c][:, i * P:i * P + P], rows[:, 4 * c + i, 0:D], ident)
                x.then_inc(m_tr, 1)
            for t in range(NT):
                if t % 4 == 0:
                    pe.wait_ge(m_ev, t // 4 + 1)
                x = mm(bank[4][:, t * NE:t * NE + NE], x2T[:, t * P:t * P + P], W("rw"), start=True, stop=True)
            x.then_inc(m_log, 1)
            pe.wait_ge(m_L, 1)
            lf = logit[:].rearrange("p t e -> p (t e)")
            for i in range(2):
                x = tr(bank[5][:, i * P:i * P + P], lf[:, i * P:i * P + P], ident)
            x.then_inc(m_LT, 1)
            pe.wait_ge(m_cnt, 1)
            mm(bank[6][:, 0:1], same_expert, cnt[:], start=True, stop=True).then_inc(m_count, 1)
            with pe.Fori(0, NBITS) as i:
                pe.wait_ge(m_cnt, i + 2)
                mm(bank[6][:, 0:1], same_expert, cnt[:], start=True, stop=True).then_inc(m_count, 1)
            pe.wait_ge(m_tot, 1)
            mm(bank[7][:, 2:4], earlier, tot[:], start=True, stop=False, skip_group_check=True)
            mm(bank[7][:, 3:4], same_expert, tot[:, 0:1], start=False, stop=True, skip_group_check=True)
            mm(bank[7][:, 0:1], same_expert, gcount[:], start=True, stop=True, skip_group_check=True).then_inc(m_base, 1)
            pe.wait_ge(m_tot2, 1)
            mm(bank[7][:, 2:4], earlier, tot2[:], start=True, stop=False, skip_group_check=True)
            mm(bank[7][:, 3:4], same_expert, tot2[:, 0:1], start=False, stop=True, skip_group_check=True).then_inc(m_base2, 1)
            for e in range(NE):
                pe.wait_ge(m_oh, e + 1)
                for h in range(2):
                    mm(bank[e // 4][:, e % 4 * P:e % 4 * P + P], ohe[:, e, h, :], place[:, h, :], start=(h == 0), stop=(h == 1))
                for h in range(2):
                    x = mm(bank[4][:, e:e + 1], ohe[:, e, h, :], kvalb[:, h:h + 1], start=(h == 0), stop=(h == 1))
                if e % 4 == 3:
                    x.then_inc(m_pos, 1)
            pe.wait_ge(m_idx, 1)

            def turn_tokens(e):
                pe.wait_ge(e_g[e % XRING], 16 * (e // XRING + 1))
                if e >= 2:
                    pe.wait_ge(e_xtc, e - 1)
                tr(bank[e % 2][:, 0:P], xe[e % XRING][:, 0:D], ident).then_inc(e_xt, 1)

            turn_tokens(0)
            for e in range(NE):
                if e + 1 < NE:
                    turn_tokens(e + 1)
                pe.wait_ge(e_w[e % WRING], 16 * (e // WRING + 1))
                pe.wait_ge(e_xtc, e + 1)
                if e >= 2:
                    pe.wait_ge(e_gelu, e - 1)
                o = bank[2 + e % 2]
                for f in range(NF):
                    x = mm(o[:, f * CAP:f * CAP + CAP], ew[e % WRING][:, f * P:f * P + P], xeT[e % 2][:], start=True, stop=True)
                x.then_inc(e_h, 1)
                pe.wait_ge(e_gelu, e + 1)
                if e >= 2:
                    pe.wait_ge(e_yg, e - 1)
                o = bank[4 + e % 2]
                mm(o[:, 0:D], ones_t[0:1, :], ew[e % WRING][0:1, 2 * F:2 * F + D], start=True, stop=False)
                for f in range(NF):
                    x = mm(o[:, 0:D], hidT[e % 2][:, f, :], ew[e % WRING][:, F + f * D:F + f * D + D], start=False, stop=(f == NF - 1))
                x.then_inc(e_y, 1)

        @block.vector
        def _(dve):
            v = nc.vector
            steps_done = [0]

            def settle(ins):
                ins.then_inc(dve_self, 1)
                steps_done[0] += 1
                dve.wait_ge(dve_self, steps_done[0])

            def attention(L):
                U, sems = L.U, lambda n: S[L.name, n]

                def own_max(n):
                    b, u = divmod(n, U)
                    g, k = divmod(u, L.GU)
                    dve.wait_ge(sems("score"), n + 1)
                    o = score_bank[n % 2][:]
                    nm = negmax[:, b % RING]
                    if not L.causal:
                        dst, src = nm[:, :, u], o.rearrange("p (h k) -> p h k", k=T)
                    elif k == 0:
                        dst, src = nm[:, 0, 4 * g:4 * g + 4], o.rearrange("p (h k) -> p h k", k=P)
                    else:
                        dst, src = nm[:, 1, 4 * g + 2 * k - 2:4 * g + 2 * k], o.rearrange("p (h k) -> p h k", k=T)
                    v.tensor_reduce(dst, src, AX, ALU.max, negate=True).then_inc(sems("maxed"), 1)

                def ready(step):
                    n = L.number[step]
                    dve.wait_ge(sems("misc_ready"), n + 1)
                    return misc_bank[n % 2]

                def read(ins):
                    ins.then_inc(sems("misc_read"), 1)

                def step(kind, b):
                    if kind == "norm":
                        dve.wait_ge(sems("rstd"), b + 1)
                        for i in range(2):
                            x = v.tensor_scalar((x1 if L is L0 else x3)[:, 2 * b + i, :], res[:, b % 2, i, :],
                                                mv[:, b % 2, i, 0:1], rstd[:, b % 2, i:i + 1], ALU.subtract, ALU.mult)
                        x.then_inc(sems("normed"), 1)
                        return
                    if kind in ("split", "stack"):
                        return
                    o = ready((kind, b))
                    o2 = o[:].rearrange("p (i c) -> p i c", i=2)
                    if kind in ("q", "k"):
                        if L.causal:
                            if b >= 2:
                                dve.wait_ge(sems("split"), b - 1)
                            read(v.tensor_tensor(rot[:, b % 2, "qk".index(kind)], o2,
                                                 W("rope").rearrange("p (i c) -> p i c", i=2), ALU.mult))
                        else:
                            if b >= 1:
                                dve.wait_ge(sems("split"), b)
                            v.tensor_scalar(qk[:, b % 2, 0, :], o2[:, 0], col("bq"), None, ALU.add)
                            read(v.tensor_scalar(qk[:, b % 2, 1, :], o2[:, 1], col("bk"), None, ALU.add))
                    elif kind == "v":
                        if b >= RING:
                            dve.wait_ge(sems("pv"), L.NG * (b - RING + 1))
                        dst = vst[L.name][b % RING][:, :, :, 0:L.DH]
                        src = o[:, 0:T].rearrange("p (k h d) -> p k h d", k=2, h=L.H)
                        if L.causal:
                            read(v.tensor_copy(dst, src))
                        else:
                            bv = W("bv").rearrange("p (h d) -> p h d", h=L.H)
                            v.tensor_tensor(dst[:, 0], src[:, 0], bv, ALU.add)
                            read(v.tensor_tensor(dst[:, 1], src[:, 1], bv, ALU.add))
                    elif kind == "max":
                        if b >= RING:
                            dve.wait_ge(sems("maxwritten"), 16 * (b - RING + 1))
                        settle(v.tensor_copy(maxT[0:L.H, b % RING, 0, :], o[0:L.H, 0:T]))
                        read(v.tensor_tensor(maxT[0:L.H, b % RING, 1, :], o[0:L.H, 0:T], maxT[0:L.H, b % RING, 0, :], ALU.subtract))
                    elif kind in ("heads0", "heads1"):
                        for qt in ((0, 1) if not L.causal else (int(kind[-1]),)):
                            ov = (o[:] if L.causal else o2[:, qt]).rearrange("p (h c) -> p h c", c=32)
                            n = L.DH
                            rs = rsum[:, qt, 0:L.H]
                            settle(v.reciprocal(rs, ov[:, :, n]))
                            hv = heads[:, b % 2, qt, :].rearrange("p (h c) -> p h c", c=n)
                            x = v.tensor_tensor(hv, ov[:, :, 0:n], rs.unsqueeze(2).to_broadcast([P, L.H, n]), ALU.mult)
                            if L.causal or qt == 1:
                                read(x)
                        if not L.causal:
                            dve.wait_ge(sems("misc_read"), L.number[kind, b] + 1)
                            settle(v.tensor_tensor(res[:, b % 2], heads[:, b % 2], x2[:, 2 * b:2 * b + 2, :], ALU.add))
                            norm_stats(b)
                    elif kind == "proj_in":
                        read(v.tensor_copy(headsF[:, b % 2, :], o[:, 0:T]))
                    elif kind == "add":
                        read(v.tensor_tensor(res[:, b % 2], o[:, 0:T].rearrange("p (i c) -> p i c", i=2), x0[:, 2 * b:2 * b + 2, :], ALU.add))
                        dve.wait_ge(sems("misc_read"), L.number[kind, b] + 1)
                        norm_stats(b)
                    elif kind == "turn":
                        read(v.tensor_copy(x1T[:, b * T:b * T + T], o[:, 0:T]))

                def norm_stats(b):
                    for i in range(2):
                        x = v.bn_stats(stats[:, b % 2, i, :], res[:, b % 2, i, :])
                    settle(x)
                    for i in range(2):
                        x = v.bn_aggr(mv[:, b % 2, i, :], stats[:, b % 2, i, :])
                    x.then_inc(sems("stats"), 1)

                for s, m, g, steps in L.slots():
                    if L is L0 and s == L.U:
                        dve.wait_ge(c_w, 1)
                        v.tensor_copy(lr[:].rearrange("p i c -> p (i c)"), value_bank[0][:, 0:3 * D]).then_inc(c_ev, 1)
                        dve.wait_ge(s_late, 64)
                        v.tensor_scalar(halfb[:, 0:1], col("cb4"), 0.5, None, ALU.mult)
                        v.tensor_scalar(halfb[:, 1:2], col("gb3"), 0.5, None, ALU.mult)
                        v.tensor_scalar(coefB[:, 0:1], col("range"), 0.3, None, ALU.mult)
                        v.tensor_scalar(coefB[:, 1:2], col("range"), 0.7, None, ALU.mult)
                    if s is not None:
                        own_max(s)
                    for st in steps:
                        step(*st)

            v.memset(qst_all[0:ROWS].rearrange("p r h i t -> p (r h i t)").bitcast(F32), 0.0)
            v.memset(zero[:], 0.0)
            v.memset(gh1[64:128], 0.0)
            v.memset(gh2[32:64], 0.0)
            v.memset(gh2[64:128], 0.0)
            v.memset(mhalf[:], -0.5).then_inc(s_init_dve, 1)
            dve.wait_ge(s_first, 48)
            dve.wait_ge(s_init_pool, 1)
            dve.wait_ge(s_init_dve, 1)
            attention(L0)

            dve.wait_ge(S["l0", "misc_read"], L0.nmisc)
            v.tensor_reduce(gsum[:], x1T[:].rearrange("p (b t) -> p b t", t=T), AX, ALU.add).then_inc(f_gf, 1)
            dve.wait_ge(f_gf, 1)
            dve.wait_ge(f_gact, 3)
            v.tensor_scalar(coefA[:], gt[:], coefB[:, 1:2], 0.1, ALU.mult, ALU.add).then_inc(f_coef, 1)
            dve.wait_ge(f_coef, 1)
            for cyc in range(3):
                for c in range(NCHUNK):
                    sl = slice(c * CH, c * CH + CH)
                    dve.wait_ge(f_act, 16 * cyc + 13 + c)
                    for i in range(2):
                        x = v.tensor_scalar(tanh[:, c, i * T:i * T + T], tanh[:, c, i * T:i * T + T], coefB[:, 0:1],
                                            coefA[:, 2 * c + i:2 * c + i + 1], ALU.mult, ALU.add)
                    settle(x)
                    dve.wait_ge(f_T, NCHUNK * cyc + c + 1)
                    settle(v.tensor_tensor(tanh[:, c, :], bank[4 + c][:], tanh[:, c, :], ALU.mult))
                    x = v.tensor_tensor(xf[:, sl], (x1T if cyc == 0 else xf)[:, sl], tanh[:, c, :], ALU.add)
                    x.then_inc(f_x, 1)
            for c in range(NCHUNK):
                sl = slice(c * CH, c * CH + CH)
                dve.wait_ge(f_x, 8 + c + 1)
                v.tensor_tensor(xf[:, sl], xf[:, sl], x1T[:, sl], ALU.add).then_inc(f_x, 1)
            for c in range(NCHUNK):
                dve.wait_ge(f_tr, c + 1)
                if c >= 2:
                    dve.wait_ge(f_rstd, c - 1)
                for i in range(4):
                    x = v.bn_stats(stats[:, c % 2, i, :], bank[c][:, i * P:i * P + P])
                settle(x)
                for i in range(4):
                    x = v.bn_aggr(mv[:, c % 2, i, :], stats[:, c % 2, i, :])
                x.then_inc(f_stats, 1)
                dve.wait_ge(f_rstd, c + 1)
                for i in range(4):
                    x = v.tensor_scalar(x2[:, 4 * c + i, :], bank[c][:, i * P:i * P + P], mv[:, c % 2, i, 0:1],
                                        rstd[:, c % 2, i:i + 1], ALU.subtract, ALU.mult)
                x.then_inc(f_norm, 1)
            dve.wait_ge(f_norm, 4)
            for r in range(RING):
                x = v.memset(vst["l1"][r][:, :, :, L1.DH:L1.DH + 1], 1.0)
            settle(x)
            attention(L1)

            dve.wait_ge(S["l1", "normed"], NB)
            for t in range(NT):
                x = v.tensor_tensor_reduce(shared[:, t * D:t * D + D], x3[:, t, :], x3[:, t, :], 1.0, 0.0, ALU.mult, ALU.add, ms[:, t:t + 1])
            x.then_inc(m_ms, 1)
            dve.wait_ge(m_rr, 1)
            for t in range(NT):
                v.scalar_tensor_tensor(out=rows[:, t, 0:D], in0=x3[:, t, :], scalar=rr[:, t:t + 1], in1=W("nw"),
                                       op0=ALU.mult, op1=ALU.mult).then_inc(m_xn, 1)
            dve.wait_ge(m_log, 1)
            v.tensor_tensor(logit[:], bank[4][:, 0:NT * NE].rearrange("p (t e) -> p t e", e=NE),
                            W("rb").unsqueeze(1).to_broadcast([P, NT, NE]), ALU.add).then_inc(m_L, 1)
            dve.wait_ge(m_L, 1)
            settle(v.tensor_reduce(lmax[:], logit[:], AX, ALU.max))
            v.tensor_tensor(lz[:], logit[:], lmax[:].unsqueeze(2).to_broadcast([P, NT, NE]), ALU.subtract).then_inc(m_z, 1)
            dve.wait_ge(m_exp, 1)
            settle(v.tensor_reduce(lsum[:], lz[:], AX, ALU.add))
            settle(v.reciprocal(lrec[:], lsum[:]))
            v.tensor_tensor(rows[:, :, D:GROW], lz[:], lrec[:].unsqueeze(2).to_broadcast([P, NT, NE]), ALU.mult).then_inc(m_probs, 1)

            dve.wait_ge(m_LT, 1)
            settle(v.tensor_copy(LT[:].rearrange("p h j -> p (h j)"), bank[5][:, 0:2 * P]))
            v.memset(ubits[:], 0)
            v.tensor_scalar(junk[:], LT[:], 0.0, 0.0, ALU.is_ge, ALU.add, accum_out=cnt[:]).then_inc(m_cnt, 1)
            dve.wait_ge(m_count, 1)
            settle(v.tensor_scalar(xbits[:], bank[6][:, 0:1], float(CAP), -1.0, ALU.is_lt, ALU.mult))
            done = steps_done[0]
            with dve.Fori(0, NBITS) as i:
                v.scalar_tensor_tensor(out=cand[:], in0=ubits[:], scalar=bits[:, bass.ds(i, 1)], in1=xbits[:],
                                       op0=ALU.bitwise_or, op1=ALU.bitwise_xor).then_inc(dve_self, 1)
                dve.wait_ge(dve_self, i * 3 + (done + 1))
                v.tensor_scalar(junk[:], LT[:], cand[:].bitcast(F32), 0.0, ALU.is_ge, ALU.add, accum_out=cnt[:]).then_inc(m_cnt, 1)
                dve.wait_ge(m_count, i + 2)
                v.tensor_scalar(inc[:], bank[6][:, 0:1], float(CAP), W("bits")[:, bass.ds(i, 1)], ALU.is_ge, ALU.mult).then_inc(dve_self, 1)
                dve.wait_ge(dve_self, i * 3 + (done + 2))
                v.tensor_tensor(ubits[:], ubits[:], inc[:], ALU.bitwise_or).then_inc(dve_self, 1)
                dve.wait_ge(dve_self, i * 3 + (done + 3))
            steps_done[0] = done + 3 * NBITS
            settle(v.tensor_tensor(cand[:], ubits[:], xbits[:], ALU.bitwise_xor))
            thr = cand[:].bitcast(F32)
            v.tensor_scalar(gtm[:], LT[:], thr, 0.0, ALU.is_gt, ALU.add, accum_out=gcount[:])
            v.memset(selm[:], 0.0)
            settle(v.tensor_scalar(eqm[:], LT[:], thr, None, ALU.is_equal))
            for h in range(2):
                x = v.tensor_tensor_scan(scan[:, h, :], eqm[:, h, :], selm[:, h, :], 0.0, ALU.add, ALU.add)
            settle(x)
            v.tensor_copy(tot[:], scan[:, :, P - 1]).then_inc(m_tot, 1)
            dve.wait_ge(m_base, 1)
            settle(v.tensor_copy(base[:, 0:1], bank[7][:, 0:1]))
            settle(v.tensor_scalar(lim[:], bank[7][:, 2:4], base[:, 0:1], None, ALU.add))
            settle(v.tensor_scalar(lim[:], lim[:], -1.0, float(CAP), ALU.mult, ALU.add))
            for h in range(2):
                x = v.scalar_tensor_tensor(out=junk[:, h, :], in0=scan[:, h, :], scalar=lim[:, h:h + 1], in1=eqm[:, h, :],
                                           op0=ALU.is_le, op1=ALU.mult)
            settle(x)
            settle(v.tensor_tensor(gtm[:], gtm[:], junk[:], ALU.add))
            for h in range(2):
                x = v.tensor_tensor_scan(scan[:, h, :], gtm[:, h, :], selm[:, h, :], 0.0, ALU.add, ALU.add)
            settle(x)
            v.tensor_copy(tot2[:], scan[:, :, P - 1]).then_inc(m_tot2, 1)
            dve.wait_ge(m_base2, 1)
            settle(v.tensor_copy(base[:, 2:4], bank[7][:, 2:4]))
            settle(v.tensor_tensor(cend[:], base[:, 2:4], scan[:, :, P - 1], ALU.add))
            for h in range(2):
                v.tensor_scalar(place[:, h, :], scan[:, h, :], base[:, 2 + h:3 + h], None, ALU.add)
                x = v.tensor_scalar(junk[:, h, :], W("iota"), base[:, 2 + h:3 + h], None, ALU.is_ge)
            settle(x)
            for h in range(2):
                x = v.scalar_tensor_tensor(out=oh[:, h, :], in0=W("iota"), scalar=cend[:, h:h + 1], in1=junk[:, h, :],
                                           op0=ALU.is_lt, op1=ALU.mult)
            settle(x)
            settle(v.tensor_copy(kvalb[:], W("kval")))
            for e in range(NE):
                v.tensor_scalar(ohe[:, e], oh[:], W("emask")[:, e:e + 1], None, ALU.mult).then_inc(m_oh, 1)
            for q in range(4):
                dve.wait_ge(m_pos, q + 1)
                x = v.tensor_scalar(le[:, 4 * q:4 * q + 4, :], bank[q][:].rearrange("p (e j) -> p e j", j=P), col("slot"), None, ALU.is_le)
            settle(x)
            settle(v.tensor_reduce(cntj[:], le, AX, ALU.add))
            v.scalar_tensor_tensor(out=idx[:], in0=bank[4][:, 0:NE], scalar=float(P), in1=cntj[:], op0=ALU.mult, op1=ALU.add).then_inc(m_idx, 1)

            for i in range(2):
                v.memset(yg[i][:, D:AROW], 0.0)

            def weigh(e):
                dve.wait_ge(e_y, e + 1)
                if e >= 2:
                    dve.wait_ge(e_add[e % 2], 16 * (e // 2))
                gate = xe[e % XRING][:, D + e:D + e + 1]
                v.tensor_copy(yg[e % 2][:, D:D + 1], gate)
                v.tensor_scalar(yg[e % 2][:, 0:D], bank[4 + e % 2][:, 0:D], gate, None, ALU.mult).then_inc(e_yg, 1)

            for e in range(NE + 1):
                if e < NE:
                    dve.wait_ge(e_xt, e + 1)
                    if e >= 2:
                        dve.wait_ge(e_h, e - 1)
                    v.tensor_copy(xeT[e % 2][:], bank[e % 2][:, 0:P]).then_inc(e_xtc, 1)
                if e >= 1:
                    weigh(e - 1)

            dve.wait_ge(s_acc, 32)
            settle(v.tensor_tensor(acc[0][:, :, 0:D + 1], acc[0][:, :, 0:D + 1], acc[1][:, :, 0:D + 1], ALU.add))
            settle(v.tensor_scalar(lsum[:], acc[0][:, :, D], 0.0, None, ALU.is_equal))
            settle(v.tensor_tensor(lsum[:], lsum[:], acc[0][:, :, D], ALU.add))
            settle(v.reciprocal(lrec[:], lsum[:]))
            for t in range(NT):
                x = v.scalar_tensor_tensor(out=acc[1][:, t, 0:D], in0=acc[0][:, t, 0:D], scalar=lrec[:, t:t + 1],
                                           in1=x3[:, t, :], op0=ALU.mult, op1=ALU.add)
            settle(x)
            for t in range(NT):
                x = v.bn_stats(fstats[:, t, :], acc[1][:, t, 0:D])
            settle(x)
            for t in range(NT):
                x = v.bn_aggr(fmv[:, t, :], fstats[:, t, :])
            x.then_inc(d_stats, 1)
            dve.wait_ge(d_rstd, 1)
            for t in range(NT):
                v.tensor_scalar(x0[:, t, :], acc[1][:, t, 0:D], fmv[:, t, 0:1], frstd[:, t:t + 1], ALU.subtract, ALU.mult).then_inc(d_norm, 1)

        @block.scalar
        def _(act):
            a = nc.scalar
            own = [0]

            def settle(ins):
                ins.then_inc(act_self, 1)
                own[0] += 1
                act.wait_ge(act_self, own[0])

            def attention(L):
                sems = lambda n: S[L.name, n]
                for s, m, g, steps in L.slots():
                    if m is not None:
                        act.wait_ge(sems("turned"), m + 1)
                        if m >= L.ring:
                            act.wait_ge(sems("pv"), (m - L.ring) // L.GU + 1)
                        a.activation(probsT[:, m % L.ring, :], turned_bank[m % 2][:], ACT.Exp, scale=float(L.DH) ** -0.5)\
                         .then_inc(sems("exped"), 1)
                    if g is not None:
                        b = g // L.NG
                        act.wait_ge(sems("pv"), g + 1)
                        if b >= 2:
                            act.wait_ge(sems("misc_read"), L.number["heads1" if L.causal else "heads0", b - 2] + 1)
                        a.copy(headsT[:, b % 2, g % L.NG, :], value_bank[g % 2][:, 0:T]).then_inc(sems("copied"), 1)
                    for kind, b in steps:
                        if kind == "split":
                            if L.causal:
                                act.wait_ge(sems("added"), b + 1)
                            else:
                                act.wait_ge(sems("misc_read"), L.number["q", b] + 1)
                            if b >= 2:
                                act.wait_ge(sems("written"), 16 * (b - 1))
                            a.copy(parts[:, b % 2, 0], qk_of(L, b)).then_inc(sems("kept"), 1)
                            act.wait_ge(sems("rest"), b + 1)
                            a.copy(parts[:, b % 2, 1], left[:, b % 2]).then_inc(sems("kept"), 1)

            attention(L0)
            act.wait_ge(s_late, 64)
            act.wait_ge(S["l0", "misc_read"], L0.nmisc)
            n = 0
            for cyc in range(3):
                for layer in range(4):
                    for c in range(NCHUNK):
                        act.wait_ge(f_z, n + 1)
                        o = bank[n % 4]
                        if layer == 0:
                            a.activation(hid1[:, c, :], o[:], ACT.Gelu, bias=col("cb1")).then_inc(f_act, 1)
                        elif layer == 1:
                            if cyc == 0 and c == 0:
                                act.wait_ge(f_pad, 1)
                            a.activation(hid2[0:64, c, :], o[0:64, :], ACT.Gelu, bias=col("cb2", 64)).then_inc(f_act, 1)
                        elif layer == 2:
                            a.activation(hid2[64:96, c, :], o[64:96, :], ACT.Gelu, bias=col("cb3")[64:96]).then_inc(f_act, 1)
                        else:
                            if cyc > 0:
                                act.wait_ge(f_x, NCHUNK * (cyc - 1) + c + 1)
                            a.activation(tanh[:, c, :], o[:], ACT.Tanh, bias=halfb[:, 0:1], scale=0.5).then_inc(f_act, 1)
                        n += 1
                if cyc == 0:
                    for i, (dst, m_, f, bname, sc) in enumerate((
                            (gh1, 64, ACT.Gelu, "gb1", 1.0 / T), (gh2, 32, ACT.Gelu, "gb2", 1.0), (gt, 128, ACT.Tanh, None, 0.5))):
                        act.wait_ge(f_r, i + 1)
                        a.activation(dst[0:m_, :], bank[0][0:m_, 0:NB], f, bias=halfb[:, 1:2] if bname is None else col(bname, m_),
                                     scale=sc).then_inc(f_gact, 1)
            for c in range(NCHUNK):
                act.wait_ge(f_tr, NCHUNK + c + 1)
                a.copy(x2T[:, c * CH:c * CH + CH], bank[4 + c][:]).then_inc(f_ev, 1)
            attention(L1)
            for c in range(4):
                act.wait_ge(m_tr, c + 1)
                a.copy(x2T[:, c * CH:c * CH + CH], bank[c][:]).then_inc(m_ev, 1)
            act.wait_ge(m_z, 1)
            a.activation(lz[:], lz[:], ACT.Exp).then_inc(m_exp, 1)
            for e in range(NE):
                act.wait_ge(e_h, e + 1)
                if e >= 2:
                    act.wait_ge(e_y, e - 1)
                for f in range(NF):
                    i = WEIGHTS["fb1"][0] + e * NF + f
                    x = a.activation(hidT[e % 2][:, f, :], bank[2 + e % 2][:, f * CAP:f * CAP + CAP], ACT.Gelu, bias=w[:, i:i + 1])
                x.then_inc(e_gelu, 1)

        @block.gpsimd
        def _(pool):
            gp = nc.gpsimd
            own = [0]

            def settle(ins):
                ins.then_inc(pool_self, 1)
                own[0] += 1
                pool.wait_ge(pool_self, own[0])

            def attention(L):
                sems = lambda n: S[L.name, n]
                for _, _, _, steps in L.slots():
                    for kind, b in steps:
                        if kind == "split":
                            if L.causal:
                                pool.wait_ge(sems("misc_read"), L.number["k", b] + 1)
                                gp.tensor_tensor(qk_of(L, b), rot[:, b % 2, :, 0, :], rot[:, b % 2, :, 1, :], ALU.add)\
                                  .then_inc(sems("added"), 1)
                            pool.wait_ge(sems("kept"), 2 * b + 1)
                            gp.tensor_tensor(left[:, b % 2], qk_of(L, b), parts[:, b % 2, 0], ALU.subtract).then_inc(sems("rest"), 1)
                            pool.wait_ge(sems("kept"), 2 * b + 2)
                            gp.tensor_tensor(parts[:, b % 2, 2], left[:, b % 2], parts[:, b % 2, 1], ALU.subtract).then_inc(sems("split"), 1)
                        if kind == "norm":
                            rsqrt(b, sems("stats"), sems("rstd"), 2)

            def rsqrt(b, ready, done, n):
                pool.wait_ge(ready, b + 1)
                settle(gp.tensor_scalar(vpe[:, b % 2, 0:n], mv[:, b % 2, 0:n, 1], EPS, None, ALU.add))
                gp.tensor_tensor(rstd[:, b % 2, 0:n], vpe[:, b % 2, 0:n], mhalf[:, 0:n], ALU.pow).then_inc(done, 1)

            settle(gp.memset(kst_all[ROWS:ROWS + 2].rearrange("p r i t -> p (r i t)").bitcast(F32), TWO_ONES))
            settle(gp.memset(ones_t[:], 1.0))
            settle(gp.memset(vst_all[:], 0.0))
            gp.memset(vst_all[:, :, :, :, L0.DH:L0.DH + 1], 1.0).then_inc(s_init_pool, 1)
            pool.wait_ge(s_init_dve, 1)
            attention(L0)
            pool.wait_ge(S["l0", "pv"], NB * L0.NG)
            pool.wait_ge(S["l0", "rstd"], NB)
            gp.memset(hid2[64:P], 0.0).then_inc(f_pad, 1)
            for c in range(NCHUNK):
                rsqrt(c, f_stats, f_rstd, 4)
            attention(L1)
            pool.wait_ge(m_ms, 1)
            settle(gp.tensor_scalar(rr[:], ms[:], 1.0 / D, EPS, ALU.mult, ALU.add))
            gp.tensor_tensor(rr[:], rr[:], mhalf[:], ALU.pow).then_inc(m_rr, 1)
            pool.wait_ge(m_idx, 1)
            pool.wait_ge(m_rows, 16)
            pool.wait_ge(s_zero, 16 * 16)

            def gather(e):
                gp.indirect_dma_start(out=xe[e % XRING][:], out_offset=None, in_=rows_dram,
                                      in_offset=bass.IndirectOffsetOnAxis(ap=idx[:, e:e + 1], axis=0)).then_inc(e_g[e % XRING], 16)

            for e in range(XRING):
                gather(e)
            for e in range(NE):
                pool.wait_ge(e_yg, e + 1)
                if e >= 2:
                    pool.wait_ge(e_add[e % 2], 16 * (e // 2))
                gp.indirect_dma_start(out=acc_dram[e % 2], out_offset=bass.IndirectOffsetOnAxis(ap=idx[:, e:e + 1], axis=0),
                                      in_=yg[e % 2][:], in_offset=None, compute_op=ALU.add).then_inc(e_add[e % 2], 16)
                if e + XRING < NE:
                    gather(e + XRING)
            pool.wait_ge(d_stats, 1)
            settle(gp.tensor_scalar(frstd[:], fmv[:, :, 1], EPS, None, ALU.add))
            gp.tensor_tensor(frstd[:], frstd[:], mhalf[:], ALU.pow).then_inc(d_rstd, 1)
    return nc


def kernel(**inputs):
    import concourse.bacc as _bacc
    from concourse.bass_utils import run_bass_kernel_spmd as _run
    import ml_dtypes

    x = {k: np.asarray(v) for k, v in inputs.items()}
    f32 = np.float32
    X = x["L0_attn_X"].reshape(NTOK, D)

    wt = np.zeros((P, NW), f32)

    def put(name, a):
        s = WEIGHTS[name][0]
        wt[:a.shape[0], s:s + a.shape[1]] = a

    rows0 = np.arange(D).reshape(2, 8, 8).transpose(0, 2, 1).reshape(-1)
    swap = rows0 ^ 1
    for n, a in (("q", x["L0_attn_W_q"]), ("k", x["L0_attn_W_k"])):
        put("w" + n, a[rows0].T)
        put(f"w{n}_swap", a[swap].T)
    put("wv", x["L0_attn_W_v"].T)
    put("wo", x["L0_attn_W_o"].T)
    dh = D // L0.H
    theta = (f32(10000.0) ** (f32(-2.0) * np.arange(dh // 2, dtype=f32) / f32(dh))).astype(f32)
    angles = np.arange(T, dtype=f32)[None, :] * theta[:, None]
    feat = rows0 % dh
    put("rope", np.concatenate([np.cos(angles)[feat // 2], np.sin(angles)[feat // 2] * np.where(feat % 2, 1, -1)[:, None]], 1).astype(f32))
    put("ident", np.eye(P, dtype=f32))
    put("cw1", x["L0_ffn_cn_w1"])
    put("cw2", x["L0_ffn_cn_w2"])
    put("cw3", x["L0_ffn_cn_w3"])
    cw4 = np.zeros((P, P), f32)
    cw4[64:96] = x["L0_ffn_cn_w4"]
    put("cw4", cw4)
    tw = np.zeros((D, D), f32)
    for blk, (src, sign) in enumerate(((2, 1), (3, -1), (0, -1), (1, 1))):
        for i in range(32):
            tw[src * 32 + i, blk * 32 + i] = sign
    put("twist", tw)
    put("gw1", x["L0_ffn_gc_w1"])
    put("gw2", x["L0_ffn_gc_w2"])
    put("gw3", np.broadcast_to(x["L0_ffn_gc_w3"], (D // 4, P)))
    H, DH, R = L1.H, L1.DH, 32
    lowrank = np.zeros((P, 3, 2, 2, D), f32)
    for i, n in enumerate("qkv"):
        U, V = x["L1_attn_U" + n], x["L1_attn_V" + n]
        for h in range(H):
            c, r0 = divmod(h * R, P)
            lowrank[r0:r0 + R, i, c, 0, h * DH:h * DH + DH] = V[h]
            if n == "v":
                lowrank[r0:r0 + R, i, c, 1, h * DH:h * DH + DH] = U[h].T
            else:
                lowrank[r0:r0 + R, i, c, 1, h::H] = U[h].T
    put("bv", np.broadcast_to(x["L1_attn_bv"].reshape(1, D), (P, D)))
    put("nw", np.broadcast_to(x["L1_ffn_norm_weight"][None], (P, D)))
    put("rb", np.broadcast_to(x["L1_ffn_router_bias"][None], (P, NE)))
    put("rw", x["L1_ffn_router_weight"].T)
    put("fb1", x["L1_ffn_fc1_bias"].reshape(NE, NF, P).transpose(2, 0, 1).reshape(P, -1))
    cols = np.zeros((P, 16), f32)
    for n, a in (("cb1", x["L0_ffn_cn_b1"]), ("cb2", x["L0_ffn_cn_b2"]), ("cb3", x["L0_ffn_cn_b3"]),
                 ("cb4", np.broadcast_to(x["L0_ffn_cn_b4"], (P,))), ("gb1", x["L0_ffn_gc_b1"]), ("gb2", x["L0_ffn_gc_b2"]),
                 ("gb3", np.broadcast_to(x["L0_ffn_gc_b3"], (P,))), ("range", np.broadcast_to(x["L0_ffn_adaptive_range"], (P,))),
                 ("bq", x["L1_attn_bq"].T.reshape(-1)), ("bk", x["L1_attn_bk"].T.reshape(-1)), ("slot", np.arange(P, dtype=f32))):
        cols[:a.shape[0], COLS[n]] = a
    cols[:, COLS["cb3"]] = 0
    cols[64:96, COLS["cb3"]] = x["L0_ffn_cn_b3"]
    put("cols", cols)
    put("iota", np.broadcast_to(np.arange(P, dtype=f32)[None], (P, P)))
    part = np.arange(P)
    put("emask", (part[:, None] % NE == np.arange(NE)[None]).astype(f32))
    put("kval", np.stack([part // NE, part // NE + 8], 1).astype(f32))
    bitnum = np.arange(NBITS - 1, -1, -1)
    put("bits", np.broadcast_to((2.0 ** bitnum)[None], (P, NBITS)).astype(f32))
    bits = np.ascontiguousarray(np.broadcast_to((1 << bitnum).astype(np.int32)[None], (P, NBITS)))

    q, k = part[:, None], part[None, :]
    maskq = np.tile(np.where(k > q, MASKED, 0.0), (1, 4))
    maskk = np.tile(np.where(q > k, MASKED, 0.0), (1, 4))
    same = (q % NE == k % NE)
    earlier = same & (q // NE < k // NE)
    cbt = np.concatenate([np.eye(P), maskq, maskk, same, earlier], 1).astype(ml_dtypes.bfloat16)

    ew = np.concatenate([x["L1_ffn_fc1_weight"].transpose(0, 2, 1),
                         x["L1_ffn_fc2_weight"].transpose(0, 2, 1).reshape(NE, NF, P, D).transpose(0, 2, 1, 3).reshape(NE, P, NF * D),
                         np.concatenate([x["L1_ffn_fc2_bias"][:, None], np.zeros((NE, P - 1, D), f32)], 1)], 2)
    arrays = {
        "in_xT": np.ascontiguousarray(X.T), "in_xtok": np.ascontiguousarray(X.reshape(NT, P, D).transpose(1, 0, 2)),
        "in_w": wt, "in_lowrank": lowrank.reshape(P, -1), "in_cb": cbt, "in_bits": bits,
        "in_ew": np.ascontiguousarray(ew),
    }
    nc = _bacc.Bacc("TRN2", target_bir_lowering=False, num_devices=1)
    args = [nc.dram_tensor(n, a.shape, mybir.dt.from_np(a.dtype), kind="ExternalInput").ap() for n, a in arrays.items()]
    out = nc.dram_tensor("out_0", (NTOK, D), F32, kind="ExternalOutput").ap()
    build_program(nc, *args, out)
    r = _run(nc, [arrays], core_ids=[0])
    return r.results[0]["out_0"].reshape(NB, T, D)
```

```python
from contextlib import ExitStack

import numpy as np

import concourse.bass as bass
from concourse import mybir

F32 = mybir.dt.float32
BF16 = mybir.dt.bfloat16
I32 = mybir.dt.int32
ALU = mybir.AluOpType
ACT = mybir.ActivationFunctionType
AX = mybir.AxisListType.X

P = 128
NB, T, D = 8, 256, 128
NTOK = NB * T
NT = NTOK // P
EPS = 1e-5
NE, F, CAP = 16, 512, 128
NF = F // P
GROW = D + NE
AROW = 132
ROWS = 96
MASKED = -1e30
RING = 4
TWO_ONES = float(np.array([0x3F803F80], np.uint32).view(np.float32)[0])
NPAIRS = 15
WRING = 4
NQ = 4
XRING = 8

K_PART = (0, 0, 0, 1, 1, 2)
Q_PART = (0, 1, 2, 0, 1, 0)


OWN_STEPS = ("norm", "rsqrt", "rms", "weigh", "split", "split2", "stack")
SPLIT, SPLIT2 = 5, 6



class Layer:

    def __init__(self, name, heads, causal):
        self.name, self.H, self.DH, self.causal = name, heads, D // heads, causal
        self.halves = ROWS // (6 * self.DH)
        self.PH = heads // self.halves
        self.GU = 3 if causal else 4
        self.NG = heads // 4
        self.U = self.GU * self.NG
        self.shift = self.U + (10 if causal else 9)
        self.lag = 4 if causal else 2
        self.ring = 8
        misc = {}
        def put(slot, *step):
            misc.setdefault(slot, []).append(step)
        for b in range(NB):
            front = -1 if b < 2 else (b - 2) * self.U
            put(front + (2 if b >= 2 else 0), "q", b)
            put(front + (4 if b >= 2 else 0), "k", b)
            put(front + (SPLIT if b >= 2 else 0), "split", b)
            put(front + (SPLIT2 if b >= 2 else 0), "split2", b)
            free = (b - RING + 1) * self.U + self.shift if b >= RING else -1
            put(max(free, front + (SPLIT2 if b >= 2 else 0)), "stack", b)
            put(max(free + 4, front + 7) if b >= RING else front + (7 if b >= 2 else 0), "v", b)
            put((b + 1) * self.U + 1, "max", b)
            tail = (b + 1) * self.U + self.shift + self.lag + (1 if causal else 0)
            put(tail, "heads0", b)
            put(tail + 1, "heads1", b)
            put(tail + 3, "proj_in", b)
            put(tail + 4, "add", b)
            put(tail + (5 if causal else 1), "rsqrt", b)
            put(tail + (6 if causal else 4), "norm", b)
            put(tail + (7 if causal else 5), "rms", b)
            put(tail + 7, "weigh", b)
            put(tail + (7 if causal else 8), "turn", b)
            put(tail + 9, "logit", b)
        absent = {"rms", "weigh", "logit"} if causal else {"k", "heads1", "proj_in", "add"}
        self.misc = {t: [s for s in steps if s[0] not in absent] for t, steps in misc.items()}
        self.first, self.last = -1, max(self.misc) + 1
        self.number, n = {}, 0
        for t in sorted(self.misc):
            for s in self.misc[t]:
                if s[0] not in OWN_STEPS:
                    self.number[s] = n
                    n += 1
        self.nmisc = n

    def slots(self):
        for t in range(self.first, self.last + 1):
            s = t if 0 <= t < NB * self.U else None
            m = t - self.shift
            m = m if 0 <= m < NB * self.U else None
            g = t - self.shift - self.lag
            g = g // self.GU - 1 if g >= self.GU and g % self.GU == 0 and g // self.GU <= NB * self.NG else None
            yield s, m, g, self.misc.get(t, [])


L0, L1 = Layer("l0", 16, True), Layer("l1", 8, False)

NCHUNK, CH = 4, 512
CYCLES = 3


def network_steps():
    steps = []
    for cyc in range(CYCLES):
        names = ["z1 0", "z1 1", "z1 2", "z1 3", "g 0", "z2 0", "twist 0", "z2 1", "twist 1", "z3 0", "g 1", "twist 2",
                 "z3 1", "g 2", "z4 0", "z4 1", "twist 3", "z4 2", "z4 3"]
        for name in names:
            kind, i = name.split()
            if kind != "g" or cyc == 0:
                steps.append((kind, cyc, int(i)))
    return steps


NETWORK = network_steps()
Z_NUMBER = {st: n for n, st in enumerate(st for st in NETWORK if st[0][0] == "z")}

WEIGHTS = {}


def lay_columns():
    at = 0
    for name, width in (
        ("wq", D), ("wq_swap", D), ("wk", D), ("wk_swap", D), ("wv", D), ("rope", 2 * T),
        ("ident", P), ("wo", D), ("cw1", D), ("cw2", D // 2), ("cw3", D // 2), ("cw4", 2 * P), ("twist", D),
        ("gw1", D // 2), ("gw2", D // 4), ("gw3", P), ("bv", D),
        ("nw", D), ("rb", NE), ("rw", NE), ("fb1", NE * NF), ("cols", 16), ("iota", P), ("emask", NE),
        ("kval", 2), ("bits", 1 + NPAIRS),
    ):
        WEIGHTS[name] = (at, at + width)
        at += width
    return at


NW = lay_columns()
NW_FIRST = WEIGHTS["wo"][1]
COLS = {n: i for i, n in enumerate(("cb1", "cb2", "cb3", "cb4", "gb1", "gb2", "gb3", "range", "bq", "bk", "slot"))}
NCB = 128 + 512 + 512 + 128 + 128


def build_program(nc, xT_in, xtok_in, w_in, lowrank_in, cb_in, bits_in, ew_in, out):
    ctx = ExitStack()
    with ctx:
        def sb(name, shape, dt=F32):
            return ctx.enter_context(nc.sbuf_tensor(name, shape, dt))

        def sem(name):
            return ctx.enter_context(nc.semaphore(name))

        bank = [ctx.enter_context(nc.psum_tensor(f"bank{i}", [P, 512], F32)) for i in range(8)]
        score_bank, turned_bank, value_bank, misc_bank = bank[0:2], bank[2:4], bank[4:6], bank[6:8]

        parts_dram = {L.name: nc.dram_tensor(f"parts_{L.name}", [NB, 3, 2, P, T], BF16, kind="Internal").ap() for L in (L0, L1)}
        maxes_dram = {L.name: nc.dram_tensor(f"maxes_{L.name}", [NB, 2, L.H, T], BF16, kind="Internal").ap() for L in (L0, L1)}
        rows_dram = nc.dram_tensor("rows", [NTOK, GROW], F32, kind="Internal").ap()
        acc_dram = [nc.dram_tensor(f"acc{i}", [NTOK, AROW], F32, kind="Internal").ap() for i in range(2)]

        w = sb("w", [P, NW])
        cb = sb("cb", [P, NCB], BF16)
        bits = sb("bits", [P, 1 + 3 * NPAIRS + 3], I32)
        xT0 = sb("xT0", [P, NTOK])
        x0 = sb("x0", [P, NT, D])
        x1 = sb("x1", [P, NT, D])
        x1T = sb("x1T", [P, NTOK])
        xf = xT0
        x2 = sb("x2", [P, NT, D])
        lowrank = x2[:].rearrange("p t c -> p (t c)")[:, 0:12 * D]
        x2T = x1T
        x3 = x1
        rot = sb("rot", [P, 2, 2, 2, T])
        qk = sb("qk", [P, 2, 2, T])
        ones_t = sb("ones_t", [1, P])
        fstats, fmv, frstd = sb("fstats", [P, NT, 6]), sb("fmv", [P, NT, 2]), sb("frstd", [P, NT])
        left = rot[:, :, :, 0]
        parts = sb("parts", [P, 2, 3, 2, T], BF16)
        kst_all = sb("kst", [P, RING, 8, T], BF16)
        kst = [kst_all[:, r] for r in range(RING)]
        qst_all = sb("qst", [P, RING, 2, 8, T], BF16)
        qst = [[qst_all[:, r, h] for h in range(2)] for r in range(RING)]
        shared = qst_all[:].rearrange("p r h i t -> p (r h i t)").bitcast(F32)
        vst_all = sb("vst", [P, RING, 2, L0.H, 32])
        vst = {"l0": [vst_all[:, r] for r in range(RING)],
               "l1": [vst_all[:, r, 0].rearrange("p (k h) c -> p k h c", k=2) for r in range(RING)]}
        negmax = sb("negmax", [P, RING, 2, 16])
        maxT = sb("maxT", [16, RING, 2, T], BF16)
        probsT = sb("probsT", [P, 8, 512])
        headsT = sb("headsT", [P, 2, 4, T])
        rsum = sb("rsum", [P, 2, 16])
        heads = sb("heads", [P, 2, 2, D])
        headsF = sb("headsF", [P, 2, T])
        res = sb("res", [P, 2, 2, D])
        stats = sb("stats", [P, 2, 4, 6])
        mv = sb("mv", [P, 2, 4, 2])
        vpe = sb("vpe", [P, 2, 4])
        rstd = sb("rstd", [P, 2, 4])
        mhalf = sb("mhalf", [P, 16])
        lr = sb("lr", [P, 3, D])

        def qk_of(L, b):
            return qk[:, b % 2]

        def W(name):
            a, b = WEIGHTS[name]
            return w[:, a:b]

        def col(name, rows=P):
            a = WEIGHTS["cols"][0] + COLS[name]
            return w[0:rows, a:a + 1]

        ident = W("ident")
        identb, maskq, maskk = cb[:, 0:128], cb[:, 128:640], cb[:, 640:1152]
        same_expert, earlier = cb[:, 1152:1280], cb[:, 1280:1408]

        s_first, s_late, s_init_pool, s_init_dve, s_zero = sem("s_first"), sem("s_late"), sem("s_init_pool"), sem("s_init_dve"), sem("s_zero")
        S = {}
        for L in (L0, L1):
            for n in ("misc_ready", "misc_read", "added", "kept", "rest", "split", "score", "maxed", "turned", "exped", "cut",
                      "pv", "copied", "stats", "rstd", "normed", "written", "maxwritten"):
                S[L.name, n] = sem(f"{n}_{L.name}")
            for r in range(RING):
                S[L.name, "stacked", r] = sem(f"stacked{r}_{L.name}")
                S[L.name, "maxrows", r] = sem(f"maxrows{r}_{L.name}")
        dve_self, act_self, pool_self = sem("dve_self"), sem("act_self"), sem("pool_self")
        f_z, f_act, f_T, f_x, f_gf, f_gact, f_coef, f_r, f_stats, f_rstd, f_norm, f_tr, f_ev = (sem("f_" + n) for n in (
            "z", "act", "T", "x", "gf", "gact", "coef", "r", "stats", "rstd", "norm", "tr", "ev"))
        c_w, c_ev, f_pad = sem("c_w"), sem("c_ev"), sem("f_pad")
        hid1, tanh, moved, hid2, hid3 = (shared[:, at * CH:(at + n) * CH].rearrange("p (c t) -> p c t", t=CH)
                                         for at, n in ((0, 4), (4, 4), (8, 4), (12, 2), (14, 2)))
        gsum = sb("gsum", [P, NB])
        gh1, gh2, gt = sb("gh1", [P, NB]), sb("gh2", [P, NB]), sb("gt", [P, NB])
        halfb = sb("halfb", [P, 2])
        coefA, coefB = sb("coefA", [P, NB]), sb("coefB", [P, 2])

        m_ms, m_rr, m_xn, m_z, m_exp, m_probs, m_rows, m_LT, m_cnt, m_tot, m_base, m_tot2, m_base2, m_oh, m_pos, m_idx = (
            sem("m_" + n) for n in ("ms", "rr", "xn", "z", "exp", "probs", "rows", "LT", "cnt",
                                    "tot", "base", "tot2", "base2", "oh", "pos", "idx"))
        m_count = sem("m_count")
        e_g = [sem(f"e_g{i}") for i in range(XRING)]
        e_w = [sem(f"e_w{i}") for i in range(WRING)]
        e_xt, e_xtc, e_h, e_gelu, e_y, e_yg = (sem("e_" + n) for n in ("xt", "xtc", "h", "gelu", "y", "yg"))
        e_add = [sem(f"e_add{i}") for i in range(2)]
        s_acc, d_sum = [sem(f"s_acc{q}") for q in range(NQ)], sem("d_sum")
        d_stats, d_rstd, d_norm, s_out = sem("d_stats"), sem("d_rstd"), sem("d_norm"), sem("s_out")
        xn, xnT = x0, x2T
        ms, rr = sb("ms", [P, NT]), sb("rr", [P, NT])
        junk = sb("junk", [P, 2, P])
        logit = sb("logit", [P, NT, NE])
        lmax, lsum, lrec = sb("lmax", [P, NT]), sb("lsum", [P, NT]), sb("lrec", [P, NT])
        lz = sb("lz", [P, NT, NE])
        LT = sb("LT", [P, 2, P])
        found, inc = sb("found", [P, 1], I32), sb("inc", [P, 1], I32)
        cand, hits, nhits = sb("cand", [P, 3], I32), sb("hits", [P, 3]), sb("nhits", [P, 1])
        cnt = sb("cnt", [P, 3], BF16)
        gcount = sb("gcount", [P, 1], BF16)
        gtm, eqm, scan, selm = (sb(n, [P, 2, P]) for n in ("gtm", "eqm", "scan", "selm"))
        tot, tot2 = sb("tot", [P, 2], BF16), sb("tot2", [P, 2], BF16)
        base, lim, cend = sb("base", [P, 4]), sb("lim", [P, 2]), sb("cend", [P, 2])
        place = sb("place", [P, 2, P], BF16)
        oh = sb("oh", [P, 2, P], BF16)
        kst_flat = kst_all[:].rearrange("p r i t -> p (r i t)")
        ohe = kst_flat[:, 0:NE * 2 * P].rearrange("p (e h s) -> p e h s", e=NE, h=2)
        kvalb = sb("kvalb", [P, 2], BF16)
        le = kst_flat[:, NE * 2 * P:NE * 3 * P].rearrange("p (e j) -> p e j", e=NE)
        cntj = sb("cntj", [P, NE])
        idx = sb("idx", [P, NE], I32)
        ew = [sb(f"ew{i}", [P, 2 * F + D]) for i in range(WRING)]
        xe_all = parts[:].rearrange("p b a s t -> p (b a s t)").bitcast(F32)
        xe = [xe_all[:, i * GROW:(i + 1) * GROW] for i in range(XRING)]
        xeT = [sb(f"xeT{i}", [P, P]) for i in range(2)]
        hidT = [headsT[:, i].rearrange("p f t -> p (f t)")[:, 0:NF * CAP].rearrange("p (f t) -> p f t", f=NF) for i in range(2)]
        yg = [sb(f"yg{i}", [P, AROW]) for i in range(2)]
        acc = [shared[:, i * NT * AROW:(i + 1) * NT * AROW].rearrange("p (t c) -> p t c", t=NT) for i in range(2)]
        zero = sb("zero", [P, NT * AROW // 8])

        block = ctx.enter_context(nc.Block())

        @block.sync
        def _(sp):
            sp.dma_start(w[:, 0:NW_FIRST], w_in[:, 0:NW_FIRST]).then_inc(s_first, 16)
            sp.dma_start(xT0[:], xT_in).then_inc(s_first, 16)
            sp.dma_start(cb[:], cb_in).then_inc(s_first, 16)

            def late_loads(t):
                if t == 1:
                    sp.dma_start(w[:, NW_FIRST:NW], w_in[:, NW_FIRST:NW]).then_inc(s_late, 16)
                    sp.dma_start(lowrank, lowrank_in).then_inc(s_late, 16)
                    sp.dma_start(x0[:], xtok_in).then_inc(s_late, 16)
                    sp.dma_start(bits[:], bits_in).then_inc(s_late, 16)
                if t == 2 * L0.U:
                    for a in range(2):
                        for i in range(8):
                            view = acc_dram[a].rearrange("(i p n) c -> i p (n c)", p=P, i=8)
                            sp.dma_start(view[i], zero[:]).then_inc(s_zero, 16)
                if t == 4 * L0.U:
                    for e in range(WRING):
                        sp.dma_start(ew[e][:], ew_in[e]).then_inc(e_w[e], 16)

            def unstacked(L, b):
                sp.wait_ge(S[L.name, "split"], b + 1)
                if b >= 1:
                    sp.wait_ge(S[L.name, "written"], 16 * b)
                sp.dma_start(parts_dram[L.name][b].rearrange("a s f t -> f (a s) t"),
                             parts[:, b % 2].rearrange("p a s t -> p (a s) t")).then_inc(S[L.name, "written"], 16)

            def stack(L, b):
                r = b % RING
                sp.wait_ge(S[L.name, "written"], 16 * (b + 1))
                if b >= RING:
                    sp.wait_ge(S[L.name, "turned"], L.U * (b - RING + 1))
                n = L.DH
                for h in range(L.halves):
                    for c, m in ((0, 3), (3, 2), (5, 1)):
                        at = (6 * h + c) * n
                        src = parts_dram[L.name][b, :, :, h * 64:h * 64 + n * 8, :].rearrange("a s (d p) t -> a s d (p t)", p=8)
                        k_src = src[K_PART[c], 1].unsqueeze(0).to_broadcast([m, n, 8 * T])
                        for t, x in ((kst[r], k_src), (qst[r][h], src[0:m, 0])):
                            sp.dma_start(t[at:at + m * n].rearrange("r p t -> r (p t)"), x)\
                              .then_inc(S[L.name, "stacked", r], 16)

            def max_rows(L, b):
                r = b % RING
                sp.wait_ge(S[L.name, "misc_read"], L.number["max", b] + 1)
                sp.dma_start(maxes_dram[L.name][b].rearrange("a h t -> h a t"), maxT[0:L.H, r])\
                  .then_inc(S[L.name, "maxwritten"], 16)
                sp.wait_ge(S[L.name, "maxwritten"], 16 * (b + 1))
                for h in range(L.halves):
                    sp.dma_start(qst[r][h][ROWS:ROWS + 2, :, :], maxes_dram[L.name][b, :, 8 * h:8 * h + 8, :])\
                      .then_inc(S[L.name, "maxrows", r], 16)

            sp.wait_ge(s_init_dve, 1)
            sp.wait_ge(s_init_pool, 1)
            for L in (L0, L1):
                for t, (_, _, _, steps) in enumerate(L.slots()):
                    if L is L0:
                        late_loads(t)
                    for kind, b in steps:
                        if kind == "split2":
                            unstacked(L, b)
                        if kind == "stack":
                            stack(L, b)
                        if kind == "max":
                            max_rows(L, b)
            rows_view = rows_dram.rearrange("(t p) c -> p t c", p=P)
            sp.wait_ge(m_xn, NB)
            sp.dma_start(rows_view[:, :, 0:D], xn[:]).then_inc(m_rows, 16)
            sp.wait_ge(m_probs, 1)
            sp.dma_start(rows_view[:, :, D:GROW], lz[:]).then_inc(m_rows, 16)
            for e in range(WRING, NE):
                sp.wait_ge(e_y, e - WRING + 1)
                sp.dma_start(ew[e % WRING][:], ew_in[e]).then_inc(e_w[e % WRING], 16)
            for a in range(2):
                sp.wait_ge(e_add[a], 16 * (NE // 2))
            for q in range(NQ):
                for a in range(2):
                    sp.dma_start(acc[a][:, 4 * q:4 * q + 4, :], acc_dram[a].rearrange("(t p) c -> p t c", p=P)[:, 4 * q:4 * q + 4, :])\
                      .then_inc(s_acc[q], 16)
            for q in range(NQ):
                sp.wait_ge(d_norm, q + 1)
                sp.dma_start(out.rearrange("(t p) c -> p t c", p=P)[:, 4 * q:4 * q + 4, :], x0[:, 4 * q:4 * q + 4, :]).then_inc(s_out, 16)
            sp.wait_ge(s_zero, 16 * 16)
            sp.wait_ge(s_out, 16 * NQ)

        @block.tensor
        def _(pe):
            mm = nc.tensor.matmul
            tr = nc.tensor.transpose

            def attention(L, xT, wq, wk, wv):
                U, sems = L.U, lambda n: S[L.name, n]

                def misc(step):
                    n = L.number[step]
                    if n >= 2:
                        pe.wait_ge(sems("misc_read"), n - 1)
                    return misc_bank[n % 2]

                def score_unit(n):
                    b, u = divmod(n, U)
                    g, k = divmod(u, L.GU)
                    r = b % RING
                    if u == 0:
                        pe.wait_ge(S[L.name, "stacked", r], 16 * 6 * L.halves * (b // RING + 1))
                    if n >= 2:
                        pe.wait_ge(sems("maxed"), n - 1)
                    o = score_bank[n % 2]
                    if not L.causal:
                        for qt in range(2):
                            x = mm(o[:, qt * T:qt * T + T], qst[r][0][0:ROWS, u, qt * P:qt * P + P],
                                   kst[r][0:ROWS, u, :], start=True, stop=True)
                    else:
                        hs = range(4 * g, 4 * g + 4) if k == 0 else range(4 * g + 2 * k - 2, 4 * g + 2 * k)
                        qt, nk = (0, P) if k == 0 else (1, T)
                        ov = o[:].rearrange("p (h k) -> p h k", k=nk)
                        mm(ov[:, :, nk - P:nk], identb, maskq[:, 0:len(hs) * P].rearrange("p (h k) -> p h k", k=P),
                           start=True, stop=False, skip_group_check=True)
                        for i, h in enumerate(hs):
                            x = mm(ov[:, i, :], qst[r][h // 8][0:ROWS, h % 8, qt * P:qt * P + P],
                                   kst[r][0:ROWS, h % 8, 0:nk], start=False, stop=True, skip_group_check=True)
                    x.then_inc(sems("score"), 1)

                def turned_unit(m):
                    b, u = divmod(m, U)
                    g, k = divmod(u, L.GU)
                    r = b % RING
                    if u == 0:
                        pe.wait_ge(S[L.name, "maxrows", r], 16 * L.halves * (b // RING + 1))
                    if m >= 2:
                        pe.wait_ge(sems("exped"), m - 1)
                    o = turned_bank[m % 2]
                    K = ROWS + 2
                    if not L.causal:
                        for kt in range(2):
                            x = mm(o[:, kt * T:kt * T + T], kst[r][0:K, u, kt * P:kt * P + P],
                                   qst[r][0][0:K, u, :], start=True, stop=True)
                    else:
                        hs = range(4 * g + 2 * k, 4 * g + 2 * k + 2) if k < 2 else range(4 * g, 4 * g + 4)
                        kt, nq = (0, T) if k < 2 else (1, P)
                        ov = o[:].rearrange("p (h q) -> p h q", q=nq)
                        for i, h in enumerate(hs):
                            x = mm(ov[:, i, :], kst[r][0:K, h % 8, kt * P:kt * P + P],
                                   qst[r][h // 8][0:K, h % 8, T - nq:T], start=True, stop=True)
                    x.then_inc(sems("turned"), 1)

                def value_group(G):
                    b, g = divmod(G, L.NG)
                    pe.wait_ge(sems("cut" if L.causal else "exped"), L.GU * (G + 1))
                    pe.wait_ge(sems("misc_read"), L.number["v", b] + 1)
                    if G >= 2:
                        pe.wait_ge(sems("copied"), G - 1)
                    elif L is L0:
                        pe.wait_ge(c_ev, 1)
                    o = value_bank[G % 2]
                    v = vst[L.name][b % RING]
                    for kt in range(2):
                        for j in range(4):
                            if L.causal:
                                unit = L.GU * G + (j // 2 if kt == 0 else 2)
                                pr = probsT[:, unit % L.ring, :]
                                pr, q0 = (pr[:, (j % 2) * T:(j % 2) * T + T], 0) if kt == 0 else (pr[:, j * P:j * P + P], P)
                            else:
                                pr, q0 = probsT[:, (L.GU * G + j) % L.ring, kt * T:kt * T + T], 0
                            x = mm(o[32 * j:32 * j + 32, q0:T], v[:, kt, 4 * g + j, :], pr,
                                   start=(kt == 0), stop=(kt == 1), skip_group_check=True)
                    x.then_inc(sems("pv"), 1)

                def step(kind, b):
                    if kind in OWN_STEPS:
                        return
                    o = misc((kind, b))
                    x = None
                    cols = slice(b * T, b * T + T)
                    if kind in ("q", "k"):
                        for i, ww in enumerate(wq if kind == "q" else wk):
                            x = mm(o[:, i * T:i * T + T], ww, xT[:, cols], start=True, stop=True)
                    elif kind == "v":
                        for i in range(2):
                            x = mm(o[:, i * P:i * P + P], xT[:, b * T + i * P:b * T + i * P + P], wv, start=True, stop=True)
                    elif kind == "max":
                        pe.wait_ge(sems("maxed"), U * (b + 1))
                        for i in range(2):
                            x = tr(o[0:L.H, i * P:i * P + P], negmax[:, b % RING, i, 0:L.H], ident)
                    elif kind in ("heads0", "heads1"):
                        pe.wait_ge(sems("copied"), L.NG * (b + 1))
                        for qt in ((0, 1) if not L.causal else (int(kind[-1]),)):
                            for g in range(L.NG):
                                at = g * P + (qt * T if not L.causal else 0)
                                x = tr(o[:, at:at + P], headsT[:, b % 2, g, qt * P:qt * P + P], ident)
                    elif kind == "proj_in":
                        pe.wait_ge(sems("misc_read"), L.number["heads1", b] + 1)
                        for i in range(2):
                            x = tr(o[:, i * P:i * P + P], heads[:, b % 2, i, :], ident)
                    elif kind == "add":
                        pe.wait_ge(sems("misc_read"), L.number["proj_in", b] + 1)
                        for i in range(2):
                            x = mm(o[:, i * P:i * P + P], headsF[:, b % 2, i * P:i * P + P], W("wo"), start=True, stop=True)
                    elif kind == "turn":
                        pe.wait_ge(sems("normed"), b + 1) if L is L0 else pe.wait_ge(m_xn, b + 1)
                        for i in range(2):
                            x = tr(o[:, i * P:i * P + P], (x1 if L is L0 else xn)[:, 2 * b + i, :], ident)
                    elif kind == "logit":
                        pe.wait_ge(sems("misc_read"), L.number["turn", b] + 1)
                        for i in range(2):
                            x = mm(o[:, i * NE:i * NE + NE], xnT[:, b * T + i * P:b * T + i * P + P], W("rw"), start=True, stop=True)
                    x.then_inc(sems("misc_ready"), 1)

                for s, m, g, steps in L.slots():
                    if L is L0 and s == L.U:
                        compose()
                    if m is not None:
                        turned_unit(m)
                    if s is not None:
                        score_unit(s)
                    if g is not None:
                        value_group(g)
                    for st in steps:
                        step(*st)

            def compose():
                pe.wait_ge(s_late, 64)
                for i in range(3):
                    for c in range(2):
                        at = (2 * i + c) * 2 * D
                        v_f, u_f = lowrank[:, at:at + D], lowrank[:, at + D:at + 2 * D]
                        x = mm(value_bank[0][:, i * D:i * D + D], v_f, u_f, start=(c == 0), stop=(c == 1))
                x.then_inc(c_w, 1)

            pe.wait_ge(s_first, 48)
            pe.wait_ge(s_init_pool, 1)
            pe.wait_ge(s_init_dve, 1)
            attention(L0, xT0, (W("wq"), W("wq_swap")), (W("wk"), W("wk_swap")), W("wv"))

            pe.wait_ge(S["l0", "misc_read"], L0.nmisc)
            pe.wait_ge(S["l0", "exped"], NB * L0.U)
            pe.wait_ge(S["l0", "maxed"], NB * L0.U)
            pe.wait_ge(S["l0", "copied"], NB * L0.NG)
            pe.wait_ge(f_pad, 1)
            for kind, cyc, i in NETWORK:
                x_now = x1T if cyc == 0 else xf
                if kind in ("z1", "twist") and cyc > 0:
                    pe.wait_ge(f_x, NCHUNK * (cyc - 1) + i + 1)
                if kind == "twist":
                    if cyc == 0 and i == 3:
                        pe.wait_ge(f_gact, 3)
                    mm(bank[4 + i][:], W("twist"), x_now[:, i * CH:i * CH + CH], start=True, stop=True).then_inc(f_T, 1)
                elif kind == "g":
                    name, src, rows_ = (("gw1", gsum, 64), ("gw2", gh1, 32), ("gw3", gh2, P))[i]
                    if i == 0:
                        pe.wait_ge(f_gf, NB)
                    else:
                        pe.wait_ge(f_gact, i)
                    mm(bank[7][0:rows_, 0:NB], W(name), src[:], start=True, stop=True).then_inc(f_r, 1)
                else:
                    n = Z_NUMBER[kind, cyc, i]
                    o = bank[n % 4]
                    if n >= 4:
                        pe.wait_ge(f_act, n - 3)
                    if kind == "z1":
                        x = mm(o[:], W("cw1"), x_now[:, i * CH:i * CH + CH], start=True, stop=True)
                    elif kind == "z2":
                        pe.wait_ge(f_act, Z_NUMBER["z1", cyc, 2 * i + 1] + 1)
                        for j in range(2):
                            x = mm(o[64 * j:64 * j + 64, :], W("cw2"), hid1[:, 2 * i + j, :], start=True, stop=True)
                    elif kind == "z3":
                        pe.wait_ge(f_act, Z_NUMBER["z2", cyc, i] + 1)
                        x = mm(o[0:64, :], W("cw3"), hid2[:, i, :], start=True, stop=True)
                    else:
                        pe.wait_ge(f_act, Z_NUMBER["z3", cyc, i // 2] + 1)
                        x = mm(o[:], W("cw4")[:, i % 2 * P:i % 2 * P + P], hid3[:, i // 2, :], start=True, stop=True)
                    x.then_inc(f_z, 1)
            for c in range(NCHUNK):
                pe.wait_ge(f_x, NCHUNK * (CYCLES - 1) + c + 1)
                for i in range(4):
                    x = tr(bank[4 + c][:, i * P:i * P + P], xf[:, c * CH + i * P:c * CH + i * P + P], ident)
                x.then_inc(f_tr, 1)
            pe.wait_ge(f_act, len(Z_NUMBER))
            for c in range(NCHUNK):
                pe.wait_ge(f_norm, c + 1)
                for i in range(4):
                    x = tr(bank[c][:, i * P:i * P + P], x2[:, 4 * c + i, :], ident)
                x.then_inc(f_tr, 1)

            pe.wait_ge(f_ev, 4)
            attention(L1, x2T, (lr[:, 0, :], lr[:, 1, :]), None, lr[:, 2, :])

            pe.wait_ge(S["l1", "misc_read"], L1.nmisc)
            pe.wait_ge(S["l1", "exped"], NB * L1.U)
            pe.wait_ge(S["l1", "maxed"], NB * L1.U)
            pe.wait_ge(S["l1", "copied"], NB * L1.NG)
            lf = logit[:].rearrange("p t e -> p (t e)")
            for i in range(2):
                x = tr(bank[5][:, i * P:i * P + P], lf[:, i * P:i * P + P], ident)
            x.then_inc(m_LT, 1)
            for i in range(2):
                pe.wait_ge(m_cnt, i + 1)
                mm(bank[6][:, 0:1], same_expert, cnt[:, 0:1], start=True, stop=True).then_inc(m_count, 1)
            with pe.Fori(0, NPAIRS) as i:
                pe.wait_ge(m_cnt, i + 3)
                mm(bank[6][:, 0:3], same_expert, cnt[:], start=True, stop=True).then_inc(m_count, 1)
            pe.wait_ge(m_tot, 1)
            mm(bank[7][:, 2:4], earlier, tot[:], start=True, stop=False, skip_group_check=True)
            mm(bank[7][:, 3:4], same_expert, tot[:, 0:1], start=False, stop=True, skip_group_check=True)
            mm(bank[7][:, 0:1], same_expert, gcount[:], start=True, stop=True, skip_group_check=True).then_inc(m_base, 1)
            pe.wait_ge(m_tot2, 1)
            mm(bank[7][:, 2:4], earlier, tot2[:], start=True, stop=False, skip_group_check=True)
            mm(bank[7][:, 3:4], same_expert, tot2[:, 0:1], start=False, stop=True, skip_group_check=True).then_inc(m_base2, 1)
            for e in range(NE):
                pe.wait_ge(m_oh, e + 1)
                for h in range(2):
                    mm(bank[e // 4][:, e % 4 * P:e % 4 * P + P], ohe[:, e, h, :], place[:, h, :], start=(h == 0), stop=(h == 1))
                for h in range(2):
                    x = mm(bank[4][:, e:e + 1], ohe[:, e, h, :], kvalb[:, h:h + 1], start=(h == 0), stop=(h == 1))
                if e % 4 == 3:
                    x.then_inc(m_pos, 1)
            pe.wait_ge(m_idx, 1)

            def turn_tokens(e):
                pe.wait_ge(e_g[e % XRING], 16 * (e // XRING + 1))
                if e >= 2:
                    pe.wait_ge(e_xtc, e - 1)
                tr(bank[e % 2][:, 0:P], xe[e % XRING][:, 0:D], ident).then_inc(e_xt, 1)

            def first_product(e):
                pe.wait_ge(e_w[e % WRING], 16 * (e // WRING + 1))
                pe.wait_ge(e_xtc, e + 1)
                if e >= 2:
                    pe.wait_ge(e_gelu, e - 1)
                o = bank[2 + e % 2]
                for f in range(NF):
                    x = mm(o[:, f * CAP:f * CAP + CAP], ew[e % WRING][:, f * P:f * P + P], xeT[e % 2][:], start=True, stop=True)
                x.then_inc(e_h, 1)

            def second_product(e):
                if e >= 2:
                    pe.wait_ge(e_yg, e - 1)
                o = bank[4 + e % 2]
                mm(o[:, 0:D], ones_t[0:1, :], ew[e % WRING][0:1, 2 * F:2 * F + D], start=True, stop=False)
                pe.wait_ge(e_gelu, e + 1)
                for f in range(NF):
                    x = mm(o[:, 0:D], hidT[e % 2][:, f, :], ew[e % WRING][:, F + f * D:F + f * D + D], start=False, stop=(f == NF - 1))
                x.then_inc(e_y, 1)

            turn_tokens(0)
            turn_tokens(1)
            first_product(0)
            for e in range(NE):
                if e + 1 < NE:
                    first_product(e + 1)
                if e + 2 < NE:
                    turn_tokens(e + 2)
                second_product(e)

        @block.vector
        def _(dve):
            v = nc.vector
            steps_done = [0]

            def settle(ins):
                ins.then_inc(dve_self, 1)
                steps_done[0] += 1
                dve.wait_ge(dve_self, steps_done[0])

            def attention(L):
                U, sems = L.U, lambda n: S[L.name, n]

                def own_max(n):
                    b, u = divmod(n, U)
                    g, k = divmod(u, L.GU)
                    dve.wait_ge(sems("score"), n + 1)
                    o = score_bank[n % 2][:]
                    nm = negmax[:, b % RING]
                    if not L.causal:
                        dst, src = nm[:, :, u], o.rearrange("p (h k) -> p h k", k=T)
                    elif k == 0:
                        dst, src = nm[:, 0, 4 * g:4 * g + 4], o.rearrange("p (h k) -> p h k", k=P)
                    else:
                        dst, src = nm[:, 1, 4 * g + 2 * k - 2:4 * g + 2 * k], o.rearrange("p (h k) -> p h k", k=T)
                    v.tensor_reduce(dst, src, AX, ALU.max, negate=True).then_inc(sems("maxed"), 1)

                def ready(step):
                    n = L.number[step]
                    dve.wait_ge(sems("misc_ready"), n + 1)
                    return misc_bank[n % 2]

                def read(ins):
                    ins.then_inc(sems("misc_read"), 1)

                def step(kind, b):
                    if kind == "norm":
                        dve.wait_ge(sems("rstd"), b + 1)
                        for i in range(2):
                            x = v.tensor_scalar((x1 if L is L0 else x3)[:, 2 * b + i, :], res[:, b % 2, i, :],
                                                mv[:, b % 2, i, 0:1], rstd[:, b % 2, i:i + 1], ALU.subtract, ALU.mult)
                        x.then_inc(sems("normed"), 1)
                        if L is L1:
                            dve.wait_ge(sems("normed"), b + 1)
                            for t in (2 * b, 2 * b + 1):
                                x = v.tensor_tensor_reduce(junk[:, t % 2, :], x3[:, t, :], x3[:, t, :], 1.0, 0.0, ALU.mult, ALU.add, ms[:, t:t + 1])
                            x.then_inc(m_ms, 1)
                        return
                    if kind == "weigh":
                        dve.wait_ge(m_rr, b + 1)
                        for t in (2 * b, 2 * b + 1):
                            x = v.scalar_tensor_tensor(out=xn[:, t, :], in0=x3[:, t, :], scalar=rr[:, t:t + 1], in1=W("nw"),
                                                       op0=ALU.mult, op1=ALU.mult)
                        x.then_inc(m_xn, 1)
                        return
                    if kind in OWN_STEPS:
                        return
                    o = ready((kind, b))
                    o2 = o[:].rearrange("p (i c) -> p i c", i=2)
                    if kind in ("q", "k"):
                        if L.causal:
                            if b >= 2:
                                dve.wait_ge(sems("split"), b - 1)
                            read(v.tensor_tensor(rot[:, b % 2, "qk".index(kind)], o2,
                                                 W("rope").rearrange("p (i c) -> p i c", i=2), ALU.mult))
                        else:
                            if b >= 1:
                                dve.wait_ge(sems("split"), b)
                            v.tensor_scalar(qk[:, b % 2, 0, :], o2[:, 0], col("bq"), None, ALU.add)
                            read(v.tensor_scalar(qk[:, b % 2, 1, :], o2[:, 1], col("bk"), None, ALU.add))
                    elif kind == "v":
                        if b >= RING:
                            dve.wait_ge(sems("pv"), L.NG * (b - RING + 1))
                        dst = vst[L.name][b % RING][:, :, :, 0:L.DH]
                        src = o[:, 0:T].rearrange("p (k h d) -> p k h d", k=2, h=L.H)
                        if L.causal:
                            read(v.tensor_copy(dst, src))
                        else:
                            bv = W("bv").rearrange("p (h d) -> p h d", h=L.H)
                            v.tensor_tensor(dst[:, 0], src[:, 0], bv, ALU.add)
                            read(v.tensor_tensor(dst[:, 1], src[:, 1], bv, ALU.add))
                    elif kind == "max":
                        if b >= RING:
                            dve.wait_ge(sems("maxwritten"), 16 * (b - RING + 1))
                        settle(v.tensor_copy(maxT[0:L.H, b % RING, 0, :], o[0:L.H, 0:T]))
                        read(v.tensor_tensor(maxT[0:L.H, b % RING, 1, :], o[0:L.H, 0:T], maxT[0:L.H, b % RING, 0, :], ALU.subtract))
                    elif kind in ("heads0", "heads1"):
                        for qt in ((0, 1) if not L.causal else (int(kind[-1]),)):
                            ov = (o[:] if L.causal else o2[:, qt]).rearrange("p (h c) -> p h c", c=32)
                            n = L.DH
                            rs = rsum[:, qt, 0:L.H]
                            settle(v.reciprocal(rs, ov[:, :, n]))
                            hv = heads[:, b % 2, qt, :].rearrange("p (h c) -> p h c", c=n)
                            x = v.tensor_tensor(hv, ov[:, :, 0:n], rs.unsqueeze(2).to_broadcast([P, L.H, n]), ALU.mult)
                            if L.causal or qt == 1:
                                read(x)
                        if not L.causal:
                            dve.wait_ge(sems("misc_read"), L.number[kind, b] + 1)
                            settle(v.tensor_tensor(res[:, b % 2], heads[:, b % 2], x2[:, 2 * b:2 * b + 2, :], ALU.add))
                            norm_stats(b)
                    elif kind == "proj_in":
                        read(v.tensor_copy(headsF[:, b % 2, :], o[:, 0:T]))
                    elif kind == "add":
                        read(v.tensor_tensor(res[:, b % 2], o[:, 0:T].rearrange("p (i c) -> p i c", i=2), x0[:, 2 * b:2 * b + 2, :], ALU.add))
                        dve.wait_ge(sems("misc_read"), L.number[kind, b] + 1)
                        norm_stats(b)
                    elif kind == "turn":
                        if L is L0:
                            v.tensor_reduce(gsum[:, b:b + 1], o[:, 0:T], AX, ALU.add).then_inc(f_gf, 1)
                        read(v.tensor_copy((x1T if L is L0 else xnT)[:, b * T:b * T + T], o[:, 0:T]))

                    elif kind == "logit":
                        read(v.tensor_tensor(logit[:, 2 * b:2 * b + 2, :], o[:, 0:2 * NE].rearrange("p (t e) -> p t e", e=NE),
                                             W("rb").unsqueeze(1).to_broadcast([P, 2, NE]), ALU.add))

                def norm_stats(b):
                    for i in range(2):
                        x = v.bn_stats(stats[:, b % 2, i, :], res[:, b % 2, i, :])
                    settle(x)
                    for i in range(2):
                        x = v.bn_aggr(mv[:, b % 2, i, :], stats[:, b % 2, i, :])
                    x.then_inc(sems("stats"), 1)

                for s, m, g, steps in L.slots():
                    if L is L0 and s == L.U:
                        dve.wait_ge(c_w, 1)
                        v.tensor_copy(lr[:].rearrange("p i c -> p (i c)"), value_bank[0][:, 0:3 * D]).then_inc(c_ev, 1)
                        dve.wait_ge(s_late, 64)
                        v.tensor_scalar(halfb[:, 0:1], col("cb4"), 0.5, None, ALU.mult)
                        v.tensor_scalar(halfb[:, 1:2], col("gb3"), 0.5, None, ALU.mult)
                        v.tensor_scalar(coefB[:, 0:1], col("range"), 0.3, None, ALU.mult)
                        v.tensor_scalar(coefB[:, 1:2], col("range"), 0.7, None, ALU.mult)
                    if s is not None:
                        own_max(s)
                    for st in steps:
                        step(*st)

            v.memset(qst_all[0:ROWS].rearrange("p r h i t -> p (r h i t)").bitcast(F32), 0.0)
            v.memset(zero[:], 0.0)
            v.memset(gh1[64:128], 0.0)
            v.memset(gh2[32:64], 0.0)
            v.memset(gh2[64:128], 0.0)
            v.memset(mhalf[:], -0.5).then_inc(s_init_dve, 1)
            dve.wait_ge(s_first, 48)
            dve.wait_ge(s_init_pool, 1)
            dve.wait_ge(s_init_dve, 1)
            attention(L0)

            dve.wait_ge(S["l0", "misc_read"], L0.nmisc)
            dve.wait_ge(f_gact, 3)
            v.tensor_scalar(coefA[:], gt[:], coefB[:, 1:2], 0.1, ALU.mult, ALU.add).then_inc(f_coef, 1)
            dve.wait_ge(f_coef, 1)
            for cyc in range(CYCLES):
                x_now = x1T if cyc == 0 else xf
                for c in range(NCHUNK):
                    dve.wait_ge(f_T, NCHUNK * cyc + c + 1)
                    for i in range(2):
                        half = slice(i * T, i * T + T)
                        x = v.scalar_tensor_tensor(out=moved[:, c, half], in0=bank[4 + c][:, half], scalar=coefA[:, 2 * c + i:2 * c + i + 1],
                                                   in1=x_now[:, c * CH + i * T:c * CH + i * T + T], op0=ALU.mult, op1=ALU.add)
                    if cyc == CYCLES - 1:
                        settle(x)
                        x = v.tensor_tensor(moved[:, c, :], moved[:, c, :], x1T[:, c * CH:c * CH + CH], ALU.add)
                settle(x)
                for c in range(NCHUNK):
                    sl = slice(c * CH, c * CH + CH)
                    dve.wait_ge(f_act, Z_NUMBER["z4", cyc, c] + 1)
                    settle(v.scalar_tensor_tensor(out=tanh[:, c, :], in0=tanh[:, c, :], scalar=coefB[:, 0:1], in1=bank[4 + c][:],
                                                  op0=ALU.mult, op1=ALU.mult))
                    v.tensor_tensor(xf[:, sl], moved[:, c, :], tanh[:, c, :], ALU.add).then_inc(f_x, 1)
            for c in range(NCHUNK):
                dve.wait_ge(f_tr, c + 1)
                if c >= 2:
                    dve.wait_ge(f_rstd, c - 1)
                for i in range(4):
                    x = v.bn_stats(stats[:, c % 2, i, :], bank[4 + c][:, i * P:i * P + P])
                settle(x)
                for i in range(4):
                    x = v.bn_aggr(mv[:, c % 2, i, :], stats[:, c % 2, i, :])
                x.then_inc(f_stats, 1)
                dve.wait_ge(f_rstd, c + 1)
                for i in range(4):
                    x = v.tensor_scalar(x2[:, 4 * c + i, :], bank[4 + c][:, i * P:i * P + P], mv[:, c % 2, i, 0:1],
                                        rstd[:, c % 2, i:i + 1], ALU.subtract, ALU.mult)
                x.then_inc(f_norm, 1)
            dve.wait_ge(f_norm, 4)
            for r in range(RING):
                x = v.memset(vst["l1"][r][:, :, :, L1.DH:L1.DH + 1], 1.0)
            settle(x)
            attention(L1)

            dve.wait_ge(S["l1", "misc_read"], L1.nmisc)
            settle(v.tensor_reduce(lmax[:], logit[:], AX, ALU.max))
            v.tensor_tensor(lz[:], logit[:], lmax[:].unsqueeze(2).to_broadcast([P, NT, NE]), ALU.subtract).then_inc(m_z, 1)
            dve.wait_ge(m_exp, 1)
            settle(v.tensor_reduce(lsum[:], lz[:], AX, ALU.add))
            settle(v.reciprocal(lrec[:], lsum[:]))
            v.tensor_tensor(lz[:], lz[:], lrec[:].unsqueeze(2).to_broadcast([P, NT, NE]), ALU.mult).then_inc(m_probs, 1)

            dve.wait_ge(m_LT, 1)
            settle(v.tensor_copy(LT[:].rearrange("p h j -> p (h j)"), bank[5][:, 0:2 * P]))
            v.tensor_scalar(junk[:], LT[:], 0.0, 0.0, ALU.is_ge, ALU.add, accum_out=cnt[:, 0:1]).then_inc(m_cnt, 1)
            dve.wait_ge(m_count, 1)
            settle(v.tensor_scalar(found[:], bank[6][:, 0:1], float(CAP), -1.0, ALU.is_lt, ALU.mult))
            settle(v.tensor_tensor(cand[:, 0:1], bits[:, 0:1], found[:], ALU.bitwise_xor))
            v.tensor_scalar(junk[:], LT[:], cand[:, 0:1].bitcast(F32), 0.0, ALU.is_ge, ALU.add, accum_out=cnt[:, 0:1]).then_inc(m_cnt, 1)
            dve.wait_ge(m_count, 2)
            settle(v.tensor_scalar(inc[:], bank[6][:, 0:1], float(CAP), W("bits")[:, 0:1], ALU.is_ge, ALU.mult))
            settle(v.scalar_tensor_tensor(out=cand[:], in0=bits[:, 1:4], scalar=inc[:], in1=found[:].to_broadcast([P, 3]),
                                          op0=ALU.bitwise_xor, op1=ALU.bitwise_xor))
            done = steps_done[0]
            with dve.Fori(0, NPAIRS) as i:
                for c, unused in enumerate((junk, gtm, eqm)):
                    x = v.tensor_scalar(unused[:], LT[:], cand[:, c:c + 1].bitcast(F32), 0.0, ALU.is_ge, ALU.add, accum_out=cnt[:, c:c + 1])
                x.then_inc(m_cnt, 1)
                v.tensor_tensor(found[:], found[:], inc[:], ALU.bitwise_xor).then_inc(dve_self, 1)
                dve.wait_ge(m_count, i + 3)
                v.tensor_scalar(hits[:], bank[6][:, 0:3], float(CAP), 0.0, ALU.is_ge, ALU.add, accum_out=nhits[:]).then_inc(dve_self, 1)
                dve.wait_ge(dve_self, i * 4 + (done + 2))
                v.tensor_scalar(inc[:], nhits[:], W("bits")[:, bass.ds(i + 1, 1)], None, ALU.mult).then_inc(dve_self, 1)
                dve.wait_ge(dve_self, i * 4 + (done + 3))
                v.scalar_tensor_tensor(out=cand[:], in0=bits[:, bass.ds(i * 3 + 4, 3)], scalar=inc[:], in1=found[:].to_broadcast([P, 3]),
                                       op0=ALU.bitwise_xor, op1=ALU.bitwise_xor).then_inc(dve_self, 1)
                dve.wait_ge(dve_self, i * 4 + (done + 4))
            steps_done[0] = done + 4 * NPAIRS
            settle(v.tensor_tensor(found[:], found[:], inc[:], ALU.bitwise_xor))
            thr = found[:].bitcast(F32)
            v.tensor_scalar(gtm[:], LT[:], thr, 0.0, ALU.is_gt, ALU.add, accum_out=gcount[:])
            v.memset(selm[:], 0.0)
            settle(v.tensor_scalar(eqm[:], LT[:], thr, None, ALU.is_equal))
            for h in range(2):
                x = v.tensor_tensor_scan(scan[:, h, :], eqm[:, h, :], selm[:, h, :], 0.0, ALU.add, ALU.add)
            settle(x)
            v.tensor_copy(tot[:], scan[:, :, P - 1]).then_inc(m_tot, 1)
            dve.wait_ge(m_base, 1)
            settle(v.tensor_copy(base[:, 0:1], bank[7][:, 0:1]))
            settle(v.tensor_scalar(lim[:], bank[7][:, 2:4], base[:, 0:1], None, ALU.add))
            settle(v.tensor_scalar(lim[:], lim[:], -1.0, float(CAP), ALU.mult, ALU.add))
            for h in range(2):
                x = v.scalar_tensor_tensor(out=junk[:, h, :], in0=scan[:, h, :], scalar=lim[:, h:h + 1], in1=eqm[:, h, :],
                                           op0=ALU.is_le, op1=ALU.mult)
            settle(x)
            settle(v.tensor_tensor(gtm[:], gtm[:], junk[:], ALU.add))
            for h in range(2):
                x = v.tensor_tensor_scan(scan[:, h, :], gtm[:, h, :], selm[:, h, :], 0.0, ALU.add, ALU.add)
            settle(x)
            v.tensor_copy(tot2[:], scan[:, :, P - 1]).then_inc(m_tot2, 1)
            dve.wait_ge(m_base2, 1)
            settle(v.tensor_copy(base[:, 2:4], bank[7][:, 2:4]))
            settle(v.tensor_tensor(cend[:], base[:, 2:4], scan[:, :, P - 1], ALU.add))
            for h in range(2):
                v.tensor_scalar(place[:, h, :], scan[:, h, :], base[:, 2 + h:3 + h], None, ALU.add)
                x = v.tensor_scalar(junk[:, h, :], W("iota"), base[:, 2 + h:3 + h], None, ALU.is_ge)
            settle(x)
            for h in range(2):
                x = v.scalar_tensor_tensor(out=oh[:, h, :], in0=W("iota"), scalar=cend[:, h:h + 1], in1=junk[:, h, :],
                                           op0=ALU.is_lt, op1=ALU.mult)
            settle(x)
            settle(v.tensor_copy(kvalb[:], W("kval")))
            for e in range(NE):
                v.tensor_scalar(ohe[:, e], oh[:], W("emask")[:, e:e + 1], None, ALU.mult).then_inc(m_oh, 1)
            for q in range(4):
                dve.wait_ge(m_pos, q + 1)
                x = v.tensor_scalar(le[:, 4 * q:4 * q + 4, :], bank[q][:].rearrange("p (e j) -> p e j", j=P), col("slot"), None, ALU.is_le)
            settle(x)
            settle(v.tensor_reduce(cntj[:], le, AX, ALU.add))
            v.scalar_tensor_tensor(out=idx[:], in0=bank[4][:, 0:NE], scalar=float(P), in1=cntj[:], op0=ALU.mult, op1=ALU.add).then_inc(m_idx, 1)

            for i in range(2):
                v.memset(yg[i][:, D:AROW], 0.0)

            def weigh(e):
                dve.wait_ge(e_y, e + 1)
                if e >= 2:
                    dve.wait_ge(e_add[e % 2], 16 * (e // 2))
                gate = xe[e % XRING][:, D + e:D + e + 1]
                v.tensor_copy(yg[e % 2][:, D:D + 1], gate)
                v.tensor_scalar(yg[e % 2][:, 0:D], bank[4 + e % 2][:, 0:D], gate, None, ALU.mult).then_inc(e_yg, 1)

            def keep_turned(e):
                dve.wait_ge(e_xt, e + 1)
                if e >= 2:
                    dve.wait_ge(e_h, e - 1)
                v.tensor_copy(xeT[e % 2][:], bank[e % 2][:, 0:P]).then_inc(e_xtc, 1)

            keep_turned(0)
            keep_turned(1)
            for e in range(NE):
                if e + 2 < NE:
                    keep_turned(e + 2)
                weigh(e)

            def mean_and_stats(q):
                dve.wait_ge(d_sum, q + 1)
                tiles = range(4 * q, 4 * q + 4)
                settle(v.reciprocal(lrec[:, 4 * q:4 * q + 4], lsum[:, 4 * q:4 * q + 4]))
                for t in tiles:
                    x = v.scalar_tensor_tensor(out=acc[1][:, t, 0:D], in0=acc[0][:, t, 0:D], scalar=lrec[:, t:t + 1],
                                               in1=x3[:, t, :], op0=ALU.mult, op1=ALU.add)
                settle(x)
                for t in tiles:
                    x = v.bn_stats(fstats[:, t, :], acc[1][:, t, 0:D])
                settle(x)
                for t in tiles:
                    x = v.bn_aggr(fmv[:, t, :], fstats[:, t, :])
                x.then_inc(d_stats, 1)

            def normalise(q):
                dve.wait_ge(d_rstd, q + 1)
                for t in range(4 * q, 4 * q + 4):
                    x = v.tensor_scalar(x0[:, t, :], acc[1][:, t, 0:D], fmv[:, t, 0:1], frstd[:, t:t + 1], ALU.subtract, ALU.mult)
                x.then_inc(d_norm, 1)

            for q in range(NQ):
                mean_and_stats(q)
                if q >= 1:
                    normalise(q - 1)
            normalise(NQ - 1)

        @block.scalar
        def _(act):
            a = nc.scalar
            own = [0]

            def settle(ins):
                ins.then_inc(act_self, 1)
                own[0] += 1
                act.wait_ge(act_self, own[0])

            def attention(L):
                sems = lambda n: S[L.name, n]
                for s, m, g, steps in L.slots():
                    if m is not None:
                        act.wait_ge(sems("turned"), m + 1)
                        if m >= L.ring:
                            act.wait_ge(sems("pv"), (m - L.ring) // L.GU + 1)
                        a.activation(probsT[:, m % L.ring, :], turned_bank[m % 2][:], ACT.Exp, scale=float(L.DH) ** -0.5)\
                         .then_inc(sems("exped"), 1)
                    if g is not None:
                        b = g // L.NG
                        act.wait_ge(sems("pv"), g + 1)
                        if b >= 2:
                            act.wait_ge(sems("misc_read"), L.number["heads1" if L.causal else "heads0", b - 2] + 1)
                        a.copy(headsT[:, b % 2, g % L.NG, :], value_bank[g % 2][:, 0:T]).then_inc(sems("copied"), 1)
                    for kind, b in steps:
                        if kind == "split":
                            if L.causal:
                                act.wait_ge(sems("added"), b + 1)
                            else:
                                act.wait_ge(sems("misc_read"), L.number["q", b] + 1)
                            if b >= 2:
                                act.wait_ge(sems("written"), 16 * (b - 1))
                            a.copy(parts[:, b % 2, 0], qk_of(L, b)).then_inc(sems("kept"), 1)
                        if kind == "split2":
                            act.wait_ge(sems("rest"), b + 1)
                            a.copy(parts[:, b % 2, 1], left[:, b % 2]).then_inc(sems("kept"), 1)

            attention(L0)
            act.wait_ge(s_late, 64)
            act.wait_ge(S["l0", "misc_read"], L0.nmisc)
            act.wait_ge(f_pad, 1)
            for kind, cyc, i in NETWORK:
                if kind == "g":
                    dst, rows_, func, bias, scale = ((gh1, 64, ACT.Gelu, col("gb1", 64), 1.0 / T), (gh2, 32, ACT.Gelu, col("gb2", 32), 1.0),
                                                     (gt, P, ACT.Tanh, halfb[:, 1:2], 0.5))[i]
                    act.wait_ge(f_r, i + 1)
                    a.activation(dst[0:rows_, :], bank[7][0:rows_, 0:NB], func, bias=bias, scale=scale).then_inc(f_gact, 1)
                elif kind != "twist":
                    n = Z_NUMBER[kind, cyc, i]
                    o = bank[n % 4]
                    act.wait_ge(f_z, n + 1)
                    if kind == "z1":
                        x = a.activation(hid1[:, i, :], o[:], ACT.Gelu, bias=col("cb1"))
                    elif kind == "z2":
                        x = a.activation(hid2[:, i, :], o[:], ACT.Gelu, bias=col("cb2"))
                    elif kind == "z3":
                        x = a.activation(hid3[0:64, i, :], o[0:64, :], ACT.Gelu, bias=col("cb3", 64))
                    else:
                        x = a.activation(tanh[:, i, :], o[:], ACT.Tanh, bias=halfb[:, 0:1], scale=0.5)
                    x.then_inc(f_act, 1)
            for c in range(NCHUNK):
                act.wait_ge(f_tr, NCHUNK + c + 1)
                a.copy(x2T[:, c * CH:c * CH + CH], bank[c][:]).then_inc(f_ev, 1)
            attention(L1)
            act.wait_ge(m_z, 1)
            a.activation(lz[:], lz[:], ACT.Exp).then_inc(m_exp, 1)
            for e in range(NE):
                act.wait_ge(e_h, e + 1)
                if e >= 2:
                    act.wait_ge(e_y, e - 1)
                for f in range(NF):
                    i = WEIGHTS["fb1"][0] + e * NF + f
                    x = a.activation(hidT[e % 2][:, f, :], bank[2 + e % 2][:, f * CAP:f * CAP + CAP], ACT.Gelu, bias=w[:, i:i + 1])
                x.then_inc(e_gelu, 1)

        @block.gpsimd
        def _(pool):
            gp = nc.gpsimd
            own = [0]

            def settle(ins):
                ins.then_inc(pool_self, 1)
                own[0] += 1
                pool.wait_ge(pool_self, own[0])

            def attention(L):
                sems = lambda n: S[L.name, n]
                for _, m, _, steps in L.slots():
                    if L.causal and m is not None:
                        k = m % L.GU
                        pool.wait_ge(sems("exped"), m + 1)
                        pr = probsT[:, m % L.ring, :].rearrange("p (h q) -> p h q", h=2 if k < 2 else 4)[:, :, 0:P]
                        gp.affine_select(out=pr, in_=pr, pattern=[[0, 2 if k < 2 else 4], [1, P]], compare_op=ALU.is_ge,
                                         fill=0.0, base=0, channel_multiplier=-1).then_inc(sems("cut"), 1)
                    for kind, b in steps:
                        if kind == "split":
                            if L.causal:
                                pool.wait_ge(sems("misc_read"), L.number["k", b] + 1)
                                gp.tensor_tensor(qk_of(L, b), rot[:, b % 2, :, 0, :], rot[:, b % 2, :, 1, :], ALU.add)\
                                  .then_inc(sems("added"), 1)
                            pool.wait_ge(sems("kept"), 2 * b + 1)
                            gp.tensor_tensor(left[:, b % 2], qk_of(L, b), parts[:, b % 2, 0], ALU.subtract).then_inc(sems("rest"), 1)
                        if kind == "split2":
                            pool.wait_ge(sems("kept"), 2 * b + 2)
                            gp.tensor_tensor(parts[:, b % 2, 2], left[:, b % 2], parts[:, b % 2, 1], ALU.subtract).then_inc(sems("split"), 1)
                        if kind == "rsqrt":
                            rsqrt(b, sems("stats"), sems("rstd"), 2)
                        if kind == "rms":
                            tiles = slice(2 * b, 2 * b + 2)
                            pool.wait_ge(m_ms, b + 1)
                            settle(gp.tensor_scalar(rr[:, tiles], ms[:, tiles], 1.0 / D, EPS, ALU.mult, ALU.add))
                            gp.tensor_tensor(rr[:, tiles], rr[:, tiles], mhalf[:, 0:2], ALU.pow).then_inc(m_rr, 1)

            def rsqrt(b, ready, done, n):
                pool.wait_ge(ready, b + 1)
                settle(gp.tensor_scalar(vpe[:, b % 2, 0:n], mv[:, b % 2, 0:n, 1], EPS, None, ALU.add))
                gp.tensor_tensor(rstd[:, b % 2, 0:n], vpe[:, b % 2, 0:n], mhalf[:, 0:n], ALU.pow).then_inc(done, 1)

            settle(gp.memset(kst_all[ROWS:ROWS + 2].rearrange("p r i t -> p (r i t)").bitcast(F32), TWO_ONES))
            settle(gp.memset(ones_t[:], 1.0))
            settle(gp.memset(vst_all[:], 0.0))
            gp.memset(vst_all[:, :, :, :, L0.DH:L0.DH + 1], 1.0).then_inc(s_init_pool, 1)
            pool.wait_ge(s_init_dve, 1)
            attention(L0)
            pool.wait_ge(S["l0", "pv"], NB * L0.NG)
            pool.wait_ge(S["l0", "rstd"], NB)
            gp.memset(hid3[64:P], 0.0).then_inc(f_pad, 1)
            for c in range(NCHUNK):
                rsqrt(c, f_stats, f_rstd, 4)
            attention(L1)
            pool.wait_ge(m_idx, 1)
            pool.wait_ge(m_rows, 32)
            pool.wait_ge(s_zero, 16 * 16)

            def gather(e):
                gp.indirect_dma_start(out=xe[e % XRING], out_offset=None, in_=rows_dram,
                                      in_offset=bass.IndirectOffsetOnAxis(ap=idx[:, e:e + 1], axis=0)).then_inc(e_g[e % XRING], 16)

            for e in range(XRING):
                gather(e)
            for e in range(NE):
                pool.wait_ge(e_yg, e + 1)
                if e >= 2:
                    pool.wait_ge(e_add[e % 2], 16 * (e // 2))
                gp.indirect_dma_start(out=acc_dram[e % 2], out_offset=bass.IndirectOffsetOnAxis(ap=idx[:, e:e + 1], axis=0),
                                      in_=yg[e % 2][:], in_offset=None, compute_op=ALU.add).then_inc(e_add[e % 2], 16)
                if e + XRING < NE:
                    gather(e + XRING)
            def add_up(q):
                tiles = slice(4 * q, 4 * q + 4)
                pool.wait_ge(s_acc[q], 32)
                settle(gp.tensor_tensor(acc[0][:, tiles, 0:D + 1], acc[0][:, tiles, 0:D + 1], acc[1][:, tiles, 0:D + 1], ALU.add))
                settle(gp.tensor_scalar(lsum[:, tiles], acc[0][:, tiles, D], 0.0, None, ALU.is_equal))
                gp.tensor_tensor(lsum[:, tiles], lsum[:, tiles], acc[0][:, tiles, D], ALU.add).then_inc(d_sum, 1)
                pool.wait_ge(d_sum, q + 1)

            def last_rsqrt(q):
                tiles = slice(4 * q, 4 * q + 4)
                pool.wait_ge(d_stats, q + 1)
                settle(gp.tensor_scalar(frstd[:, tiles], fmv[:, tiles, 1], EPS, None, ALU.add))
                gp.tensor_tensor(frstd[:, tiles], frstd[:, tiles], mhalf[:, 0:4], ALU.pow).then_inc(d_rstd, 1)
                pool.wait_ge(d_rstd, q + 1)

            for q in range(NQ):
                add_up(q)
                if q >= 1:
                    last_rsqrt(q - 1)
            last_rsqrt(NQ - 1)
    return nc


def kernel(**inputs):
    import concourse.bacc as _bacc
    from concourse.bass_utils import run_bass_kernel_spmd as _run
    import ml_dtypes

    x = {k: np.asarray(v) for k, v in inputs.items()}
    f32 = np.float32
    X = x["L0_attn_X"].reshape(NTOK, D)

    wt = np.zeros((P, NW), f32)

    def put(name, a):
        s = WEIGHTS[name][0]
        wt[:a.shape[0], s:s + a.shape[1]] = a

    rows0 = np.arange(D).reshape(2, 8, 8).transpose(0, 2, 1).reshape(-1)
    swap = rows0 ^ 1
    for n, a in (("q", x["L0_attn_W_q"]), ("k", x["L0_attn_W_k"])):
        put("w" + n, a[rows0].T)
        put(f"w{n}_swap", a[swap].T)
    put("wv", x["L0_attn_W_v"].T)
    put("wo", x["L0_attn_W_o"].T)
    dh = D // L0.H
    theta = (f32(10000.0) ** (f32(-2.0) * np.arange(dh // 2, dtype=f32) / f32(dh))).astype(f32)
    angles = np.arange(T, dtype=f32)[None, :] * theta[:, None]
    feat = rows0 % dh
    put("rope", np.concatenate([np.cos(angles)[feat // 2], np.sin(angles)[feat // 2] * np.where(feat % 2, 1, -1)[:, None]], 1).astype(f32))
    put("ident", np.eye(P, dtype=f32))
    put("cw1", x["L0_ffn_cn_w1"])
    put("cw2", x["L0_ffn_cn_w2"])
    cw3, cw4 = np.zeros((P, D // 2), f32), np.zeros((P, 2 * P), f32)
    for j in range(2):
        cw3[64 * j:64 * j + 64, 32 * j:32 * j + 32] = x["L0_ffn_cn_w3"]
        cw4[32 * j:32 * j + 32, P * j:P * j + P] = x["L0_ffn_cn_w4"]
    put("cw3", cw3)
    put("cw4", cw4)
    tw = np.zeros((D, D), f32)
    for blk, (src, sign) in enumerate(((2, 1), (3, -1), (0, -1), (1, 1))):
        for i in range(32):
            tw[src * 32 + i, blk * 32 + i] = sign
    put("twist", tw)
    put("gw1", x["L0_ffn_gc_w1"])
    put("gw2", x["L0_ffn_gc_w2"])
    put("gw3", np.broadcast_to(x["L0_ffn_gc_w3"], (D // 4, P)))
    H, DH, R = L1.H, L1.DH, 32
    lowrank = np.zeros((P, 3, 2, 2, D), f32)
    for i, n in enumerate("qkv"):
        U, V = x["L1_attn_U" + n], x["L1_attn_V" + n]
        for h in range(H):
            c, r0 = divmod(h * R, P)
            lowrank[r0:r0 + R, i, c, 0, h * DH:h * DH + DH] = V[h]
            if n == "v":
                lowrank[r0:r0 + R, i, c, 1, h * DH:h * DH + DH] = U[h].T
            else:
                lowrank[r0:r0 + R, i, c, 1, h::H] = U[h].T
    put("bv", np.broadcast_to(x["L1_attn_bv"].reshape(1, D), (P, D)))
    put("nw", np.broadcast_to(x["L1_ffn_norm_weight"][None], (P, D)))
    put("rb", np.broadcast_to(x["L1_ffn_router_bias"][None], (P, NE)))
    put("rw", x["L1_ffn_router_weight"].T)
    put("fb1", x["L1_ffn_fc1_bias"].reshape(NE, NF, P).transpose(2, 0, 1).reshape(P, -1))
    cols = np.zeros((P, 16), f32)
    for n, a in (("cb1", x["L0_ffn_cn_b1"]), ("cb2", np.tile(x["L0_ffn_cn_b2"], 2)), ("cb3", np.tile(x["L0_ffn_cn_b3"], 2)),
                 ("cb4", np.broadcast_to(x["L0_ffn_cn_b4"], (P,))), ("gb1", x["L0_ffn_gc_b1"]), ("gb2", x["L0_ffn_gc_b2"]),
                 ("gb3", np.broadcast_to(x["L0_ffn_gc_b3"], (P,))), ("range", np.broadcast_to(x["L0_ffn_adaptive_range"], (P,))),
                 ("bq", x["L1_attn_bq"].T.reshape(-1)), ("bk", x["L1_attn_bk"].T.reshape(-1)), ("slot", np.arange(P, dtype=f32))):
        cols[:a.shape[0], COLS[n]] = a
    put("cols", cols)
    put("iota", np.broadcast_to(np.arange(P, dtype=f32)[None], (P, P)))
    part = np.arange(P)
    put("emask", (part[:, None] % NE == np.arange(NE)[None]).astype(f32))
    put("kval", np.stack([part // NE, part // NE + 8], 1).astype(f32))
    low = np.arange(2 * NPAIRS - 2, -1, -2)
    put("bits", np.broadcast_to(np.concatenate([[2.0 ** (2 * NPAIRS)], 2.0 ** low])[None], (P, 1 + NPAIRS)).astype(f32))
    bits = np.concatenate([[1 << (2 * NPAIRS)], ((1 << low)[:, None] * np.arange(1, 4)[None]).reshape(-1), [0, 0, 0]]).astype(np.int32)
    bits = np.ascontiguousarray(np.broadcast_to(bits[None], (P, bits.size)))

    q, k = part[:, None], part[None, :]
    maskq = np.tile(np.where(k > q, MASKED, 0.0), (1, 4))
    maskk = np.tile(np.where(q > k, MASKED, 0.0), (1, 4))
    same = (q % NE == k % NE)
    earlier = same & (q // NE < k // NE)
    cbt = np.concatenate([np.eye(P), maskq, maskk, same, earlier], 1).astype(ml_dtypes.bfloat16)

    ew = np.concatenate([x["L1_ffn_fc1_weight"].transpose(0, 2, 1),
                         x["L1_ffn_fc2_weight"].transpose(0, 2, 1).reshape(NE, NF, P, D).transpose(0, 2, 1, 3).reshape(NE, P, NF * D),
                         np.concatenate([x["L1_ffn_fc2_bias"][:, None], np.zeros((NE, P - 1, D), f32)], 1)], 2)
    arrays = {
        "in_xT": np.ascontiguousarray(X.T), "in_xtok": np.ascontiguousarray(X.reshape(NT, P, D).transpose(1, 0, 2)),
        "in_w": wt, "in_lowrank": lowrank.reshape(P, -1), "in_cb": cbt, "in_bits": bits,
        "in_ew": np.ascontiguousarray(ew),
    }
    nc = _bacc.Bacc("TRN2", target_bir_lowering=False, num_devices=1)
    args = [nc.dram_tensor(n, a.shape, mybir.dt.from_np(a.dtype), kind="ExternalInput").ap() for n, a in arrays.items()]
    out = nc.dram_tensor("out_0", (NTOK, D), F32, kind="ExternalOutput").ap()
    build_program(nc, *args, out)
    r = _run(nc, [arrays], core_ids=[0])
    return r.results[0]["out_0"].reshape(NB, T, D)
```

```python
from contextlib import ExitStack

import numpy as np

import concourse.bass as bass
from concourse import mybir

F32 = mybir.dt.float32
BF16 = mybir.dt.bfloat16
I32 = mybir.dt.int32
ALU = mybir.AluOpType
ACT = mybir.ActivationFunctionType
AX = mybir.AxisListType.X

P = 128
NB, T, D = 8, 256, 128
NTOK = NB * T
NT = NTOK // P
EPS = 1e-5
NE, F, CAP = 16, 512, 128
NF = F // P
GROW = D + NE
AROW = 132
ROWS = 96
MASKED = -1e30
RING = 4
TWO_ONES = float(np.array([0x3F803F80], np.uint32).view(np.float32)[0])
NPAIRS = 15
WRING = 4
NQ = 4
XRING = 8

K_PART = (0, 0, 0, 1, 1, 2)

OWN_STEPS = ("norm", "rsqrt", "rms", "weigh", "split", "split2", "stack")
SLOTS = {
    "l0": dict(shift=13, lag=4, q=2, k=4, split=5, split2=7, v=7, v_free=4, max=2, heads0=2, heads1=2, proj_in=3,
               add=5, rsqrt=5, norm=7, turn=10),
    "l1": dict(shift=9, lag=2, q=1, split=5, split2=6, v=8, v_free=5, max=1, heads0=0, rsqrt=2, norm=3, rms=4,
               weigh=7, turn=8, logit=10),
}


class Layer:

    def __init__(self, name, heads, causal):
        self.name, self.H, self.DH, self.causal = name, heads, D // heads, causal
        self.halves = ROWS // (6 * self.DH)
        self.GU = 3 if causal else 4
        self.NG = heads // 4
        self.U = self.GU * self.NG
        at = SLOTS[name]
        self.shift = self.U + at["shift"]
        self.lag = at["lag"]
        self.ring = 8
        misc = {}
        def put(slot, *step):
            misc.setdefault(slot, []).append(step)
        for b in range(NB):
            front = (b - 2) * self.U
            free = (b - RING + 1) * self.U + self.shift if b >= RING else -1
            for step in ("q", "k", "split", "split2"):
                if step in at:
                    put(front + at[step] if b >= 2 else -1, step, b)
            put(max(free, front + at["split2"]) if b >= 2 else -1, "stack", b)
            put(max(free + at["v_free"], front + at["v"]) if b >= 2 else -1, "v", b)
            put((b + 1) * self.U + at["max"], "max", b)
            tail = (b + 1) * self.U + self.shift + self.lag
            for step in ("heads0", "heads1", "proj_in", "add", "rsqrt", "norm", "rms", "weigh", "turn", "logit"):
                if step in at:
                    put(tail + at[step], step, b)
        self.misc = misc
        self.first, self.last = -1, max(self.misc) + 1
        self.number, n = {}, 0
        for t in sorted(self.misc):
            for s in self.misc[t]:
                if s[0] not in OWN_STEPS:
                    self.number[s] = n
                    n += 1
        self.nmisc = n

    def early(self, t):
        at = NB * self.U + self.shift + self.lag + SLOTS["l0"]["heads1"] + 1
        return [st for st, n in zip(NETWORK, EARLY_SLOTS) if self.causal and t == at + n]

    def slots(self):
        for t in range(self.first, self.last + 1):
            s = t if 0 <= t < NB * self.U else None
            m = t - self.shift
            m = m if 0 <= m < NB * self.U else None
            g = t - self.shift - self.lag
            g = g // self.GU - 1 if g >= self.GU and g % self.GU == 0 and g // self.GU <= NB * self.NG else None
            yield t, s, m, g, self.misc.get(t, [])


L0, L1 = Layer("l0", 16, True), Layer("l1", 8, False)

NCHUNK, CH = 4, 512
CYCLES = 3


def network_steps():
    steps = []
    for cyc in range(CYCLES):
        names = ["z1 0", "z1 1", "z1 2", "twist 0", "z2 0", "twist 1", "z1 3", "g 0", "twist 2", "z2 1", "z3 0", "g 1",
                 "z3 1", "g 2", "z4 0", "z4 1", "twist 3", "z4 2", "z4 3"]
        if cyc > 0:
            names = ["z1 0", "twist 0", "z1 1", "twist 1", "z1 2", "z2 0", "z1 3", "twist 2", "z2 1", "z3 0", "twist 3",
                     "z3 1", "z4 0", "z4 1", "z4 2", "z4 3"]
        for name in names:
            kind, i = name.split()
            if kind != "g" or cyc == 0:
                steps.append((kind, cyc, int(i)))
    return steps


NETWORK = network_steps()
EARLY_SLOTS = (0, 0, 2, 4, 5, 6)
EARLY = len(EARLY_SLOTS)
Z_NUMBER = {st: n for n, st in enumerate(st for st in NETWORK if st[0][0] == "z")}

WEIGHTS = {}


def lay_columns():
    at = 0
    for name, width in (
        ("wq", D), ("wq_swap", D), ("wk", D), ("wk_swap", D), ("wv", D), ("rope", 2 * T),
        ("ident", P), ("wo", D), ("cw1", D), ("cw2", D // 2), ("cw3", D // 2), ("cw4", 2 * P), ("twist", D),
        ("gw1", D // 2), ("gw2", D // 4), ("gw3", P), ("bv", D),
        ("nw", D), ("rb", NE), ("rw", NE), ("fb1", NE * NF), ("cols", 16), ("iota", P), ("emask", NE),
        ("kval", 2), ("bits", 1 + NPAIRS),
    ):
        WEIGHTS[name] = (at, at + width)
        at += width
    return at


NW = lay_columns()
NW_FIRST = WEIGHTS["wo"][1]
COLS = {n: i for i, n in enumerate(("cb1", "cb2", "cb3", "cb4", "gb1", "gb2", "gb3", "range", "bq", "bk", "slot"))}
NCB = 128 + 512 + 512 + 128 + 128


def build_program(nc, xT_in, xtok_in, w_in, lowrank_in, cb_in, bits_in, ew_in, out):
    ctx = ExitStack()
    with ctx:
        def sb(name, shape, dt=F32):
            return ctx.enter_context(nc.sbuf_tensor(name, shape, dt))

        def sem(name):
            return ctx.enter_context(nc.semaphore(name))

        bank = [ctx.enter_context(nc.psum_tensor(f"bank{i}", [P, 512], F32)) for i in range(8)]
        score_bank, turned_bank = bank[0:2], bank[2:4]
        value_banks, misc_banks = {"l0": bank[4:6], "l1": bank[6:8]}, {"l0": bank[6:8], "l1": bank[4:6]}

        parts_dram = {L.name: nc.dram_tensor(f"parts_{L.name}", [NB, 3, 2, P, T], BF16, kind="Internal").ap() for L in (L0, L1)}
        maxes_dram = {L.name: nc.dram_tensor(f"maxes_{L.name}", [NB, 2, L.H, T], BF16, kind="Internal").ap() for L in (L0, L1)}
        rows_dram = nc.dram_tensor("rows", [NTOK, GROW], F32, kind="Internal").ap()
        acc_dram = [nc.dram_tensor(f"acc{i}", [NTOK, AROW], F32, kind="Internal").ap() for i in range(2)]

        w = sb("w", [P, NW])
        cb = sb("cb", [P, NCB], BF16)
        bits = sb("bits", [P, 1 + 3 * NPAIRS + 3], I32)
        xT0 = sb("xT0", [P, NTOK])
        x0 = sb("x0", [P, NT, D])
        x1 = sb("x1", [P, NT, D])
        x1T = sb("x1T", [P, NTOK])
        xf = xT0
        x2 = sb("x2", [P, NT, D])
        lowrank = x2[:].rearrange("p t c -> p (t c)")[:, 0:12 * D]
        x2T = x1T
        x3 = x1
        rot = sb("rot", [P, 2, 2, 2, T])
        qk = sb("qk", [P, 2, 2, T])
        ones_t = sb("ones_t", [1, P])
        fstats, fmv, frstd = sb("fstats", [P, NT, 6]), sb("fmv", [P, NT, 2]), sb("frstd", [P, NT])
        left = rot[:, :, :, 0]
        parts = sb("parts", [P, 2, 3, 2, T], BF16)
        kst_all = sb("kst", [P, RING, 8, T], BF16)
        kst = [kst_all[:, r] for r in range(RING)]
        qst_all = sb("qst", [P, RING, 2, 8, T], BF16)
        qst = [[qst_all[:, r, h] for h in range(2)] for r in range(RING)]
        shared = qst_all[:].rearrange("p r h i t -> p (r h i t)").bitcast(F32)
        vst_all = sb("vst", [P, RING, 2, L0.H, 32])
        vst = {"l0": [vst_all[:, r] for r in range(RING)],
               "l1": [vst_all[:, r, 0].rearrange("p (k h) c -> p k h c", k=2) for r in range(RING)]}
        negmax = sb("negmax", [P, RING, 2, 16])
        maxT = sb("maxT", [16, RING, 2, T], BF16)
        probsT = sb("probsT", [P, 8, 512])
        headsT = sb("headsT", [P, 2, 4, T])
        rsum = sb("rsum", [P, 2, 16])
        heads = sb("heads", [P, 2, 2, D])
        headsF = sb("headsF", [P, 2, T])
        res = sb("res", [P, 2, 2, D])
        stats = sb("stats", [P, 2, 4, 6])
        mv = sb("mv", [P, 2, 4, 2])
        vpe = sb("vpe", [P, 2, 4])
        rstd = sb("rstd", [P, 2, 4])
        mhalf = sb("mhalf", [P, 16])
        lr = sb("lr", [P, 3, D])

        def qk_of(b):
            return qk[:, b % 2]

        def W(name):
            a, b = WEIGHTS[name]
            return w[:, a:b]

        def col(name, rows=P):
            a = WEIGHTS["cols"][0] + COLS[name]
            return w[0:rows, a:a + 1]

        ident = W("ident")
        at_bias = WEIGHTS["cols"][0] + COLS["bq"]
        qk_bias = w[:, at_bias:at_bias + 2]
        identb, maskq, maskk = cb[:, 0:128], cb[:, 128:640], cb[:, 640:1152]
        same_expert, earlier = cb[:, 1152:1280], cb[:, 1280:1408]

        s_first, s_late, s_cb, s_x, s_init_late, s_ones, s_init_pool, s_init_dve, s_zero = sem("s_first"), sem("s_late"), sem("s_cb"), sem("s_x"), sem("s_init_late"), sem("s_ones"), sem("s_init_pool"), sem("s_init_dve"), sem("s_zero")
        S = {}
        for L in (L0, L1):
            for n in ("misc_ready", "misc_read", "added", "kept", "rest", "split", "score", "maxed", "turned", "exped", "cut",
                      "pv", "copied", "stats", "rstd", "normed", "written", "maxwritten"):
                S[L.name, n] = sem(f"{n}_{L.name}")
            for r in range(RING):
                S[L.name, "stacked", r] = sem(f"stacked{r}_{L.name}")
                S[L.name, "maxrows", r] = sem(f"maxrows{r}_{L.name}")
        dve_self, act_self, pool_self = sem("dve_self"), sem("act_self"), sem("pool_self")
        f_z, f_act, f_T, f_x, f_gf, f_gact, f_coef, f_r, f_stats, f_rstd, f_norm, f_tr, f_ev = (sem("f_" + n) for n in (
            "z", "act", "T", "x", "gf", "gact", "coef", "r", "stats", "rstd", "norm", "tr", "ev"))
        c_w, c_ev, f_pad = sem("c_w"), sem("c_ev"), sem("f_pad")
        hid1, tanh, moved, hid2, hid3 = (shared[:, at * CH:(at + n) * CH].rearrange("p (c t) -> p c t", t=CH)
                                         for at, n in ((0, 4), (4, 4), (8, 4), (12, 2), (14, 2)))
        gsum = sb("gsum", [P, NB])
        gh1, gh2, gt = sb("gh1", [P, NB]), sb("gh2", [P, NB]), sb("gt", [P, NB])
        halfb = sb("halfb", [P, 2])
        coefA, coefB = sb("coefA", [P, NB]), sb("coefB", [P, 2])

        m_ms, m_rr, m_xn, m_z, m_exp, m_probs, m_rows, m_LT, m_cnt, m_tot, m_base, m_tot2, m_base2, m_oh, m_pos, m_idx = (
            sem("m_" + n) for n in ("ms", "rr", "xn", "z", "exp", "probs", "rows", "LT", "cnt",
                                    "tot", "base", "tot2", "base2", "oh", "pos", "idx"))
        m_count = sem("m_count")
        e_g = [sem(f"e_g{i}") for i in range(XRING)]
        e_w = [sem(f"e_w{i}") for i in range(WRING)]
        e_xt, e_xtc, e_h, e_gelu, e_y, e_yg = (sem("e_" + n) for n in ("xt", "xtc", "h", "gelu", "y", "yg"))
        e_add = [sem(f"e_add{i}") for i in range(2)]
        s_acc, d_sum = [sem(f"s_acc{q}") for q in range(NQ)], sem("d_sum")
        d_stats, d_rstd, d_norm, s_out = sem("d_stats"), sem("d_rstd"), sem("d_norm"), sem("s_out")
        xn, xnT = x0, x2T
        ms, rr = sb("ms", [P, NT]), sb("rr", [P, NT])
        junk = sb("junk", [P, 2, P])
        logit = sb("logit", [P, NT, NE])
        lmax, lsum, lrec = sb("lmax", [P, NT]), sb("lsum", [P, NT]), sb("lrec", [P, NT])
        lz = sb("lz", [P, NT, NE])
        LT = sb("LT", [P, 2, P])
        found, inc = sb("found", [P, 1], I32), sb("inc", [P, 1], I32)
        cand, hits, nhits = sb("cand", [P, 3], I32), sb("hits", [P, 3]), sb("nhits", [P, 1])
        cnt = sb("cnt", [P, 3], BF16)
        gcount = sb("gcount", [P, 1], BF16)
        gtm, eqm, scan, selm = (sb(n, [P, 2, P]) for n in ("gtm", "eqm", "scan", "selm"))
        tot, tot2 = sb("tot", [P, 2], BF16), sb("tot2", [P, 2], BF16)
        base, lim, cend = sb("base", [P, 4]), sb("lim", [P, 2]), sb("cend", [P, 2])
        place = sb("place", [P, 2, P], BF16)
        oh = sb("oh", [P, 2, P], BF16)
        kst_flat = kst_all[:].rearrange("p r i t -> p (r i t)")
        ohe = kst_flat[:, 0:NE * 2 * P].rearrange("p (e h s) -> p e h s", e=NE, h=2)
        kvalb = sb("kvalb", [P, 2], BF16)
        le = kst_flat[:, NE * 2 * P:NE * 3 * P].rearrange("p (e j) -> p e j", e=NE)
        cntj = sb("cntj", [P, NE])
        idx = sb("idx", [P, NE], I32)
        ew = [sb(f"ew{i}", [P, 2 * F + D]) for i in range(WRING)]
        xe_all = parts[:].rearrange("p b a s t -> p (b a s t)").bitcast(F32)
        xe = [xe_all[:, i * GROW:(i + 1) * GROW] for i in range(XRING)]
        xeT = [sb(f"xeT{i}", [P, P]) for i in range(2)]
        hidT = [headsT[:, i].rearrange("p f t -> p (f t)")[:, 0:NF * CAP].rearrange("p (f t) -> p f t", f=NF) for i in range(2)]
        yg = [sb(f"yg{i}", [P, AROW]) for i in range(2)]
        acc = [shared[:, i * NT * AROW:(i + 1) * NT * AROW].rearrange("p (t c) -> p t c", t=NT) for i in range(2)]
        zero = sb("zero", [P, NT * AROW // 8])

        block = ctx.enter_context(nc.Block())

        @block.sync
        def _(sp):
            sp.dma_start(w[:, 0:NW_FIRST], w_in[:, 0:NW_FIRST]).then_inc(s_first, 16)
            sp.dma_start(xT0[:, 0:2 * T], xT_in[:, 0:2 * T]).then_inc(s_first, 16)
            sp.dma_start(cb[:], cb_in).then_inc(s_cb, 16)
            sp.dma_start(xT0[:, 2 * T:], xT_in[:, 2 * T:]).then_inc(s_x, 16)

            def late_loads():
                sp.dma_start(w[:, NW_FIRST:NW], w_in[:, NW_FIRST:NW]).then_inc(s_late, 16)
                sp.dma_start(lowrank, lowrank_in).then_inc(s_late, 16)
                sp.dma_start(x0[:], xtok_in).then_inc(s_late, 16)
                sp.dma_start(bits[:], bits_in).then_inc(s_late, 16)

            def between_loads():
                for e in range(WRING):
                    sp.dma_start(ew[e][:], ew_in[e]).then_inc(e_w[e], 16)
                for a in range(2):
                    sp.dma_start(acc_dram[a].rearrange("(p n r) c -> p n (r c)", p=P, n=8),
                                 zero[:].unsqueeze(1).to_broadcast([P, 8, NT * AROW // 8])).then_inc(s_zero, 16)

            def unstacked(L, b):
                sp.wait_ge(S[L.name, "split"], b + 1)
                if b >= 1:
                    sp.wait_ge(S[L.name, "written"], 16 * b)
                sp.dma_start(parts_dram[L.name][b].rearrange("a s f t -> f (a s) t"),
                             parts[:, b % 2].rearrange("p a s t -> p (a s) t")).then_inc(S[L.name, "written"], 16)

            def stack(L, b):
                r = b % RING
                if L is L0 and b == 2:
                    sp.wait_ge(s_init_late, 1)
                sp.wait_ge(S[L.name, "written"], 16 * (b + 1))
                if b >= RING:
                    sp.wait_ge(S[L.name, "turned"], L.U * (b - RING + 1))
                n = L.DH
                for h in range(L.halves):
                    for c, m in ((0, 3), (3, 2), (5, 1)):
                        at = (6 * h + c) * n
                        src = parts_dram[L.name][b, :, :, h * 64:h * 64 + n * 8, :].rearrange("a s (d p) t -> a s d (p t)", p=8)
                        k_src = src[K_PART[c], 1].unsqueeze(0).to_broadcast([m, n, 8 * T])
                        for t, x in ((kst[r], k_src), (qst[r][h], src[0:m, 0])):
                            sp.dma_start(t[at:at + m * n].rearrange("r p t -> r (p t)"), x)\
                              .then_inc(S[L.name, "stacked", r], 16)

            def max_rows(L, b):
                r = b % RING
                sp.wait_ge(S[L.name, "misc_read"], L.number["max", b] + 1)
                sp.dma_start(maxes_dram[L.name][b].rearrange("a h t -> h a t"), maxT[0:L.H, r])\
                  .then_inc(S[L.name, "maxwritten"], 16)
                sp.wait_ge(S[L.name, "maxwritten"], 16 * (b + 1))
                for h in range(L.halves):
                    sp.dma_start(qst[r][h][ROWS:ROWS + 2, :, :], maxes_dram[L.name][b, :, 8 * h:8 * h + 8, :])\
                      .then_inc(S[L.name, "maxrows", r], 16)

            sp.wait_ge(s_init_dve, 1)
            for L in (L0, L1):
                if L is L1:
                    between_loads()
                for t, _, _, _, steps in L.slots():
                    if L is L0 and t == 1:
                        late_loads()
                    for kind, b in steps:
                        if kind == "split2":
                            unstacked(L, b)
                        if kind == "stack":
                            stack(L, b)
                        if kind == "max":
                            max_rows(L, b)
            rows_view = rows_dram.rearrange("(t p) c -> p t c", p=P)
            sp.wait_ge(m_xn, NB)
            sp.dma_start(rows_view[:, :, 0:D], xn[:]).then_inc(m_rows, 16)
            sp.wait_ge(m_probs, 1)
            sp.dma_start(rows_view[:, :, D:GROW], lz[:]).then_inc(m_rows, 16)
            for e in range(WRING, NE):
                sp.wait_ge(e_y, e - WRING + 1)
                sp.dma_start(ew[e % WRING][:], ew_in[e]).then_inc(e_w[e % WRING], 16)
            for a in range(2):
                sp.wait_ge(e_add[a], 16 * (NE // 2))
            for q in range(NQ):
                for a in range(2):
                    sp.dma_start(acc[a][:, 4 * q:4 * q + 4, :], acc_dram[a].rearrange("(t p) c -> p t c", p=P)[:, 4 * q:4 * q + 4, :])\
                      .then_inc(s_acc[q], 16)
            for q in range(NQ):
                sp.wait_ge(d_norm, q + 1)
                sp.dma_start(out.rearrange("(t p) c -> p t c", p=P)[:, 4 * q:4 * q + 4, :], x0[:, 4 * q:4 * q + 4, :]).then_inc(s_out, 16)
            sp.wait_ge(s_zero, 32)
            sp.wait_ge(s_out, 16 * NQ)

        @block.tensor
        def _(pe):
            mm = nc.tensor.matmul
            tr = nc.tensor.transpose

            def network_step(kind, cyc, i):
                x_now = x1T if cyc == 0 else xf
                if kind in ("z1", "twist") and cyc > 0:
                    pe.wait_ge(f_x, NCHUNK * (cyc - 1) + i + 1)
                if kind == "twist":
                    if cyc == 0 and i == 3:
                        pe.wait_ge(f_gact, 3)
                    mm(bank[4 + i][:], W("twist"), x_now[:, i * CH:i * CH + CH], start=True, stop=True).then_inc(f_T, 1)
                elif kind == "g":
                    name, src, rows_ = (("gw1", gsum, 64), ("gw2", gh1, 32), ("gw3", gh2, P))[i]
                    if i == 0:
                        pe.wait_ge(f_gf, NB)
                    else:
                        pe.wait_ge(f_gact, i)
                    mm(bank[7][0:rows_, 0:NB], W(name), src[:], start=True, stop=True).then_inc(f_r, 1)
                else:
                    n = Z_NUMBER[kind, cyc, i]
                    o = bank[n % 4]
                    if n >= 4:
                        pe.wait_ge(f_act, n - 3)
                    if kind == "z1":
                        x = mm(o[:], W("cw1"), x_now[:, i * CH:i * CH + CH], start=True, stop=True)
                    elif kind == "z2":
                        pe.wait_ge(f_act, Z_NUMBER["z1", cyc, 2 * i + 1] + 1)
                        for j in range(2):
                            x = mm(o[64 * j:64 * j + 64, :], W("cw2"), hid1[:, 2 * i + j, :], start=True, stop=True)
                    elif kind == "z3":
                        pe.wait_ge(f_act, Z_NUMBER["z2", cyc, i] + 1)
                        x = mm(o[0:64, :], W("cw3"), hid2[:, i, :], start=True, stop=True)
                    else:
                        pe.wait_ge(f_act, Z_NUMBER["z3", cyc, i // 2] + 1)
                        x = mm(o[:], W("cw4")[:, i % 2 * P:i % 2 * P + P], hid3[:, i // 2, :], start=True, stop=True)
                    x.then_inc(f_z, 1)

            def attention(L, xT, wq, wk, wv, first=None):
                U, sems = L.U, lambda n: S[L.name, n]

                def misc(step):
                    n = L.number[step]
                    if n >= 2:
                        pe.wait_ge(sems("misc_read"), n - 1)
                    return misc_banks[L.name][n % 2]

                def score_unit(n):
                    b, u = divmod(n, U)
                    g, k = divmod(u, L.GU)
                    r = b % RING
                    if u == 0:
                        pe.wait_ge(S[L.name, "stacked", r], 16 * 6 * L.halves * (b // RING + 1))
                    if n >= 2:
                        pe.wait_ge(sems("maxed"), n - 1)
                    o = score_bank[n % 2]
                    if not L.causal:
                        for qt in range(2):
                            x = mm(o[:, qt * T:qt * T + T], qst[r][0][0:ROWS, u, qt * P:qt * P + P],
                                   kst[r][0:ROWS, u, :], start=True, stop=True)
                    else:
                        hs = range(4 * g, 4 * g + 4) if k == 0 else range(4 * g + 2 * k - 2, 4 * g + 2 * k)
                        qt, nk = (0, P) if k == 0 else (1, T)
                        ov = o[:].rearrange("p (h k) -> p h k", k=nk)
                        mm(ov[:, :, nk - P:nk], identb, maskq[:, 0:len(hs) * P].rearrange("p (h k) -> p h k", k=P),
                           start=True, stop=False, skip_group_check=True)
                        for i, h in enumerate(hs):
                            x = mm(ov[:, i, :], qst[r][h // 8][0:ROWS, h % 8, qt * P:qt * P + P],
                                   kst[r][0:ROWS, h % 8, 0:nk], start=False, stop=True, skip_group_check=True)
                    x.then_inc(sems("score"), 1)

                def turned_unit(m):
                    b, u = divmod(m, U)
                    g, k = divmod(u, L.GU)
                    r = b % RING
                    if u == 0:
                        pe.wait_ge(S[L.name, "maxrows", r], 16 * L.halves * (b // RING + 1))
                    if m >= 2:
                        pe.wait_ge(sems("exped"), m - 1)
                    o = turned_bank[m % 2]
                    K = ROWS + 2
                    if not L.causal:
                        for kt in range(2):
                            x = mm(o[:, kt * T:kt * T + T], kst[r][0:K, u, kt * P:kt * P + P],
                                   qst[r][0][0:K, u, :], start=True, stop=True)
                    else:
                        hs = range(4 * g + 2 * k, 4 * g + 2 * k + 2) if k < 2 else range(4 * g, 4 * g + 4)
                        kt, nq = (0, T) if k < 2 else (1, P)
                        ov = o[:].rearrange("p (h q) -> p h q", q=nq)
                        for i, h in enumerate(hs):
                            x = mm(ov[:, i, :], kst[r][0:K, h % 8, kt * P:kt * P + P],
                                   qst[r][h // 8][0:K, h % 8, T - nq:T], start=True, stop=True)
                    x.then_inc(sems("turned"), 1)

                def value_group(G):
                    b, g = divmod(G, L.NG)
                    pe.wait_ge(sems("cut" if L.causal else "exped"), L.GU * (G + 1))
                    pe.wait_ge(sems("misc_read"), L.number["v", b] + 1)
                    if G >= 2:
                        pe.wait_ge(sems("copied"), G - 1)
                    elif L is L0:
                        pe.wait_ge(c_ev, 1)
                    o = value_banks[L.name][G % 2]
                    v = vst[L.name][b % RING]
                    for kt in range(2):
                        for j in range(4):
                            if L.causal:
                                unit = L.GU * G + (j // 2 if kt == 0 else 2)
                                pr = probsT[:, unit % L.ring, :]
                                pr, q0 = (pr[:, (j % 2) * T:(j % 2) * T + T], 0) if kt == 0 else (pr[:, j * P:j * P + P], P)
                            else:
                                pr, q0 = probsT[:, (L.GU * G + j) % L.ring, kt * T:kt * T + T], 0
                            x = mm(o[32 * j:32 * j + 32, q0:T], v[:, kt, 4 * g + j, :], pr,
                                   start=(kt == 0), stop=(kt == 1), skip_group_check=True)
                    x.then_inc(sems("pv"), 1)

                def step(kind, b):
                    if kind in OWN_STEPS:
                        return
                    o = misc((kind, b))
                    x = None
                    cols = slice(b * T, b * T + T)
                    if kind in ("q", "k"):
                        if L is L0 and b == 2:
                            pe.wait_ge(s_x, 16)
                        for i, ww in enumerate(wq if kind == "q" else wk):
                            x = mm(o[:, i * T:i * T + T], ww, xT[:, cols], start=True, stop=True)
                    elif kind == "v":
                        for i in range(2):
                            x = mm(o[:, i * P:i * P + P], xT[:, b * T + i * P:b * T + i * P + P], wv, start=True, stop=True)
                    elif kind == "max":
                        pe.wait_ge(sems("maxed"), U * (b + 1))
                        for i in range(2):
                            x = tr(o[0:L.H, i * P:i * P + P], negmax[:, b % RING, i, 0:L.H], ident)
                    elif kind in ("heads0", "heads1"):
                        pe.wait_ge(sems("copied"), L.NG * (b + 1))
                        for qt in ((0, 1) if not L.causal else (int(kind[-1]),)):
                            for g in range(L.NG):
                                at = g * P + (qt * T if not L.causal else 0)
                                x = tr(o[:, at:at + P], headsT[:, b % 2, g, qt * P:qt * P + P], ident)
                    elif kind == "proj_in":
                        pe.wait_ge(sems("misc_read"), L.number["heads1", b] + 1)
                        for i in range(2):
                            x = tr(o[:, i * P:i * P + P], heads[:, b % 2, i, :], ident)
                    elif kind == "add":
                        pe.wait_ge(sems("misc_read"), L.number["proj_in", b] + 1)
                        for i in range(2):
                            x = mm(o[:, i * P:i * P + P], headsF[:, b % 2, i * P:i * P + P], W("wo"), start=True, stop=True)
                    elif kind == "turn":
                        pe.wait_ge(sems("normed"), b + 1) if L is L0 else pe.wait_ge(m_xn, b + 1)
                        for i in range(2):
                            x = tr(o[:, i * P:i * P + P], (x1 if L is L0 else xn)[:, 2 * b + i, :], ident)
                    elif kind == "logit":
                        pe.wait_ge(sems("misc_read"), L.number["turn", b] + 1)
                        for i in range(2):
                            x = mm(o[:, i * NE:i * NE + NE], xnT[:, b * T + i * P:b * T + i * P + P], W("rw"), start=True, stop=True)
                    x.then_inc(sems("misc_ready"), 1)

                for t, s, m, g, steps in L.slots():
                    for st in L.early(t):
                        pe.wait_ge(sems("maxed"), NB * U)
                        pe.wait_ge(sems("exped"), NB * U)
                        pe.wait_ge(sems("copied"), NB * L.NG)
                        pe.wait_ge(sems("misc_read"), L.number["turn", 5] + 1)
                        network_step(*st)
                    if L is L0 and s == 0:
                        pe.wait_ge(s_cb, 16)
                    if L is L0 and m == 0:
                        pe.wait_ge(s_ones, 1)
                    if t == 0 and first:
                        first()
                    if L is L0 and s == L.U:
                        compose()
                    if m is not None:
                        turned_unit(m)
                    if s is not None:
                        score_unit(s)
                    if g is not None:
                        value_group(g)
                    for st in steps:
                        step(*st)

            def compose():
                pe.wait_ge(s_late, 64)
                for i in range(3):
                    for c in range(2):
                        at = (2 * i + c) * 2 * D
                        v_f, u_f = lowrank[:, at:at + D], lowrank[:, at + D:at + 2 * D]
                        x = mm(value_banks["l0"][0][:, i * D:i * D + D], v_f, u_f, start=(c == 0), stop=(c == 1))
                x.then_inc(c_w, 1)

            pe.wait_ge(s_first, 32)
            attention(L0, xT0, (W("wq"), W("wq_swap")), (W("wk"), W("wk_swap")), W("wv"))

            pe.wait_ge(S["l0", "misc_read"], L0.nmisc)
            pe.wait_ge(S["l0", "exped"], NB * L0.U)
            pe.wait_ge(S["l0", "maxed"], NB * L0.U)
            pe.wait_ge(S["l0", "copied"], NB * L0.NG)
            pe.wait_ge(f_pad, 1)
            for st in NETWORK[EARLY:]:
                network_step(*st)
            for c in range(NCHUNK):
                pe.wait_ge(f_x, NCHUNK * (CYCLES - 1) + c + 1)
                for i in range(4):
                    x = tr(bank[4 + c][:, i * P:i * P + P], xf[:, c * CH + i * P:c * CH + i * P + P], ident)
                x.then_inc(f_tr, 1)
            pe.wait_ge(f_act, len(Z_NUMBER))
            def turn_back(c):
                pe.wait_ge(f_norm, c + 1)
                for i in range(4):
                    x = tr(bank[c][:, i * P:i * P + P], x2[:, 4 * c + i, :], ident)
                x.then_inc(f_tr, 1)

            def turn_rest():
                turn_back(2)
                turn_back(3)
                pe.wait_ge(f_ev, 4)

            turn_back(0)
            turn_back(1)
            pe.wait_ge(f_ev, 1)
            attention(L1, x2T, (lr[:, 0, :], lr[:, 1, :]), None, lr[:, 2, :], turn_rest)

            pe.wait_ge(S["l1", "misc_read"], L1.nmisc)
            pe.wait_ge(S["l1", "exped"], NB * L1.U)
            pe.wait_ge(S["l1", "maxed"], NB * L1.U)
            pe.wait_ge(S["l1", "copied"], NB * L1.NG)
            lf = logit[:].rearrange("p t e -> p (t e)")
            for i in range(2):
                x = tr(bank[5][:, i * P:i * P + P], lf[:, i * P:i * P + P], ident)
            x.then_inc(m_LT, 1)
            for i in range(2):
                pe.wait_ge(m_cnt, i + 1)
                mm(bank[6][:, 0:1], same_expert, cnt[:, 0:1], start=True, stop=True).then_inc(m_count, 1)
            for n in range(NPAIRS):
                pe.wait_ge(m_cnt, n + 3)
                mm(bank[6][:, 0:3], same_expert, cnt[:], start=True, stop=True).then_inc(m_count, 1)
            pe.wait_ge(m_tot, 1)
            mm(bank[7][:, 2:4], earlier, tot[:], start=True, stop=False, skip_group_check=True)
            mm(bank[7][:, 3:4], same_expert, tot[:, 0:1], start=False, stop=True, skip_group_check=True)
            mm(bank[7][:, 0:1], same_expert, gcount[:], start=True, stop=True, skip_group_check=True).then_inc(m_base, 1)
            pe.wait_ge(m_tot2, 1)
            mm(bank[7][:, 2:4], earlier, tot2[:], start=True, stop=False, skip_group_check=True)
            mm(bank[7][:, 3:4], same_expert, tot2[:, 0:1], start=False, stop=True, skip_group_check=True).then_inc(m_base2, 1)
            for e in range(NE):
                pe.wait_ge(m_oh, e + 1)
                for h in range(2):
                    mm(bank[e // 4][:, e % 4 * P:e % 4 * P + P], ohe[:, e, h, :], place[:, h, :], start=(h == 0), stop=(h == 1))
                for h in range(2):
                    x = mm(bank[4][:, e:e + 1], ohe[:, e, h, :], kvalb[:, h:h + 1], start=(h == 0), stop=(h == 1))
                if e % 4 == 3:
                    x.then_inc(m_pos, 1)
            pe.wait_ge(m_idx, 1)

            def turn_tokens(e):
                pe.wait_ge(e_g[e % XRING], 16 * (e // XRING + 1))
                if e >= 2:
                    pe.wait_ge(e_xtc, e - 1)
                tr(bank[e % 2][:, 0:P], xe[e % XRING][:, 0:D], ident).then_inc(e_xt, 1)

            def first_product(e):
                pe.wait_ge(e_w[e % WRING], 16 * (e // WRING + 1))
                pe.wait_ge(e_xtc, e + 1)
                if e >= 2:
                    pe.wait_ge(e_gelu, e - 1)
                o = bank[2 + e % 2]
                for f in range(NF):
                    x = mm(o[:, f * CAP:f * CAP + CAP], ew[e % WRING][:, f * P:f * P + P], xeT[e % 2][:], start=True, stop=True)
                x.then_inc(e_h, 1)

            def second_product(e):
                if e >= 2:
                    pe.wait_ge(e_yg, e - 1)
                o = bank[4 + e % 2]
                mm(o[:, 0:D], ones_t[0:1, :], ew[e % WRING][0:1, 2 * F:2 * F + D], start=True, stop=False)
                pe.wait_ge(e_gelu, e + 1)
                for f in range(NF):
                    x = mm(o[:, 0:D], hidT[e % 2][:, f, :], ew[e % WRING][:, F + f * D:F + f * D + D], start=False, stop=(f == NF - 1))
                x.then_inc(e_y, 1)

            turn_tokens(0)
            turn_tokens(1)
            first_product(0)
            for e in range(NE):
                if e + 1 < NE:
                    first_product(e + 1)
                if e + 2 < NE:
                    turn_tokens(e + 2)
                second_product(e)

        @block.vector
        def _(dve):
            v = nc.vector
            steps_done = [0]

            def settle(ins):
                ins.then_inc(dve_self, 1)
                steps_done[0] += 1
                dve.wait_ge(dve_self, steps_done[0])

            def attention(L, first=None):
                U, sems = L.U, lambda n: S[L.name, n]

                def own_max(n):
                    b, u = divmod(n, U)
                    g, k = divmod(u, L.GU)
                    dve.wait_ge(sems("score"), n + 1)
                    o = score_bank[n % 2][:]
                    nm = negmax[:, b % RING]
                    if not L.causal:
                        dst, src = nm[:, :, u], o.rearrange("p (h k) -> p h k", k=T)
                    elif k == 0:
                        dst, src = nm[:, 0, 4 * g:4 * g + 4], o.rearrange("p (h k) -> p h k", k=P)
                    else:
                        dst, src = nm[:, 1, 4 * g + 2 * k - 2:4 * g + 2 * k], o.rearrange("p (h k) -> p h k", k=T)
                    v.tensor_reduce(dst, src, AX, ALU.max, negate=True).then_inc(sems("maxed"), 1)

                def ready(step):
                    n = L.number[step]
                    dve.wait_ge(sems("misc_ready"), n + 1)
                    return misc_banks[L.name][n % 2]

                def read(ins):
                    ins.then_inc(sems("misc_read"), 1)

                def step(kind, b):
                    if kind == "norm":
                        dve.wait_ge(sems("rstd"), b + 1)
                        for i in range(2):
                            x = v.tensor_scalar((x1 if L is L0 else x3)[:, 2 * b + i, :], res[:, b % 2, i, :],
                                                mv[:, b % 2, i, 0:1], rstd[:, b % 2, i:i + 1], ALU.subtract, ALU.mult)
                        x.then_inc(sems("normed"), 1)
                        if L is L1:
                            dve.wait_ge(sems("normed"), b + 1)
                            for t in (2 * b, 2 * b + 1):
                                x = v.tensor_tensor_reduce(junk[:, t % 2, :], x3[:, t, :], x3[:, t, :], 1.0, 0.0, ALU.mult, ALU.add, ms[:, t:t + 1])
                            x.then_inc(m_ms, 1)
                        return
                    if kind == "weigh":
                        dve.wait_ge(m_rr, b + 1)
                        for t in (2 * b, 2 * b + 1):
                            x = v.scalar_tensor_tensor(out=xn[:, t, :], in0=x3[:, t, :], scalar=rr[:, t:t + 1], in1=W("nw"),
                                                       op0=ALU.mult, op1=ALU.mult)
                        x.then_inc(m_xn, 1)
                        return
                    if kind in OWN_STEPS:
                        return
                    o = ready((kind, b))
                    o2 = o[:].rearrange("p (i c) -> p i c", i=2)
                    if kind in ("q", "k"):
                        if L.causal:
                            if b >= 2:
                                dve.wait_ge(sems("split"), b - 1)
                            read(v.tensor_tensor(rot[:, b % 2, "qk".index(kind)], o2,
                                                 W("rope").rearrange("p (i c) -> p i c", i=2), ALU.mult))
                        else:
                            if b >= 2:
                                dve.wait_ge(sems("split"), b - 1)
                            read(v.tensor_tensor(qk[:, b % 2], o2, qk_bias.unsqueeze(2).to_broadcast([P, 2, T]), ALU.add))
                    elif kind == "v":
                        if L is L0 and b == 0:
                            dve.wait_ge(s_init_pool, 1)
                        if b >= RING:
                            dve.wait_ge(sems("pv"), L.NG * (b - RING + 1))
                        dst = vst[L.name][b % RING][:, :, :, 0:L.DH]
                        src = o[:, 0:T].rearrange("p (k h d) -> p k h d", k=2, h=L.H)
                        if L.causal:
                            read(v.tensor_copy(dst, src))
                        else:
                            bv = W("bv").rearrange("p (h d) -> p h d", h=L.H)
                            read(v.tensor_tensor(dst, src, bv.unsqueeze(1).to_broadcast([P, 2, L.H, L.DH]), ALU.add))
                    elif kind == "max":
                        if b >= RING:
                            dve.wait_ge(sems("maxwritten"), 16 * (b - RING + 1))
                        settle(v.tensor_copy(maxT[0:L.H, b % RING, 0, :], o[0:L.H, 0:T]))
                        read(v.tensor_tensor(maxT[0:L.H, b % RING, 1, :], o[0:L.H, 0:T], maxT[0:L.H, b % RING, 0, :], ALU.subtract))
                    elif kind in ("heads0", "heads1"):
                        n, part = L.DH, slice(int(kind[-1]), int(kind[-1]) + 1) if L.causal else slice(0, 2)
                        ov = o[:].rearrange("p (q h c) -> p q h c", h=L.H, c=32)
                        rs = rsum[:, part, 0:L.H]
                        settle(v.reciprocal(rs, ov[:, :, :, n]))
                        hv = heads[:, b % 2, part, :].rearrange("p q (h c) -> p q h c", c=n)
                        read(v.tensor_tensor(hv, ov[:, :, :, 0:n], rs.unsqueeze(3).to_broadcast(list(hv.shape)), ALU.mult))
                        if not L.causal:
                            dve.wait_ge(sems("misc_read"), L.number[kind, b] + 1)
                            settle(v.tensor_tensor(res[:, b % 2], heads[:, b % 2], x2[:, 2 * b:2 * b + 2, :], ALU.add))
                            norm_stats(b)
                    elif kind == "proj_in":
                        read(v.tensor_copy(headsF[:, b % 2, :], o[:, 0:T]))
                    elif kind == "add":
                        read(v.tensor_tensor(res[:, b % 2], o[:, 0:T].rearrange("p (i c) -> p i c", i=2), x0[:, 2 * b:2 * b + 2, :], ALU.add))
                        dve.wait_ge(sems("misc_read"), L.number[kind, b] + 1)
                        norm_stats(b)
                    elif kind == "turn":
                        if L is L0:
                            v.tensor_reduce(gsum[:, b:b + 1], o[:, 0:T], AX, ALU.add).then_inc(f_gf, 1)
                        read(v.tensor_copy((x1T if L is L0 else xnT)[:, b * T:b * T + T], o[:, 0:T]))

                    elif kind == "logit":
                        read(v.tensor_tensor(logit[:, 2 * b:2 * b + 2, :], o[:, 0:2 * NE].rearrange("p (t e) -> p t e", e=NE),
                                             W("rb").unsqueeze(1).to_broadcast([P, 2, NE]), ALU.add))

                def norm_stats(b):
                    for i in range(2):
                        x = v.bn_stats(stats[:, b % 2, i, :], res[:, b % 2, i, :])
                    settle(x)
                    for i in range(2):
                        x = v.bn_aggr(mv[:, b % 2, i, :], stats[:, b % 2, i, :])
                    x.then_inc(sems("stats"), 1)

                for t, s, m, g, steps in L.slots():
                    if t == 0 and first:
                        first()
                    if L is L0 and s == L.U:
                        dve.wait_ge(c_w, 1)
                        v.tensor_copy(lr[:].rearrange("p i c -> p (i c)"), value_banks["l0"][0][:, 0:3 * D]).then_inc(c_ev, 1)
                        dve.wait_ge(s_late, 64)
                        v.tensor_scalar(halfb[:, 0:1], col("cb4"), 0.5, None, ALU.mult)
                        v.tensor_scalar(halfb[:, 1:2], col("gb3"), 0.5, None, ALU.mult)
                        v.tensor_scalar(coefB[:, 0:1], col("range"), 0.3, None, ALU.mult)
                        v.tensor_scalar(coefB[:, 1:2], col("range"), 0.7, None, ALU.mult)
                    if s is not None:
                        own_max(s)
                    for st in steps:
                        step(*st)

            v.memset(mhalf[:], -0.5)
            v.memset(qst_all[0:ROWS, 0:2].rearrange("p r h i t -> p (r h i t)").bitcast(F32), 0.0).then_inc(s_init_dve, 1)
            dve.wait_ge(s_first, 32)
            dve.wait_ge(s_init_dve, 1)
            def init_late():
                v.memset(gh1[64:128], 0.0)
                v.memset(gh2[32:64], 0.0)
                v.memset(gh2[64:128], 0.0)
                v.memset(zero[:], 0.0)
                v.memset(qst_all[0:ROWS, 2:RING].rearrange("p r h i t -> p (r h i t)").bitcast(F32), 0.0).then_inc(s_init_late, 1)
                dve.wait_ge(s_init_late, 1)

            attention(L0, init_late)

            dve.wait_ge(S["l0", "misc_read"], L0.nmisc)
            dve.wait_ge(f_gact, 3)
            v.tensor_scalar(coefA[:], gt[:], coefB[:, 1:2], 0.1, ALU.mult, ALU.add).then_inc(f_coef, 1)
            dve.wait_ge(f_coef, 1)
            def first_part(cyc, c):
                x_now = x1T if cyc == 0 else xf
                dve.wait_ge(f_T, NCHUNK * cyc + c + 1)
                for i in range(2):
                    half = slice(i * T, i * T + T)
                    x = v.scalar_tensor_tensor(out=moved[:, c, half], in0=bank[4 + c][:, half], scalar=coefA[:, 2 * c + i:2 * c + i + 1],
                                               in1=x_now[:, c * CH + i * T:c * CH + i * T + T], op0=ALU.mult, op1=ALU.add)
                if cyc == CYCLES - 1:
                    settle(x)
                    x = v.tensor_tensor(moved[:, c, :], moved[:, c, :], x1T[:, c * CH:c * CH + CH], ALU.add)
                settle(x)

            def second_part(cyc, c):
                sl = slice(c * CH, c * CH + CH)
                dve.wait_ge(f_act, Z_NUMBER["z4", cyc, c] + 1)
                settle(v.scalar_tensor_tensor(out=tanh[:, c, :], in0=tanh[:, c, :], scalar=coefB[:, 0:1], in1=bank[4 + c][:],
                                              op0=ALU.mult, op1=ALU.mult))
                v.tensor_tensor(xf[:, sl], moved[:, c, :], tanh[:, c, :], ALU.add).then_inc(f_x, 1)

            for c in range(NCHUNK):
                first_part(0, c)
                second_part(0, c)
            for cyc in range(1, CYCLES):
                for c in range(NCHUNK):
                    first_part(cyc, c)
                for c in range(NCHUNK):
                    second_part(cyc, c)

            def network_norm(c):
                dve.wait_ge(f_tr, c + 1)
                if c >= 2:
                    dve.wait_ge(f_rstd, c - 1)
                for i in range(4):
                    x = v.bn_stats(stats[:, c % 2, i, :], bank[4 + c][:, i * P:i * P + P])
                settle(x)
                for i in range(4):
                    x = v.bn_aggr(mv[:, c % 2, i, :], stats[:, c % 2, i, :])
                x.then_inc(f_stats, 1)
                dve.wait_ge(f_rstd, c + 1)
                for i in range(4):
                    x = v.tensor_scalar(x2[:, 4 * c + i, :], bank[4 + c][:, i * P:i * P + P], mv[:, c % 2, i, 0:1],
                                        rstd[:, c % 2, i:i + 1], ALU.subtract, ALU.mult)
                x.then_inc(f_norm, 1)
            network_norm(0)
            network_norm(1)
            for r in range(RING):
                x = v.memset(vst["l1"][r][:, :, :, L1.DH:L1.DH + 1], 1.0)
            settle(x)
            attention(L1, lambda: (network_norm(2), network_norm(3)))

            dve.wait_ge(S["l1", "misc_read"], L1.nmisc)
            settle(v.tensor_reduce(lmax[:], logit[:], AX, ALU.max))
            v.tensor_tensor(lz[:], logit[:], lmax[:].unsqueeze(2).to_broadcast([P, NT, NE]), ALU.subtract).then_inc(m_z, 1)
            dve.wait_ge(m_exp, 1)
            settle(v.tensor_reduce(lsum[:], lz[:], AX, ALU.add))
            settle(v.reciprocal(lrec[:], lsum[:]))
            v.tensor_tensor(lz[:], lz[:], lrec[:].unsqueeze(2).to_broadcast([P, NT, NE]), ALU.mult).then_inc(m_probs, 1)

            dve.wait_ge(m_LT, 1)
            settle(v.tensor_copy(LT[:].rearrange("p h j -> p (h j)"), bank[5][:, 0:2 * P]))
            v.tensor_scalar(junk[:], LT[:], 0.0, 0.0, ALU.is_ge, ALU.add, accum_out=cnt[:, 0:1]).then_inc(m_cnt, 1)
            dve.wait_ge(m_count, 1)
            settle(v.tensor_scalar(found[:], bank[6][:, 0:1], float(CAP), -1.0, ALU.is_lt, ALU.mult))
            settle(v.tensor_tensor(cand[:, 0:1], bits[:, 0:1], found[:], ALU.bitwise_xor))
            v.tensor_scalar(junk[:], LT[:], cand[:, 0:1].bitcast(F32), 0.0, ALU.is_ge, ALU.add, accum_out=cnt[:, 0:1]).then_inc(m_cnt, 1)
            dve.wait_ge(m_count, 2)
            settle(v.tensor_scalar(inc[:], bank[6][:, 0:1], float(CAP), W("bits")[:, 0:1], ALU.is_ge, ALU.mult))
            settle(v.scalar_tensor_tensor(out=cand[:], in0=bits[:, 1:4], scalar=inc[:], in1=found[:].to_broadcast([P, 3]),
                                          op0=ALU.bitwise_xor, op1=ALU.bitwise_xor))
            for n in range(NPAIRS):
                for c, unused in enumerate((junk, gtm, eqm)):
                    x = v.tensor_scalar(unused[:], LT[:], cand[:, c:c + 1].bitcast(F32), 0.0, ALU.is_ge, ALU.add, accum_out=cnt[:, c:c + 1])
                x.then_inc(m_cnt, 1)
                v.tensor_tensor(found[:], found[:], inc[:], ALU.bitwise_xor)
                dve.wait_ge(m_count, n + 3)
                settle(v.tensor_scalar(hits[:], bank[6][:, 0:3], float(CAP), 0.0, ALU.is_ge, ALU.add, accum_out=nhits[:]))
                settle(v.tensor_scalar(inc[:], nhits[:], W("bits")[:, n + 1:n + 2], None, ALU.mult))
                settle(v.scalar_tensor_tensor(out=cand[:], in0=bits[:, 3 * n + 4:3 * n + 7], scalar=inc[:], in1=found[:].to_broadcast([P, 3]),
                                              op0=ALU.bitwise_xor, op1=ALU.bitwise_xor))
            settle(v.tensor_tensor(found[:], found[:], inc[:], ALU.bitwise_xor))
            thr = found[:].bitcast(F32)
            v.tensor_scalar(gtm[:], LT[:], thr, 0.0, ALU.is_gt, ALU.add, accum_out=gcount[:])
            v.memset(selm[:], 0.0)
            settle(v.tensor_scalar(eqm[:], LT[:], thr, None, ALU.is_equal))
            for h in range(2):
                x = v.tensor_tensor_scan(scan[:, h, :], eqm[:, h, :], selm[:, h, :], 0.0, ALU.add, ALU.add)
            settle(x)
            v.tensor_copy(tot[:], scan[:, :, P - 1]).then_inc(m_tot, 1)
            dve.wait_ge(m_base, 1)
            settle(v.tensor_copy(base[:, 0:1], bank[7][:, 0:1]))
            settle(v.tensor_scalar(lim[:], bank[7][:, 2:4], base[:, 0:1], None, ALU.add))
            settle(v.tensor_scalar(lim[:], lim[:], -1.0, float(CAP), ALU.mult, ALU.add))
            for h in range(2):
                x = v.scalar_tensor_tensor(out=junk[:, h, :], in0=scan[:, h, :], scalar=lim[:, h:h + 1], in1=eqm[:, h, :],
                                           op0=ALU.is_le, op1=ALU.mult)
            settle(x)
            settle(v.tensor_tensor(gtm[:], gtm[:], junk[:], ALU.add))
            for h in range(2):
                x = v.tensor_tensor_scan(scan[:, h, :], gtm[:, h, :], selm[:, h, :], 0.0, ALU.add, ALU.add)
            settle(x)
            v.tensor_copy(tot2[:], scan[:, :, P - 1]).then_inc(m_tot2, 1)
            dve.wait_ge(m_base2, 1)
            settle(v.tensor_copy(base[:, 2:4], bank[7][:, 2:4]))
            settle(v.tensor_tensor(cend[:], base[:, 2:4], scan[:, :, P - 1], ALU.add))
            for h in range(2):
                v.tensor_scalar(place[:, h, :], scan[:, h, :], base[:, 2 + h:3 + h], None, ALU.add)
                x = v.tensor_scalar(junk[:, h, :], W("iota"), base[:, 2 + h:3 + h], None, ALU.is_ge)
            settle(x)
            for h in range(2):
                x = v.scalar_tensor_tensor(out=oh[:, h, :], in0=W("iota"), scalar=cend[:, h:h + 1], in1=junk[:, h, :],
                                           op0=ALU.is_lt, op1=ALU.mult)
            settle(x)
            settle(v.tensor_copy(kvalb[:], W("kval")))
            for e in range(NE):
                v.tensor_scalar(ohe[:, e], oh[:], W("emask")[:, e:e + 1], None, ALU.mult).then_inc(m_oh, 1)
            for q in range(4):
                dve.wait_ge(m_pos, q + 1)
                x = v.tensor_scalar(le[:, 4 * q:4 * q + 4, :], bank[q][:].rearrange("p (e j) -> p e j", j=P), col("slot"), None, ALU.is_le)
            settle(x)
            settle(v.tensor_reduce(cntj[:], le, AX, ALU.add))
            v.scalar_tensor_tensor(out=idx[:], in0=bank[4][:, 0:NE], scalar=float(P), in1=cntj[:], op0=ALU.mult, op1=ALU.add).then_inc(m_idx, 1)

            for i in range(2):
                v.memset(yg[i][:, D:AROW], 0.0)

            def weigh(e):
                dve.wait_ge(e_y, e + 1)
                if e >= 2:
                    dve.wait_ge(e_add[e % 2], 16 * (e // 2))
                gate = xe[e % XRING][:, D + e:D + e + 1]
                v.tensor_copy(yg[e % 2][:, D:D + 1], gate)
                v.tensor_scalar(yg[e % 2][:, 0:D], bank[4 + e % 2][:, 0:D], gate, None, ALU.mult).then_inc(e_yg, 1)

            def keep_turned(e):
                dve.wait_ge(e_xt, e + 1)
                if e >= 2:
                    dve.wait_ge(e_h, e - 1)
                v.tensor_copy(xeT[e % 2][:], bank[e % 2][:, 0:P]).then_inc(e_xtc, 1)

            keep_turned(0)
            keep_turned(1)
            for e in range(NE):
                if e + 2 < NE:
                    keep_turned(e + 2)
                weigh(e)

            def mean_and_stats(q):
                dve.wait_ge(d_sum, q + 1)
                tiles = range(4 * q, 4 * q + 4)
                settle(v.reciprocal(lrec[:, 4 * q:4 * q + 4], lsum[:, 4 * q:4 * q + 4]))
                for t in tiles:
                    x = v.scalar_tensor_tensor(out=acc[1][:, t, 0:D], in0=acc[0][:, t, 0:D], scalar=lrec[:, t:t + 1],
                                               in1=x3[:, t, :], op0=ALU.mult, op1=ALU.add)
                settle(x)
                for t in tiles:
                    x = v.bn_stats(fstats[:, t, :], acc[1][:, t, 0:D])
                settle(x)
                for t in tiles:
                    x = v.bn_aggr(fmv[:, t, :], fstats[:, t, :])
                x.then_inc(d_stats, 1)

            def normalise(q):
                dve.wait_ge(d_rstd, q + 1)
                for t in range(4 * q, 4 * q + 4):
                    x = v.tensor_scalar(x0[:, t, :], acc[1][:, t, 0:D], fmv[:, t, 0:1], frstd[:, t:t + 1], ALU.subtract, ALU.mult)
                x.then_inc(d_norm, 1)

            for q in range(NQ):
                mean_and_stats(q)
                if q >= 1:
                    normalise(q - 1)
            normalise(NQ - 1)

        @block.scalar
        def _(act):
            a = nc.scalar
            own = [0]

            def settle(ins):
                ins.then_inc(act_self, 1)
                own[0] += 1
                act.wait_ge(act_self, own[0])

            def network_step(kind, cyc, i):
                if kind == "g":
                    dst, rows_, func, bias, scale = ((gh1, 64, ACT.Gelu, col("gb1", 64), 1.0 / T), (gh2, 32, ACT.Gelu, col("gb2", 32), 1.0),
                                                     (gt, P, ACT.Tanh, halfb[:, 1:2], 0.5))[i]
                    act.wait_ge(f_r, i + 1)
                    a.activation(dst[0:rows_, :], bank[7][0:rows_, 0:NB], func, bias=bias, scale=scale).then_inc(f_gact, 1)
                elif kind != "twist":
                    n = Z_NUMBER[kind, cyc, i]
                    o = bank[n % 4]
                    act.wait_ge(f_z, n + 1)
                    if kind == "z1":
                        x = a.activation(hid1[:, i, :], o[:], ACT.Gelu, bias=col("cb1"))
                    elif kind == "z2":
                        x = a.activation(hid2[:, i, :], o[:], ACT.Gelu, bias=col("cb2"))
                    elif kind == "z3":
                        x = a.activation(hid3[0:64, i, :], o[0:64, :], ACT.Gelu, bias=col("cb3", 64))
                    else:
                        x = a.activation(tanh[:, i, :], o[:], ACT.Tanh, bias=halfb[:, 0:1], scale=0.5)
                    x.then_inc(f_act, 1)

            def attention(L, first=None):
                sems = lambda n: S[L.name, n]
                for t, s, m, g, steps in L.slots():
                    for st in L.early(t):
                        act.wait_ge(s_late, 64)
                        network_step(*st)
                    if t == 0 and first:
                        first()
                    if m is not None:
                        act.wait_ge(sems("turned"), m + 1)
                        if m >= L.ring:
                            act.wait_ge(sems("pv"), (m - L.ring) // L.GU + 1)
                        a.activation(probsT[:, m % L.ring, :], turned_bank[m % 2][:], ACT.Exp, scale=float(L.DH) ** -0.5)\
                         .then_inc(sems("exped"), 1)
                    if g is not None:
                        b = g // L.NG
                        act.wait_ge(sems("pv"), g + 1)
                        if b >= 2:
                            act.wait_ge(sems("misc_read"), L.number["heads1" if L.causal else "heads0", b - 2] + 1)
                        a.copy(headsT[:, b % 2, g % L.NG, :], value_banks[L.name][g % 2][:, 0:T]).then_inc(sems("copied"), 1)
                    for kind, b in steps:
                        if kind == "split":
                            if L.causal:
                                act.wait_ge(sems("added"), b + 1)
                            else:
                                act.wait_ge(sems("misc_read"), L.number["q", b] + 1)
                            if b >= 2:
                                act.wait_ge(sems("written"), 16 * (b - 1))
                            a.copy(parts[:, b % 2, 0], qk_of(b)).then_inc(sems("kept"), 1)
                        if kind == "split2":
                            act.wait_ge(sems("rest"), b + 1)
                            a.copy(parts[:, b % 2, 1], left[:, b % 2]).then_inc(sems("kept"), 1)

            attention(L0)
            act.wait_ge(S["l0", "misc_read"], L0.nmisc)
            for st in NETWORK[EARLY:]:
                network_step(*st)

            def keep_turned(c):
                act.wait_ge(f_tr, NCHUNK + c + 1)
                a.copy(x2T[:, c * CH:c * CH + CH], bank[c][:]).then_inc(f_ev, 1)

            keep_turned(0)
            keep_turned(1)
            attention(L1, lambda: (keep_turned(2), keep_turned(3)))
            act.wait_ge(m_z, 1)
            a.activation(lz[:], lz[:], ACT.Exp).then_inc(m_exp, 1)
            for e in range(NE):
                act.wait_ge(e_h, e + 1)
                if e >= 2:
                    act.wait_ge(e_y, e - 1)
                for f in range(NF):
                    i = WEIGHTS["fb1"][0] + e * NF + f
                    x = a.activation(hidT[e % 2][:, f, :], bank[2 + e % 2][:, f * CAP:f * CAP + CAP], ACT.Gelu, bias=w[:, i:i + 1])
                x.then_inc(e_gelu, 1)

        @block.gpsimd
        def _(pool):
            gp = nc.gpsimd
            own = [0]

            def settle(ins):
                ins.then_inc(pool_self, 1)
                own[0] += 1
                pool.wait_ge(pool_self, own[0])

            def attention(L, first=None):
                sems = lambda n: S[L.name, n]
                for t, _, m, _, steps in L.slots():
                    if t == 0 and first:
                        first()
                    if L.causal and m is not None:
                        k = m % L.GU
                        pool.wait_ge(sems("exped"), m + 1)
                        pr = probsT[:, m % L.ring, :].rearrange("p (h q) -> p h q", h=2 if k < 2 else 4)[:, :, 0:P]
                        gp.affine_select(out=pr, in_=pr, pattern=[[0, 2 if k < 2 else 4], [1, P]], compare_op=ALU.is_ge,
                                         fill=0.0, base=0, channel_multiplier=-1).then_inc(sems("cut"), 1)
                    for kind, b in steps:
                        if kind == "split":
                            if L.causal:
                                pool.wait_ge(sems("misc_read"), L.number["k", b] + 1)
                                gp.tensor_tensor(qk_of(b), rot[:, b % 2, :, 0, :], rot[:, b % 2, :, 1, :], ALU.add)\
                                  .then_inc(sems("added"), 1)
                            pool.wait_ge(sems("kept"), 2 * b + 1)
                            gp.tensor_tensor(left[:, b % 2], qk_of(b), parts[:, b % 2, 0], ALU.subtract).then_inc(sems("rest"), 1)
                        if kind == "split2":
                            pool.wait_ge(sems("kept"), 2 * b + 2)
                            gp.tensor_tensor(parts[:, b % 2, 2], left[:, b % 2], parts[:, b % 2, 1], ALU.subtract).then_inc(sems("split"), 1)
                        if kind == "rsqrt":
                            rsqrt(b, sems("stats"), sems("rstd"), 2)
                        if kind == "rms":
                            tiles = slice(2 * b, 2 * b + 2)
                            pool.wait_ge(m_ms, b + 1)
                            settle(gp.tensor_scalar(rr[:, tiles], ms[:, tiles], 1.0 / D, EPS, ALU.mult, ALU.add))
                            gp.tensor_tensor(rr[:, tiles], rr[:, tiles], mhalf[:, 0:2], ALU.pow).then_inc(m_rr, 1)

            def rsqrt(b, ready, done, n):
                pool.wait_ge(ready, b + 1)
                settle(gp.tensor_scalar(vpe[:, b % 2, 0:n], mv[:, b % 2, 0:n, 1], EPS, None, ALU.add))
                gp.tensor_tensor(rstd[:, b % 2, 0:n], vpe[:, b % 2, 0:n], mhalf[:, 0:n], ALU.pow).then_inc(done, 1)

            settle(gp.memset(vst_all[:], 0.0))
            gp.memset(vst_all[:, :, :, :, L0.DH:L0.DH + 1], 1.0).then_inc(s_init_pool, 1)
            pool.wait_ge(s_init_pool, 1)
            pool.wait_ge(s_init_dve, 1)

            def init_ones():
                pool.wait_ge(S["l0", "split"], 2)
                settle(gp.memset(kst_all[ROWS:ROWS + 2].rearrange("p r i t -> p (r i t)").bitcast(F32), TWO_ONES))
                gp.memset(ones_t[:], 1.0).then_inc(s_ones, 1)
                pool.wait_ge(s_ones, 1)

            attention(L0, init_ones)
            pool.wait_ge(S["l0", "pv"], NB * L0.NG)
            pool.wait_ge(S["l0", "rstd"], NB)
            gp.memset(hid3[64:P], 0.0).then_inc(f_pad, 1)
            rsqrt(0, f_stats, f_rstd, 4)
            rsqrt(1, f_stats, f_rstd, 4)
            attention(L1, lambda: (rsqrt(2, f_stats, f_rstd, 4), rsqrt(3, f_stats, f_rstd, 4)))
            pool.wait_ge(m_idx, 1)
            pool.wait_ge(m_rows, 32)
            pool.wait_ge(s_zero, 32)

            def gather(e):
                gp.indirect_dma_start(out=xe[e % XRING], out_offset=None, in_=rows_dram,
                                      in_offset=bass.IndirectOffsetOnAxis(ap=idx[:, e:e + 1], axis=0)).then_inc(e_g[e % XRING], 16)

            for e in range(XRING):
                gather(e)
            for e in range(NE):
                pool.wait_ge(e_yg, e + 1)
                if e >= 2:
                    pool.wait_ge(e_add[e % 2], 16 * (e // 2))
                gp.indirect_dma_start(out=acc_dram[e % 2], out_offset=bass.IndirectOffsetOnAxis(ap=idx[:, e:e + 1], axis=0),
                                      in_=yg[e % 2][:], in_offset=None, compute_op=ALU.add).then_inc(e_add[e % 2], 16)
                if e + XRING < NE:
                    gather(e + XRING)
            def add_up(q):
                tiles = slice(4 * q, 4 * q + 4)
                pool.wait_ge(s_acc[q], 32)
                settle(gp.tensor_tensor(acc[0][:, tiles, 0:D + 1], acc[0][:, tiles, 0:D + 1], acc[1][:, tiles, 0:D + 1], ALU.add))
                settle(gp.tensor_scalar(lsum[:, tiles], acc[0][:, tiles, D], 0.0, None, ALU.is_equal))
                gp.tensor_tensor(lsum[:, tiles], lsum[:, tiles], acc[0][:, tiles, D], ALU.add).then_inc(d_sum, 1)
                pool.wait_ge(d_sum, q + 1)

            def last_rsqrt(q):
                tiles = slice(4 * q, 4 * q + 4)
                pool.wait_ge(d_stats, q + 1)
                settle(gp.tensor_scalar(frstd[:, tiles], fmv[:, tiles, 1], EPS, None, ALU.add))
                gp.tensor_tensor(frstd[:, tiles], frstd[:, tiles], mhalf[:, 0:4], ALU.pow).then_inc(d_rstd, 1)
                pool.wait_ge(d_rstd, q + 1)

            for q in range(NQ):
                add_up(q)
                if q >= 1:
                    last_rsqrt(q - 1)
            last_rsqrt(NQ - 1)
    return nc


def kernel(**inputs):
    import concourse.bacc as _bacc
    from concourse.bass_utils import run_bass_kernel_spmd as _run
    import ml_dtypes

    x = {k: np.asarray(v) for k, v in inputs.items()}
    f32 = np.float32
    X = x["L0_attn_X"].reshape(NTOK, D)

    wt = np.zeros((P, NW), f32)

    def put(name, a):
        s = WEIGHTS[name][0]
        wt[:a.shape[0], s:s + a.shape[1]] = a

    rows0 = np.arange(D).reshape(2, 8, 8).transpose(0, 2, 1).reshape(-1)
    swap = rows0 ^ 1
    for n, a in (("q", x["L0_attn_W_q"]), ("k", x["L0_attn_W_k"])):
        put("w" + n, a[rows0].T)
        put(f"w{n}_swap", a[swap].T)
    put("wv", x["L0_attn_W_v"].T)
    put("wo", x["L0_attn_W_o"].T)
    dh = D // L0.H
    theta = (f32(10000.0) ** (f32(-2.0) * np.arange(dh // 2, dtype=f32) / f32(dh))).astype(f32)
    angles = np.arange(T, dtype=f32)[None, :] * theta[:, None]
    feat = rows0 % dh
    put("rope", np.concatenate([np.cos(angles)[feat // 2], np.sin(angles)[feat // 2] * np.where(feat % 2, 1, -1)[:, None]], 1).astype(f32))
    put("ident", np.eye(P, dtype=f32))
    put("cw1", x["L0_ffn_cn_w1"])
    put("cw2", x["L0_ffn_cn_w2"])
    cw3, cw4 = np.zeros((P, D // 2), f32), np.zeros((P, 2 * P), f32)
    for j in range(2):
        cw3[64 * j:64 * j + 64, 32 * j:32 * j + 32] = x["L0_ffn_cn_w3"]
        cw4[32 * j:32 * j + 32, P * j:P * j + P] = x["L0_ffn_cn_w4"]
    put("cw3", cw3)
    put("cw4", cw4)
    tw = np.zeros((D, D), f32)
    for blk, (src, sign) in enumerate(((2, 1), (3, -1), (0, -1), (1, 1))):
        for i in range(32):
            tw[src * 32 + i, blk * 32 + i] = sign
    put("twist", tw)
    put("gw1", x["L0_ffn_gc_w1"])
    put("gw2", x["L0_ffn_gc_w2"])
    put("gw3", np.broadcast_to(x["L0_ffn_gc_w3"], (D // 4, P)))
    H, DH, R = L1.H, L1.DH, 32
    lowrank = np.zeros((P, 3, 2, 2, D), f32)
    for i, n in enumerate("qkv"):
        U, V = x["L1_attn_U" + n], x["L1_attn_V" + n]
        for h in range(H):
            c, r0 = divmod(h * R, P)
            lowrank[r0:r0 + R, i, c, 0, h * DH:h * DH + DH] = V[h]
            if n == "v":
                lowrank[r0:r0 + R, i, c, 1, h * DH:h * DH + DH] = U[h].T
            else:
                lowrank[r0:r0 + R, i, c, 1, h::H] = U[h].T
    put("bv", np.broadcast_to(x["L1_attn_bv"].reshape(1, D), (P, D)))
    put("nw", np.broadcast_to(x["L1_ffn_norm_weight"][None], (P, D)))
    put("rb", np.broadcast_to(x["L1_ffn_router_bias"][None], (P, NE)))
    put("rw", x["L1_ffn_router_weight"].T)
    put("fb1", x["L1_ffn_fc1_bias"].reshape(NE, NF, P).transpose(2, 0, 1).reshape(P, -1))
    cols = np.zeros((P, 16), f32)
    for n, a in (("cb1", x["L0_ffn_cn_b1"]), ("cb2", np.tile(x["L0_ffn_cn_b2"], 2)), ("cb3", np.tile(x["L0_ffn_cn_b3"], 2)),
                 ("cb4", np.broadcast_to(x["L0_ffn_cn_b4"], (P,))), ("gb1", x["L0_ffn_gc_b1"]), ("gb2", x["L0_ffn_gc_b2"]),
                 ("gb3", np.broadcast_to(x["L0_ffn_gc_b3"], (P,))), ("range", np.broadcast_to(x["L0_ffn_adaptive_range"], (P,))),
                 ("bq", x["L1_attn_bq"].T.reshape(-1)), ("bk", x["L1_attn_bk"].T.reshape(-1)), ("slot", np.arange(P, dtype=f32))):
        cols[:a.shape[0], COLS[n]] = a
    put("cols", cols)
    put("iota", np.broadcast_to(np.arange(P, dtype=f32)[None], (P, P)))
    part = np.arange(P)
    put("emask", (part[:, None] % NE == np.arange(NE)[None]).astype(f32))
    put("kval", np.stack([part // NE, part // NE + 8], 1).astype(f32))
    low = np.arange(2 * NPAIRS - 2, -1, -2)
    put("bits", np.broadcast_to(np.concatenate([[2.0 ** (2 * NPAIRS)], 2.0 ** low])[None], (P, 1 + NPAIRS)).astype(f32))
    bits = np.concatenate([[1 << (2 * NPAIRS)], ((1 << low)[:, None] * np.arange(1, 4)[None]).reshape(-1), [0, 0, 0]]).astype(np.int32)
    bits = np.ascontiguousarray(np.broadcast_to(bits[None], (P, bits.size)))

    q, k = part[:, None], part[None, :]
    maskq = np.tile(np.where(k > q, MASKED, 0.0), (1, 4))
    maskk = np.tile(np.where(q > k, MASKED, 0.0), (1, 4))
    same = (q % NE == k % NE)
    earlier = same & (q // NE < k // NE)
    cbt = np.concatenate([np.eye(P), maskq, maskk, same, earlier], 1).astype(ml_dtypes.bfloat16)

    ew = np.concatenate([x["L1_ffn_fc1_weight"].transpose(0, 2, 1),
                         x["L1_ffn_fc2_weight"].transpose(0, 2, 1).reshape(NE, NF, P, D).transpose(0, 2, 1, 3).reshape(NE, P, NF * D),
                         np.concatenate([x["L1_ffn_fc2_bias"][:, None], np.zeros((NE, P - 1, D), f32)], 1)], 2)
    arrays = {
        "in_xT": np.ascontiguousarray(X.T), "in_xtok": np.ascontiguousarray(X.reshape(NT, P, D).transpose(1, 0, 2)),
        "in_w": wt, "in_lowrank": lowrank.reshape(P, -1), "in_cb": cbt, "in_bits": bits,
        "in_ew": np.ascontiguousarray(ew),
    }
    nc = _bacc.Bacc("TRN2", target_bir_lowering=False, num_devices=1)
    args = [nc.dram_tensor(n, a.shape, mybir.dt.from_np(a.dtype), kind="ExternalInput").ap() for n, a in arrays.items()]
    out = nc.dram_tensor("out_0", (NTOK, D), F32, kind="ExternalOutput").ap()
    build_program(nc, *args, out)
    r = _run(nc, [arrays], core_ids=[0])
    return r.results[0]["out_0"].reshape(NB, T, D)
```
